# Optimizing a Trainium2 kernel written in Bass

```python
import numpy as np
import jax
import jax.numpy as jnp

def _softmax(x, axis=-1):
    return jax.nn.softmax(x, axis=axis)

def _gelu(x):
    return jax.nn.gelu(x, approximate=True)

def _silu(x):
    return jax.nn.silu(x)

def _sigmoid(x):
    return jax.nn.sigmoid(x)

def _layernorm(x, axis=-1, eps=1e-05):
    m = jnp.mean(x, axis=axis, keepdims=True)
    v = jnp.var(x, axis=axis, keepdims=True)
    return (x - m) / jnp.sqrt(v + eps)

def _scatter_add(tgt, idx, src, axis=0):
    return tgt.at[idx].add(src)

def _segment_sum(src, seg, n):
    return jax.ops.segment_sum(src, seg, n)
kernel_name = 'mk_lm_tower_d2_tok_ids256_r4_30bf47'

def setup_inputs(seed: int=0):
    np.random.seed(seed)
    _w = jnp.asarray

    def _rec_inputs():
        import jax
        import jax.numpy as jnp
        _rk = jax.random.key(seed)
        x = jax.random.randint(jax.random.fold_in(_rk, 1), (128, 200), 0, 50001, jnp.int32)
        return x
    x = _rec_inputs()

    def _L0_tok_setup():
        import jax, jax.numpy as jnp
        import numpy as np
        L = 2
        MAXLEN = 200
        HID = 64
        DFF = 4 * HID
        NITEM = 50001
        EPS = 1e-12

        def _ln(x, w, b):
            u = jnp.mean(x, axis=-1, keepdims=True)
            s = jnp.mean((x - u) ** 2, axis=-1, keepdims=True)
            return w * (x - u) / jnp.sqrt(s + EPS) + b
        key = jax.random.key(seed)
        ks = jax.random.split(key, 12)
        inp = {'input_ids': jax.random.randint(ks[0], (128, MAXLEN), 0, NITEM, dtype=jnp.int64), 'item_emb': jax.random.normal(ks[1], (NITEM, HID), jnp.float32) * 0.02, 'pos_emb': jax.random.normal(ks[2], (MAXLEN, HID), jnp.float32) * 0.02, 'ln0_w': jnp.ones((HID,), jnp.float32), 'ln0_b': jnp.zeros((HID,), jnp.float32), 'cw': jax.random.normal(ks[3], (L, MAXLEN // 2 + 1, HID, 2), jnp.float32) * 0.02, 'fln_w': jnp.ones((L, HID), jnp.float32), 'fln_b': jnp.zeros((L, HID), jnp.float32), 'd1_w': jax.random.normal(ks[4], (L, HID, DFF), jnp.float32) * 0.02, 'd1_b': jnp.zeros((L, DFF), jnp.float32), 'd2_w': jax.random.normal(ks[5], (L, DFF, HID), jnp.float32) * 0.02, 'd2_b': jnp.zeros((L, HID), jnp.float32), 'iln_w': jnp.ones((L, HID), jnp.float32), 'iln_b': jnp.zeros((L, HID), jnp.float32)}
        return inp
    _L0_tok_all = _L0_tok_setup()
    _L0_tok_in = {k: v for k, v in _L0_tok_all.items() if k in ('item_emb', 'pos_emb', 'ln0_w', 'ln0_b', 'cw', 'fln_w', 'fln_b', 'd1_w', 'd1_b', 'd2_w', 'd2_b', 'iln_w', 'iln_b')}
    del _L0_tok_all

    def _L0_attn_setup():
        import jax, jax.numpy as jnp
        import numpy as np
        import math
        PI = math.pi

        def _encode_phase(x, w1, b1, w2, b2):
            h = jnp.tanh(jnp.einsum('bld,ed->ble', x, w1) + b1)
            return jnp.tanh(jnp.einsum('bld,kd->blk', h, w2) + b2) * PI
        key = jax.random.key(seed)
        ks = jax.random.split(key, 12)
        B, L, D, K = (2, 512, 64, 32)
        s = 0.02
        return {'x': jax.random.normal(ks[0], (B, L, D), dtype=jnp.float32), 'kw1': jax.random.normal(ks[1], (D, D), dtype=jnp.float32) * s, 'kb1': jnp.zeros((D,), dtype=jnp.float32), 'kw2': jax.random.normal(ks[2], (K, D), dtype=jnp.float32) * s, 'kb2': jnp.zeros((K,), dtype=jnp.float32), 'qw1': jax.random.normal(ks[3], (D, D), dtype=jnp.float32) * s, 'qb1': jnp.zeros((D,), dtype=jnp.float32), 'qw2': jax.random.normal(ks[4], (K, D), dtype=jnp.float32) * s, 'qb2': jnp.zeros((K,), dtype=jnp.float32), 'vw': jax.random.normal(ks[5], (D, D), dtype=jnp.float32) * s, 'vb': jnp.zeros((D,), dtype=jnp.float32)}
    _L0_attn_all = _L0_attn_setup()
    _L0_attn_in = {k: v for k, v in _L0_attn_all.items() if k in ('kw1', 'kb1', 'kw2', 'kb2', 'qw1', 'qb1', 'qw2', 'qb2', 'vw', 'vb')}
    del _L0_attn_all

    def _L0_ffn_setup():
        import jax, jax.numpy as jnp
        import numpy as np
        B, T, IN_DIM = (64, 64, 64)
        HID, OUT_DIM = (128, 64)
        N_LAYERS, N_EXPERTS, N_SHARED = (2, 16, 1)
        key = jax.random.key(seed)
        ks = jax.random.split(key, 10)
        s = 0.02
        x = jax.random.normal(ks[0], (B, T, IN_DIM), dtype=jnp.float32)
        route_id = jax.random.randint(ks[1], (B,), 0, N_EXPERTS)
        Wi = jax.random.normal(ks[2], (HID, IN_DIM), dtype=jnp.float32) * s
        bi = jnp.zeros((HID,), dtype=jnp.float32)
        Wr = jax.random.normal(ks[3], (N_LAYERS, N_EXPERTS, HID, HID), dtype=jnp.float32) * s
        br = jax.random.normal(ks[4], (N_LAYERS, N_EXPERTS, HID), dtype=jnp.float32) * s
        Ws = jax.random.normal(ks[5], (N_LAYERS, N_SHARED, HID, HID), dtype=jnp.float32) * s
        bs = jax.random.normal(ks[6], (N_LAYERS, N_SHARED, HID), dtype=jnp.float32) * s
        Wo = jax.random.normal(ks[7], (OUT_DIM, HID), dtype=jnp.float32) * s
        bo = jnp.zeros((OUT_DIM,), dtype=jnp.float32)
        return {'x': x, 'route_id': route_id, 'Wi': Wi, 'bi': bi, 'Wr': Wr, 'br': br, 'Ws': Ws, 'bs': bs, 'Wo': Wo, 'bo': bo}
    _L0_ffn_all = _L0_ffn_setup()
    _L0_ffn_in = {k: v for k, v in _L0_ffn_all.items() if k in ('route_id', 'Wi', 'bi', 'Wr', 'br', 'Ws', 'bs', 'Wo', 'bo')}
    del _L0_ffn_all

    def _L1_attn_setup():
        import jax, jax.numpy as jnp
        import numpy as np
        BATCH, L, H, P = (8, 2048, 64, 64)
        DT_MIN, DT_MAX = (0.001, 0.1)

        def _binop(qi, qj):
            A_i, b_i = qi
            A_j, b_j = qj
            return (A_j * A_i, A_j * b_i + b_j)
        key = jax.random.key(seed)
        ks = jax.random.split(key, 8)
        signal = jax.random.normal(ks[0], (BATCH, L, H), dtype=jnp.float32)
        Lambda_re = -(0.1 + 0.5 * jax.random.uniform(ks[1], (P,), dtype=jnp.float32))
        Lambda_im = np.float32(np.pi) * jax.random.normal(ks[2], (P,), dtype=jnp.float32)
        B_ri = jax.random.normal(ks[3], (P, H, 2), dtype=jnp.float32) / np.float32(np.sqrt(2 * H))
        C_re = jax.random.normal(ks[4], (H, P), dtype=jnp.float32) / np.float32(np.sqrt(P))
        C_im = jax.random.normal(ks[5], (H, P), dtype=jnp.float32) / np.float32(np.sqrt(P))
        D = jax.random.uniform(ks[6], (H,), dtype=jnp.float32)
        log_step = jax.random.uniform(ks[7], (P,), dtype=jnp.float32, minval=np.float32(np.log(DT_MIN)), maxval=np.float32(np.log(DT_MAX)))
        return {'signal': signal, 'Lambda_re': Lambda_re, 'Lambda_im': Lambda_im, 'B_ri': B_ri, 'C_re': C_re, 'C_im': C_im, 'D': D, 'log_step': log_step}
    _L1_attn_all = _L1_attn_setup()
    _L1_attn_in = {k: v for k, v in _L1_attn_all.items() if k in ('Lambda_re', 'Lambda_im', 'B_ri', 'C_re', 'C_im', 'D', 'log_step')}
    del _L1_attn_all

    def _L1_ffn_setup():
        import jax, jax.numpy as jnp
        import numpy as np
        B, K, D = (128, 16, 64)
        E = 32
        H = int(D * 0.25)
        key = jax.random.key(seed)
        ks = jax.random.split(key, 7)
        d_rs = D ** (-0.5)
        h_rs = H ** (-0.5)
        x = jax.random.normal(ks[0], (B, K, D), dtype=jnp.float32)
        router_w = jax.random.uniform(ks[1], (E, D), jnp.float32, -d_rs, d_rs)
        router_b = jax.random.uniform(ks[2], (E,), jnp.float32, -d_rs, d_rs)
        W1 = jax.random.uniform(ks[3], (E, D, H), jnp.float32, -h_rs, h_rs)
        b1 = jax.random.uniform(ks[4], (E, H), jnp.float32, -h_rs, h_rs)
        W2 = jax.random.uniform(ks[5], (E, H, D), jnp.float32, -d_rs, d_rs)
        b2 = jax.random.uniform(ks[6], (E, D), jnp.float32, -d_rs, d_rs)
        return {'x': x, 'router_w': router_w, 'router_b': router_b, 'W1': W1, 'b1': b1, 'W2': W2, 'b2': b2}
    _L1_ffn_all = _L1_ffn_setup()
    _L1_ffn_in = {k: v for k, v in _L1_ffn_all.items() if k in ('router_w', 'router_b', 'W1', 'b1', 'W2', 'b2')}
    del _L1_ffn_all
    return {'x': x, 'L0_tok_item_emb': _L0_tok_in['item_emb'], 'L0_tok_pos_emb': _L0_tok_in['pos_emb'], 'L0_tok_ln0_w': _L0_tok_in['ln0_w'], 'L0_tok_ln0_b': _L0_tok_in['ln0_b'], 'L0_tok_cw': _L0_tok_in['cw'], 'L0_tok_fln_w': _L0_tok_in['fln_w'], 'L0_tok_fln_b': _L0_tok_in['fln_b'], 'L0_tok_d1_w': _L0_tok_in['d1_w'], 'L0_tok_d1_b': _L0_tok_in['d1_b'], 'L0_tok_d2_w': _L0_tok_in['d2_w'], 'L0_tok_d2_b': _L0_tok_in['d2_b'], 'L0_tok_iln_w': _L0_tok_in['iln_w'], 'L0_tok_iln_b': _L0_tok_in['iln_b'], 'L0_attn_kw1': _L0_attn_in['kw1'], 'L0_attn_kb1': _L0_attn_in['kb1'], 'L0_attn_kw2': _L0_attn_in['kw2'], 'L0_attn_kb2': _L0_attn_in['kb2'], 'L0_attn_qw1': _L0_attn_in['qw1'], 'L0_attn_qb1': _L0_attn_in['qb1'], 'L0_attn_qw2': _L0_attn_in['qw2'], 'L0_attn_qb2': _L0_attn_in['qb2'], 'L0_attn_vw': _L0_attn_in['vw'], 'L0_attn_vb': _L0_attn_in['vb'], 'L0_ffn_route_id': _L0_ffn_in['route_id'], 'L0_ffn_Wi': _L0_ffn_in['Wi'], 'L0_ffn_bi': _L0_ffn_in['bi'], 'L0_ffn_Wr': _L0_ffn_in['Wr'], 'L0_ffn_br': _L0_ffn_in['br'], 'L0_ffn_Ws': _L0_ffn_in['Ws'], 'L0_ffn_bs': _L0_ffn_in['bs'], 'L0_ffn_Wo': _L0_ffn_in['Wo'], 'L0_ffn_bo': _L0_ffn_in['bo'], 'L1_attn_Lambda_re': _L1_attn_in['Lambda_re'], 'L1_attn_Lambda_im': _L1_attn_in['Lambda_im'], 'L1_attn_B_ri': _L1_attn_in['B_ri'], 'L1_attn_C_re': _L1_attn_in['C_re'], 'L1_attn_C_im': _L1_attn_in['C_im'], 'L1_attn_D': _L1_attn_in['D'], 'L1_attn_log_step': _L1_attn_in['log_step'], 'L1_ffn_router_w': _L1_ffn_in['router_w'], 'L1_ffn_router_b': _L1_ffn_in['router_b'], 'L1_ffn_W1': _L1_ffn_in['W1'], 'L1_ffn_b1': _L1_ffn_in['b1'], 'L1_ffn_W2': _L1_ffn_in['W2'], 'L1_ffn_b2': _L1_ffn_in['b2']}

def reference(x, L0_tok_item_emb, L0_tok_pos_emb, L0_tok_ln0_w, L0_tok_ln0_b, L0_tok_cw, L0_tok_fln_w, L0_tok_fln_b, L0_tok_d1_w, L0_tok_d1_b, L0_tok_d2_w, L0_tok_d2_b, L0_tok_iln_w, L0_tok_iln_b, L0_attn_kw1, L0_attn_kb1, L0_attn_kw2, L0_attn_kb2, L0_attn_qw1, L0_attn_qb1, L0_attn_qw2, L0_attn_qb2, L0_attn_vw, L0_attn_vb, L0_ffn_route_id, L0_ffn_Wi, L0_ffn_bi, L0_ffn_Wr, L0_ffn_br, L0_ffn_Ws, L0_ffn_bs, L0_ffn_Wo, L0_ffn_bo, L1_attn_Lambda_re, L1_attn_Lambda_im, L1_attn_B_ri, L1_attn_C_re, L1_attn_C_im, L1_attn_D, L1_attn_log_step, L1_ffn_router_w, L1_ffn_router_b, L1_ffn_W1, L1_ffn_b1, L1_ffn_W2, L1_ffn_b2):
    import jax
    import jax.numpy as jnp

    def _L0_tok_ref(input_ids, item_emb, pos_emb, ln0_w, ln0_b, cw, fln_w, fln_b, d1_w, d1_b, d2_w, d2_b, iln_w, iln_b):
        import jax, jax.numpy as jnp
        import numpy as np
        L = 2
        MAXLEN = 200
        HID = 64
        DFF = 4 * HID
        NITEM = 50001
        EPS = 1e-12

        def _ln(x, w, b):
            u = jnp.mean(x, axis=-1, keepdims=True)
            s = jnp.mean((x - u) ** 2, axis=-1, keepdims=True)
            return w * (x - u) / jnp.sqrt(s + EPS) + b
        seq_len = input_ids.shape[1]
        x = item_emb[input_ids] + pos_emb[None, :, :]
        x = _ln(x, ln0_w, ln0_b)
        for l in range(L):
            f = jnp.fft.rfft(x, axis=1, norm='ortho')
            w = (cw[l, :, :, 0] + 1j * cw[l, :, :, 1])[None]
            y = jnp.fft.irfft(f * w, n=seq_len, axis=1, norm='ortho')
            x = _ln(y + x, fln_w[l], fln_b[l])
            h = jax.nn.gelu(jnp.einsum('bsh,hf->bsf', x, d1_w[l]) + d1_b[l], approximate=False)
            h = jnp.einsum('bsf,fh->bsh', h, d2_w[l]) + d2_b[l]
            x = _ln(h + x, iln_w[l], iln_b[l])
        return x

    def _L0_attn_ref(x, kw1, kb1, kw2, kb2, qw1, qb1, qw2, qb2, vw, vb):
        import jax, jax.numpy as jnp
        import numpy as np
        import math
        PI = math.pi

        def _encode_phase(x, w1, b1, w2, b2):
            h = jnp.tanh(jnp.einsum('bld,ed->ble', x, w1) + b1)
            return jnp.tanh(jnp.einsum('bld,kd->blk', h, w2) + b2) * PI
        B, L, D = x.shape
        key_phase = _encode_phase(x, kw1, kb1, kw2, kb2)
        query_phase = _encode_phase(x, qw1, qb1, qw2, qb2)
        K = key_phase.shape[-1]
        value = jnp.einsum('bld,ed->ble', x, vw) + vb
        cos_k = jnp.cos(key_phase)[..., None]
        sin_k = jnp.sin(key_phase)[..., None]
        v_exp = value[:, :, None, :]
        mem_real = jnp.cumsum(cos_k * v_exp, axis=1)
        mem_imag = jnp.cumsum(sin_k * v_exp, axis=1)
        cos_q = jnp.cos(query_phase)[..., None]
        sin_q = jnp.sin(query_phase)[..., None]
        retrieved = jnp.sum(mem_real * cos_q + mem_imag * sin_q, axis=2)
        positions = jnp.arange(1, L + 1, dtype=x.dtype)
        norm = jnp.sqrt(positions * K)[None, :, None]
        return retrieved / norm

    def _L0_ffn_ref(x, route_id, Wi, bi, Wr, br, Ws, bs, Wo, bo):
        import jax, jax.numpy as jnp
        import numpy as np
        B, T, IN_DIM = (64, 64, 64)
        HID, OUT_DIM = (128, 64)
        N_LAYERS, N_EXPERTS, N_SHARED = (2, 16, 1)
        flat = x.reshape(-1, x.shape[-1])
        n_tok = flat.shape[0]
        route = jnp.repeat(route_id, n_tok // route_id.shape[0])
        h = jax.nn.relu(flat @ Wi.T + bi)
        n_layers, n_experts = (Wr.shape[0], Wr.shape[1])
        for l in range(n_layers):
            shared = (jnp.einsum('nd,shd->snh', h, Ws[l]) + bs[l][:, None, :]).mean(axis=0)
            routed = jnp.zeros_like(h)
            for e in range(n_experts):
                ye = h @ Wr[l, e].T + br[l, e]
                routed = routed + jnp.where((route == e)[:, None], ye, 0.0)
            h = jax.nn.relu(shared + routed + h)
        out = h @ Wo.T + bo
        return out.reshape(*x.shape[:-1], out.shape[-1])

    def _L1_attn_ref(signal, Lambda_re, Lambda_im, B_ri, C_re, C_im, D, log_step):
        import jax, jax.numpy as jnp
        import numpy as np
        BATCH, L, H, P = (8, 2048, 64, 64)
        DT_MIN, DT_MAX = (0.001, 0.1)

        def _binop(qi, qj):
            A_i, b_i = qi
            A_j, b_j = qj
            return (A_j * A_i, A_j * b_i + b_j)
        Lam = jax.lax.complex(Lambda_re, Lambda_im)
        B_tilde = jax.lax.complex(B_ri[..., 0], B_ri[..., 1])
        C_tilde = jax.lax.complex(C_re, C_im)
        Delta = jnp.exp(log_step)
        Lambda_bar = jnp.exp(Lam * Delta)
        B_bar = ((Lambda_bar - 1.0) / Lam)[:, None] * B_tilde
        Bu = jnp.einsum('ph,blh->blp', B_bar, signal.astype(B_bar.dtype))
        A = jnp.broadcast_to(Lambda_bar, Bu.shape)
        _, xs = jax.lax.associative_scan(_binop, (A, Bu), axis=1)
        y = jnp.einsum('hp,blp->blh', C_tilde, xs).real + D * signal
        return y

    def _L1_ffn_ref(x, router_w, router_b, W1, b1, W2, b2):
        import jax, jax.numpy as jnp
        import numpy as np
        B, K, D = (128, 16, 64)
        E = 32
        H = int(D * 0.25)
        xf = x.reshape(-1, D)
        logits = xf @ router_w.T + router_b
        idx = jnp.argmax(logits, axis=-1)
        w1t = jnp.take(W1, idx, axis=0)
        h = jnp.einsum('nd,ndh->nh', xf, w1t) + jnp.take(b1, idx, axis=0)
        h = jax.nn.relu(h)
        w2t = jnp.take(W2, idx, axis=0)
        out = jnp.einsum('nh,nhd->nd', h, w2t) + jnp.take(b2, idx, axis=0)
        out = jax.nn.relu(out)
        return out.reshape(x.shape)
    h = _L0_tok_ref(x, L0_tok_item_emb, L0_tok_pos_emb, L0_tok_ln0_w, L0_tok_ln0_b, L0_tok_cw, L0_tok_fln_w, L0_tok_fln_b, L0_tok_d1_w, L0_tok_d1_b, L0_tok_d2_w, L0_tok_d2_b, L0_tok_iln_w, L0_tok_iln_b)
    h = h + _L0_attn_ref(_layernorm(h, axis=-1), L0_attn_kw1, L0_attn_kb1, L0_attn_kw2, L0_attn_kb2, L0_attn_qw1, L0_attn_qb1, L0_attn_qw2, L0_attn_qb2, L0_attn_vw, L0_attn_vb)
    h = h + _L0_ffn_ref(_layernorm(h, axis=-1), L0_ffn_route_id, L0_ffn_Wi, L0_ffn_bi, L0_ffn_Wr, L0_ffn_br, L0_ffn_Ws, L0_ffn_bs, L0_ffn_Wo, L0_ffn_bo)
    h = h + _L1_attn_ref(_layernorm(h, axis=-1), L1_attn_Lambda_re, L1_attn_Lambda_im, L1_attn_B_ri, L1_attn_C_re, L1_attn_C_im, L1_attn_D, L1_attn_log_step)
    h = h + _L1_ffn_ref(_layernorm(h, axis=-1), L1_ffn_router_w, L1_ffn_router_b, L1_ffn_W1, L1_ffn_b1, L1_ffn_W2, L1_ffn_b2)
    return h

_drawn_inputs = setup_inputs


def setup_inputs(seed=0):
    import zlib

    import numpy as np

    out = dict(_drawn_inputs(seed))
    spreads = {'L0_tok_ln0_w': (1.0, 0.2),
     'L0_tok_ln0_b': (0.0, 0.1),
     'L0_tok_fln_w': (1.0, 0.2),
     'L0_tok_fln_b': (0.0, 0.1),
     'L0_tok_d1_b': (0.0, 0.279),
     'L0_tok_d2_b': (0.0, 0.1),
     'L0_tok_iln_w': (1.0, 0.2),
     'L0_tok_iln_b': (0.0, 0.1),
     'L0_attn_kb1': (0.0, 0.8),
     'L0_attn_kb2': (0.0, 0.1),
     'L0_attn_qb1': (0.0, 0.8),
     'L0_attn_qb2': (0.0, 0.1),
     'L0_attn_vb': (0.0, 0.1),
     'L0_ffn_bi': (0.0, 0.8),
     'L0_ffn_bo': (0.0, 0.434)}
    factors = {'L0_tok_cw': 4.677,
     'L0_tok_d1_w': 4.859,
     'L0_attn_kw1': 8.0,
     'L0_attn_kw2': 8.0,
     'L0_attn_qw1': 8.0,
     'L0_attn_qw2': 8.0,
     'L0_ffn_Wi': 8.0,
     'L0_ffn_Wr': 8.0,
     'L0_ffn_br': 8.0,
     'L0_ffn_Ws': 8.0,
     'L0_ffn_bs': 8.0,
     'L0_ffn_Wo': 6.931,
     'L1_ffn_router_b': 2.858,
     'L1_ffn_W1': 2.758,
     'L1_ffn_b1': 35.109,
     'L1_ffn_b2': 7.539}
    for name, (base, spread) in spreads.items():
        noise = np.random.default_rng([zlib.crc32(name.encode()), seed]).standard_normal(out[name].shape)
        drawn = base * np.exp(spread * noise) if base else spread * noise
        out[name] = jnp.asarray(drawn.astype(out[name].dtype))
    for name, factor in factors.items():
        out[name] = (out[name] * factor).astype(out[name].dtype)
    return out
```

```python
from contextlib import ExitStack

import concourse.bass as bass
from concourse import mybir

F32 = mybir.dt.float32
BF16 = mybir.dt.bfloat16
I32 = mybir.dt.int32
ACT = mybir.ActivationFunctionType
ALU = mybir.AluOpType
AX_X = mybir.AxisListType.X

NB, SEQ, HID = 128, 200, 64
NJ = SEQ // 2
PC = 2 * HID
DFF, LAYERS = 256, 2
SEQ_TILE = 4
COLS = SEQ_TILE * NJ
SEQ_TILES = NB // SEQ_TILE
PAIR_TILE = 4
PCOLS = PAIR_TILE * NB
PAIR_TILES = NJ // PAIR_TILE
NLAG = 2 * SEQ
PHASES = 32
LH = 128
NEXP0, NGROUP = 16, 64
GCOLS = 2 * NJ
NEXP1, EH = 32, 16
FCH = NEXP1 * EH // 128
SLOT = LH + 1
PI = 3.141592653589793
BIG = 2.0 ** 100


def at_least(eng, sem, value):
    if isinstance(value, int) and value <= 0:
        return
    eng.wait_ge(sem, value)


def run_steps(eng, tiles, skew, step):
    first = skew + 2 + skew % 2
    turns = (tiles - first) // 2
    for t in range(first):
        step(t, t % 2)
    with eng.Fori(0, turns) as i:
        for u in range(2):
            step(2 * i + (first + u), u)
    for t in range(first + 2 * turns, tiles + skew):
        step(t, t % 2)


def half(t, parity):
    return (t - parity) // 2


def exists(n, tiles):
    return not isinstance(n, int) or 0 <= n < tiles


def ds(start, size):
    return bass.ds(start, size)


def clear_all(nc, sems):
    with nc.Block() as block:
        @block.sync
        def _(sp):
            for s in sems:
                sp.sem_clear(s)



class Norm:

    def __init__(self, ctx, nc, sem, tag, cols, eps, parts=1):
        self.eps, self.cols, self.parts = eps, cols, parts
        self.centered = ctx.enter_context(nc.psum_tensor(f"{tag}_centered", [128, 512], F32))
        self.variance = ctx.enter_context(nc.psum_tensor(f"{tag}_variance", [128, 512], F32))
        self.square = ctx.enter_context(nc.sbuf_tensor(f"{tag}_square", [128, cols], F32))
        self.logvar = ctx.enter_context(nc.sbuf_tensor(f"{tag}_logvar", [128, cols], F32))
        self.rstd = ctx.enter_context(nc.sbuf_tensor(f"{tag}_rstd", [128, cols], F32))
        self.centered_ready, self.square_ready = sem("n_centered_ready"), sem("n_square_ready")
        self.variance_ready, self.log_ready = sem("n_variance_ready"), sem("n_log_ready")
        self.rstd_ready, self.norm_done = sem("n_rstd_ready"), sem("n_norm_done")


def pe_variance(pe, G, L, n):
    at_least(pe, L.square_ready, n + 1)
    at_least(pe, L.log_ready, n)
    pe.matmul(L.variance[:, 0:L.cols], G.mean_m[:], L.square[:, :], start=True,
              stop=True).then_inc(L.variance_ready, 1)


def act_square(act, L, n, bias=0.0):
    at_least(act, L.centered_ready, n + 1)
    at_least(act, L.variance_ready, n)
    act.activation(L.square[:, :], L.centered[:, 0:L.cols], ACT.Square,
                   bias=bias).then_inc(L.square_ready, 1)


def act_rstd(act, L, n):
    at_least(act, L.variance_ready, n + 1)
    at_least(act, L.rstd_ready, n)
    act.activation(L.logvar[:, :], L.variance[:, 0:L.cols], ACT.Ln,
                   bias=L.eps).then_inc(L.log_ready, 1)
    at_least(act, L.log_ready, n + 1)
    at_least(act, L.norm_done, L.parts * n)
    act.activation(L.rstd[:, :], L.logvar[:, :], ACT.Exp, scale=-0.5).then_inc(L.rstd_ready, 1)



def phase_embed(nc, G):
    D = G.dram
    with ExitStack() as ctx:
        sb = lambda n, s, d=F32: ctx.enter_context(nc.sbuf_tensor(n, s, d))
        pt = lambda n: ctx.enter_context(nc.psum_tensor(n, [128, 512], F32))
        sem = lambda n: G.ctx.enter_context(nc.semaphore("e_" + n))
        L = Norm(ctx, nc, sem, "e", COLS, 1e-12)
        ids = sb("e_ids", [NJ, 2 * NB], I32)
        ids_tile = sb("e_ids_tile", [NJ, 2, 2 * SEQ_TILE], I32)
        rows = sb("e_rows", [NJ, 2, SEQ_TILE * PC])
        z = sb("e_z", [128, COLS])
        y = sb("e_y", [128, COLS])
        x0 = sb("e_x0", [128, 2, COLS])
        pos = sb("e_pos", [128, NJ])
        cw = sb("e_cw", [101, LAYERS, 2, HID])
        dft = sb("e_dft", [101, 2, NLAG])
        lag = sb("e_lag", [HID, LAYERS, NLAG])
        d2t = sb("e_d2t", [HID, LAYERS, DFF])
        d2b = sb("e_d2b", [128, LAYERS])
        pz, pback, pk0, pk1 = pt("e_pz"), pt("e_pback"), pt("e_pk0"), pt("e_pk1")
        pk = [pk0, pk1]
        ids_here, loads = sem("ids_here"), sem("loads")
        ids_copied, tile_begun = sem("ids_copied"), sem("tile_begun")
        rows_here = [sem("rows_here0"), sem("rows_here1")]
        z_turned, z_ready, x0_ready = sem("z_turned"), sem("z_ready"), sem("x0_ready")
        back_turned, back_done = sem("back_turned"), sem("back_done")
        lag_copied = sem("lag_copied")
        prep_made, prep_copied, prep_out = sem("prep_made"), sem("prep_copied"), sem("prep_out")
        pairs = [(ids, D["ids"])]
        weights = [(G.ident, D["ident"]), (G.flip, D["flip"]), (G.center_m, D["center_m"]), (G.mean_m, D["mean_m"]),
                   (pos, D["pos"]), (G.vec, D["vec"]), (cw, D["cw"]), (dft, D["dft"]),
                   (d2t, D["d2t"]), (d2b, D["d2b"]), (G.d1, D["d1"]), (G.gelu_b, D["gelu_b"])]

        with nc.Block() as block:
            @block.sync
            def _(sp):
                for dst, src in pairs:
                    sp.dma_start(dst[:], src).then_inc(ids_here, 16)
                for dst, src in weights:
                    sp.dma_start(dst[:], src).then_inc(loads, 16)
                sp.wait_ge(prep_copied, 2)
                for l in range(LAYERS):
                    sp.dma_start(G.lag_dram[l], lag[:, l, :]).then_inc(prep_out, 16)
                sp.wait_ge(prep_out, 16 * LAYERS)

            @block.gpsimd
            def _(pool):
                pool.wait_ge(ids_here, 16)

                def step(t, k):
                    at_least(pool, z_turned, t - 1)
                    pool.tensor_copy(ids_tile[:, k, :],
                                     ids[:, ds(t * 2 * SEQ_TILE, 2 * SEQ_TILE)]).then_inc(ids_copied, 1)
                    pool.wait_ge(ids_copied, t + 1)
                    pool.sem_inc(tile_begun, 1)
                    for q in range(2 * SEQ_TILE):
                        pool.indirect_dma_start(
                            rows[:, k, q * HID:(q + 1) * HID], None, D["item_emb"],
                            bass.IndirectOffsetOnAxis(ap=ids_tile[:, k, q:q + 1], axis=0)
                        ).then_inc(rows_here[k], 16)
                run_steps(pool, SEQ_TILES, 0, step)

            @block.tensor
            def _(pe):
                pe.wait_ge(loads, 16 * len(weights))
                for l in range(LAYERS):
                    for c in range(2):
                        mm = pe.matmul(pk[l][0:HID, 0:NLAG], cw[:, l, c, :], dft[:, c, :],
                                       start=(c == 0), stop=(c == 1))
                    mm.then_inc(prep_made, 1)
                pe.wait_ge(prep_copied, 2)
                for l in range(LAYERS):
                    for ck in range(2):
                        mm = pe.matmul(pk0[:, (2 * l + ck) * HID:(2 * l + ck + 1) * HID],
                                       d2t[:, l, ck * 128:(ck + 1) * 128], G.center_m[0:HID, 0:HID],
                                       start=True, stop=True)
                pe.matmul(pk1[:, 0:LAYERS], G.center_m[:], d2b[:, :], start=True,
                          stop=True).then_inc(prep_made, 1)

                def step(t, k):
                    n = t
                    if exists(n, SEQ_TILES):
                        pe.wait_ge(rows_here[k], 128 * half(n, k) + 128)
                        at_least(pe, z_ready, n)
                        for q in range(SEQ_TILE):
                            mm = pe.transpose(pz[:, q * NJ:(q + 1) * NJ], rows[:, k, q * PC:(q + 1) * PC],
                                              G.ident[0:NJ, 0:NJ])
                        mm.then_inc(z_turned, 1)
                        pe.wait_ge(z_ready, n + 1)
                        at_least(pe, L.norm_done, n)
                        pe.matmul(L.centered[:, 0:COLS], G.center_m[:], z[:, :], start=True,
                                  stop=True).then_inc(L.centered_ready, 1)
                        pe_variance(pe, G, L, n)
                    m = t - 1
                    if exists(m, SEQ_TILES):
                        pe.wait_ge(x0_ready, m + 1)
                        at_least(pe, back_done, m)
                        for q in range(SEQ_TILE):
                            mm = pe.transpose(pback[0:NJ, q * PC:(q + 1) * PC],
                                              x0[:, 1 - k, q * NJ:(q + 1) * NJ], G.ident[:])
                        mm.then_inc(back_turned, 1)
                run_steps(pe, SEQ_TILES, 1, step)

            @block.scalar
            def _(act):
                act.preload_act_table_set("natural_log_exp_and_others")
                act.wait_ge(loads, 16 * len(weights))

                def step(t, k):
                    act_square(act, L, t)
                    act_rstd(act, L, t)
                    at_least(act, L.norm_done, t + 1)
                    at_least(act, back_turned, t - 1)
                    act.activation(x0[:, k, :], y[:, :], ACT.Identity, bias=G.vec[:, 1:2],
                                   scale=G.vec[:, 0:1]).then_inc(x0_ready, 1)
                run_steps(act, SEQ_TILES, 0, step)

            @block.vector
            def _(dve):
                for l in range(LAYERS):
                    dve.wait_ge(prep_made, l + 1)
                    dve.tensor_copy(lag[:, l, :], pk[l][0:HID, 0:NLAG]).then_inc(lag_copied, 1)
                    dve.wait_ge(lag_copied, l + 1)
                    dve.tensor_scalar(lag[:, l, SEQ - 1:SEQ], pk[l][0:HID, SEQ - 1:SEQ], 1.0, None,
                                      ALU.add).then_inc(prep_copied, 1)
                dve.wait_ge(prep_made, 3)
                dve.tensor_copy(G.d2c[:], pk0[:, 0:4 * HID].rearrange("p (l c h) -> p l c h", l=2, c=2))
                dve.tensor_copy(G.d2bc[:], pk1[:, 0:LAYERS])

                def step(t, k):
                    if exists(t, SEQ_TILES):
                        dve.wait_ge(z_turned, t + 1)
                        at_least(dve, L.centered_ready, t)
                        dve.tensor_tensor(z[:].rearrange("p (b j) -> p b j", j=NJ),
                                          pz[:, 0:COLS].rearrange("p (b j) -> p b j", j=NJ),
                                          pos[:].unsqueeze(1).to_broadcast([128, SEQ_TILE, NJ]),
                                          ALU.add).then_inc(z_ready, 1)
                        dve.wait_ge(L.rstd_ready, t + 1)
                        at_least(dve, x0_ready, t)
                        dve.tensor_tensor(y[:, :], L.centered[:, 0:COLS], L.rstd[:, :],
                                          ALU.mult).then_inc(L.norm_done, 1)
                    m = t - 1
                    if exists(m, SEQ_TILES):
                        dve.wait_ge(back_turned, m + 1)
                        dve.tensor_copy(G.bp[:, :, ds(m * SEQ_TILE, SEQ_TILE)].rearrange("p f b -> p b f"),
                                        pback[0:NJ, :].rearrange("p (b f) -> p b f", f=PC)
                                        ).then_inc(back_done, 1)
                run_steps(dve, SEQ_TILES, 1, step)



def phase_conv(nc, G, layer):
    with ExitStack() as ctx:
        tag = f"c{layer}_"
        sems = []

        def sem(name):
            sems.append(ctx.enter_context(nc.semaphore(tag + name)))
            return sems[-1]
        toep = ctx.enter_context(nc.sbuf_tensor(tag + "toep", [NJ, 2, 2, SEQ + 1], F32))
        po = [ctx.enter_context(nc.psum_tensor(f"{tag}po{i}", [128, 512], F32)) for i in range(2)]
        toep_here = [sem("toep_here0"), sem("toep_here1")]
        conv_made, po_out = sem("conv_made"), [sem("po_out0"), sem("po_out1")]
        steps = HID // 2

        with nc.Block() as block:
            @block.sync
            def _(sp):
                def step(t, k):
                    at_least(sp, conv_made, t - 1)
                    src = bass.AP(G.lag_dram.tensor, G.lag_dram[layer].offset + t * (2 * NLAG),
                                  [[2, NJ], [NLAG, 2], [1, SEQ + 1]])
                    sp.dma_start(toep[:, k, :, :], src).then_inc(toep_here[k], 16)
                run_steps(sp, steps, 0, step)

            @block.tensor
            def _(pe):
                def step(t, k):
                    pe.wait_ge(toep_here[k], 16 * half(t, k) + 16)
                    at_least(pe, po_out[k], half(t, k))
                    for ch in range(2):
                        for po_par in range(2):
                            for in_par in range(2):
                                a = 1 - po_par + in_par
                                mm = pe.matmul(
                                    po[k][0:NJ, (2 * po_par + ch) * NB:(2 * po_par + ch + 1) * NB],
                                    toep[:, k, ch, a:a + SEQ - 1:2],
                                    G.bp[:, ds(2 * t + (in_par * HID + ch), 1), :].rearrange("p f b -> p (f b)"),
                                    start=(in_par == 0), stop=(in_par == 1))
                    mm.then_inc(conv_made, 1)
                run_steps(pe, steps, 0, step)

            def out_ap(t):
                return G.y.rearrange("p b (o c) -> p o c b", o=2)[:, :, ds(2 * t, 2), :]

            def in_ap(k):
                return po[k][0:NJ, :].rearrange("p (o c b) -> p o c b", o=2, c=2)

            @block.vector
            def _(dve):
                def step(t, k):
                    if k == 0:
                        dve.wait_ge(conv_made, t + 1)
                        dve.tensor_copy(out_ap(t), in_ap(0)).then_inc(po_out[0], 1)
                run_steps(dve, steps, 0, step)

            @block.scalar
            def _(act):
                def step(t, k):
                    if k == 1:
                        act.wait_ge(conv_made, t + 1)
                        act.activation(out_ap(t), in_ap(1), ACT.Identity).then_inc(po_out[1], 1)
                run_steps(act, steps, 0, step)
        clear_all(nc, sems)



def phase_ffn(nc, G, layer):
    last = layer == LAYERS - 1
    NT = SEQ_TILES
    with ExitStack() as ctx:
        tag = f"f{layer}_"
        sb = lambda n, s, d=F32: ctx.enter_context(nc.sbuf_tensor(tag + n, s, d))
        pt = lambda n: ctx.enter_context(nc.psum_tensor(tag + n, [128, 512], F32))
        sems = []

        def sem(name):
            sems.append(ctx.enter_context(nc.semaphore(tag + name)))
            return sems[-1]
        L1 = Norm(ctx, nc, lambda n: sem("1" + n), tag + "n1", COLS, 1e-12)
        L2 = Norm(ctx, nc, lambda n: sem("2" + n), tag + "n2", COLS, 1e-12)
        rows = sb("rows", [NJ, 2, SEQ_TILE * PC])
        z = sb("z", [128, COLS])
        y1 = sb("y1", [128, COLS])
        x1 = sb("x1", [128, 2, COLS])
        y2 = sb("y2", [128, COLS])
        x2 = sb("x2", [128, 2, COLS])
        g = sb("g", [128, 4, COLS])
        pz, pback = pt("pz"), pt("pback")
        pf = [pt("pf0"), pt("pf1")]
        rows_here = [sem("rows_here0"), sem("rows_here1")]
        z_turned, z_ready, x1_ready = sem("z_turned"), sem("z_ready"), sem("x1_ready")
        up_made, gelu_done, begun = sem("up_made"), sem("gelu_done"), sem("begun")
        x2_ready, back_turned, back_done = sem("x2_ready"), sem("back_turned"), sem("back_done")
        w = lambda i: G.vec[:, i:i + 1]
        fw, fb, iw, ib = w(2 + layer), w(4 + layer), w(6 + layer), w(8 + layer)

        with nc.Block() as block:
            @block.sync
            def _(sp):
                def step(t, k):
                    at_least(sp, z_turned, t - 1)
                    sp.dma_start(rows[:, k, :], G.y_flat[:, ds(t * (SEQ_TILE * PC), SEQ_TILE * PC)]
                                 ).then_inc(rows_here[k], 16)
                run_steps(sp, NT, 0, step)

            @block.tensor
            def _(pe):
                def step(t, k):
                    n, m, r = t, t - 2, t - 3
                    if exists(n, NT):
                        pe.wait_ge(rows_here[k], 16 * half(n, k) + 16)
                        at_least(pe, z_ready, n)
                        for q in range(SEQ_TILE):
                            mm = pe.transpose(pz[:, q * NJ:(q + 1) * NJ], rows[:, k, q * PC:(q + 1) * PC],
                                              G.flip[:])
                        mm.then_inc(z_turned, 1)
                    if exists(m, NT):
                        pe.wait_ge(x1_ready, m + 1)
                        for q in range(4):
                            at_least(pe, gelu_done, 4 * m + q - 1)
                            par, ck = q // 2, q % 2
                            pe.matmul(pf[q % 2][:, 0:COLS], G.d1[:, layer, par, ck * 128:(ck + 1) * 128],
                                      x1[:, k, :], start=True, stop=True).then_inc(up_made, 1)
                    if exists(n, NT):
                        pe.wait_ge(z_ready, n + 1)
                        at_least(pe, L1.norm_done, n)
                        pe.matmul(L1.centered[:, 0:COLS], G.center_m[:], z[:, :], start=True,
                                  stop=True).then_inc(L1.centered_ready, 1)
                    if exists(m, NT):
                        at_least(pe, L2.norm_done, m)
                        pe.matmul(L2.centered[:, 0:COLS], G.center_m[:], x1[:, k, :], start=True,
                                  stop=False, skip_group_check=True)
                        pe.wait_ge(gelu_done, 4 * m + 4)
                        for ck in range(2):
                            for par in range(2):
                                mm = pe.matmul(L2.centered[par * HID:(par + 1) * HID, 0:COLS],
                                               G.d2c[:, layer, ck, :], g[:, 2 * par + ck, :],
                                               start=False, stop=(ck == 1), skip_group_check=True)
                        mm.then_inc(L2.centered_ready, 1)
                    if exists(n, NT):
                        pe_variance(pe, G, L1, n)
                    if exists(m, NT):
                        pe_variance(pe, G, L2, m)
                    if exists(r, NT) and not last:
                        pe.wait_ge(x2_ready, r + 1)
                        at_least(pe, back_done, r)
                        for q in range(SEQ_TILE):
                            mm = pe.transpose(pback[0:NJ, q * PC:(q + 1) * PC],
                                              x2[:, 1 - k, q * NJ:(q + 1) * NJ], G.ident[:])
                        mm.then_inc(back_turned, 1)
                run_steps(pe, NT, 3, step)

            @block.scalar
            def _(act):
                def step(t, k):
                    n, m = t, t - 2
                    if exists(m, NT):
                        at_least(act, L2.centered_ready, m)
                        for q in range(4):
                            at_least(act, up_made, 4 * m + q + 1)
                            act.activation(g[:, q, :], pf[q % 2][:, 0:COLS], ACT.Gelu,
                                           bias=G.gelu_b[:, layer, q % 2:q % 2 + 1]).then_inc(gelu_done, 1)
                    if exists(n, NT):
                        act_square(act, L1, n)
                    if exists(m, NT):
                        act_square(act, L2, m, bias=G.d2bc[:, layer:layer + 1])
                    act.preload_act_table_set("natural_log_exp_and_others")
                    if exists(n, NT):
                        act_rstd(act, L1, n)
                    if exists(m, NT):
                        act_rstd(act, L2, m)
                run_steps(act, NT, 2, step)

            @block.vector
            def _(dve):
                def step(t, k):
                    n, m, r = t, t - 2, t - 3
                    if exists(n, NT):
                        dve.wait_ge(z_turned, n + 1)
                        at_least(dve, L1.centered_ready, n)
                        dve.tensor_copy(z[:, :], pz[:, 0:COLS]).then_inc(z_ready, 1)
                        dve.wait_ge(L1.rstd_ready, n + 1)
                        at_least(dve, x1_ready, n)
                        dve.tensor_tensor(y1[:, :], L1.centered[:, 0:COLS], L1.rstd[:, :],
                                          ALU.mult).then_inc(L1.norm_done, 1)
                    if exists(m, NT):
                        dve.wait_ge(L2.rstd_ready, m + 1)
                        at_least(dve, x2_ready, m)
                        dve.scalar_tensor_tensor(out=y2[:, :], in0=L2.centered[:, 0:COLS],
                                                 scalar=G.d2bc[:, layer:layer + 1], in1=L2.rstd[:, :],
                                                 op0=ALU.add, op1=ALU.mult).then_inc(L2.norm_done, 1)
                        if last:
                            dve.wait_ge(L2.norm_done, m + 1)
                            dve.tensor_scalar(G.t_flat[:, ds(m * COLS, COLS)], y2[:, :], iw, ib, ALU.mult,
                                              ALU.add).then_inc(x2_ready, 1)
                    if exists(r, NT) and not last:
                        dve.wait_ge(back_turned, r + 1)
                        dve.tensor_copy(G.bp[:, :, ds(r * SEQ_TILE, SEQ_TILE)].rearrange("p f b -> p b f"),
                                        pback[0:NJ, :].rearrange("p (b f) -> p b f", f=PC)
                                        ).then_inc(back_done, 1)
                run_steps(dve, NT, 3, step)

            @block.gpsimd
            def _(pool):
                def step(t, k):
                    n, m = t, t - 2
                    if exists(n, NT):
                        pool.wait_ge(L1.norm_done, n + 1)
                        at_least(pool, L2.centered_ready, n - 1)
                        pool.sem_inc(begun, 1)
                        pool.tensor_scalar(x1[:, k, :], y1[:, :], fw, fb, ALU.mult,
                                           ALU.add).then_inc(x1_ready, 1)
                    if exists(m, NT) and not last:
                        pool.wait_ge(L2.norm_done, m + 1)
                        at_least(pool, back_turned, m - 1)
                        pool.sem_inc(begun, 1)
                        pool.tensor_scalar(x2[:, k, :], y2[:, :], iw, ib, ALU.mult, ALU.add).then_inc(x2_ready, 1)
                run_steps(pool, NT, 2, step)
        clear_all(nc, sems)



def phase_attention(nc, G):
    D, NT = G.dram, SEQ_TILES
    with ExitStack() as ctx:
        sb = lambda n, s, d=F32: ctx.enter_context(nc.sbuf_tensor("a_" + n, s, d))
        pt = lambda n: ctx.enter_context(nc.psum_tensor("a_" + n, [128, 512], F32))
        sem = lambda n: G.ctx.enter_context(nc.semaphore("a_" + n))
        L = Norm(ctx, nc, sem, "a", COLS, 1e-5, parts=2)
        TOK = SEQ_TILE * SEQ
        w1, w2, vw = sb("w1", [128, 128]), sb("w2", [128, 128]), sb("vw", [128, HID])
        mask, vb, vec = sb("mask", [NJ, 3 * NJ]), sb("vb", [NJ, HID]), sb("vec", [128, 8])
        xn = sb("xn", [128, 2, TOK])
        hid, phase, folded = sb("hid", [128, TOK]), sb("phase", [128, TOK]), sb("folded", [128, TOK])
        phik, phiq = sb("phik", [128, 2, TOK]), sb("phiq", [128, 2, TOK])
        v = sb("v", [NJ, 2, 2 * SEQ_TILE * HID])
        probs = sb("probs", [NJ, 2, 3 * NJ])
        wbase, rt = sb("wbase", [128, 2, SLOT]), sb("rt", [1, NGROUP], I32)
        r1, r2, r3 = (sb(f"r{i}", [1, NGROUP]) for i in range(3))
        pw = [pt("pw0"), pt("pw1")]
        pv, po = pt("pv"), pt("po")
        ps = [pt("ps0"), pt("ps1")]
        loads, cleared, table_ready = sem("loads"), sem("cleared"), sem("table_ready")
        chain = sem("chain")
        proj_made, tanh_done, folded_ready, phi_ready = sem("proj_made"), sem("tanh_done"), sem("folded_ready"), sem("phi_ready")
        v_made, v_ready = sem("v_made"), sem("v_ready")
        score_made, probs_ready, out_made, stream_done = sem("score_made"), sem("probs_ready"), sem("out_made"), sem("stream_done")
        weights = [(w1, D["a_w1"]), (w2, D["a_w2"]), (vw, D["a_vw"]), (mask, D["a_mask"]), (vb, D["a_vb"]),
                   (vec, D["a_vec"]), (G.expert_w, D["r_w"]), (wbase, D["r_base"]), (rt, D["route"])]

        with nc.Block() as block:
            @block.sync
            def _(sp):
                for dst, src in weights:
                    sp.dma_start(dst[:], src).then_inc(loads, 16)

            @block.gpsimd
            def _(pool):
                pool.memset(xn[HID:128, :, :], 0.0).then_inc(cleared, 1)
                pool.memset(phik[HID:128, :, :], 0.0).then_inc(cleared, 1)
                pool.memset(phiq[HID:128, :, :], 0.0).then_inc(cleared, 1)
                pool.wait_ge(loads, 16 * len(weights))
                pool.wait_ge(cleared, 3)
                for l in range(2):
                    pool.tensor_tensor(wbase[:, l, 0:LH], wbase[:, l, 0:LH], G.ident[:],
                                       ALU.add).then_inc(table_ready, 1)
                pool.wait_ge(table_ready, 2)
                for l in range(2):
                    pool.tensor_tensor(G.expert_w[:, l, :, :], G.expert_w[:, l, :, :],
                                       wbase[:, l, :].unsqueeze(1).to_broadcast([128, NEXP0 + 1, SLOT]),
                                       ALU.add)

            @block.tensor
            def _(pe):
                pe.wait_ge(loads, 16 * len(weights))
                pe.wait_ge(cleared, 3)

                def step(t, k):
                    n, m, r = t, t - 1, t - 2
                    if exists(n, NT):
                        at_least(pe, L.norm_done, 2 * n)
                        pe.matmul(L.centered[:, 0:COLS], G.center_m[:], G.t_flat[:, ds(n * COLS, COLS)],
                                  start=True, stop=True).then_inc(L.centered_ready, 1)
                    if exists(m, NT):
                        pe.wait_ge(L.norm_done, 2 * m + 2)
                        for h in range(2):
                            at_least(pe, tanh_done, 4 * m - 2 + h + 1)
                            pe.matmul(pw[h][:, 0:COLS], w1[:], xn[:, 1 - k, h * COLS:(h + 1) * COLS],
                                      start=True, stop=True).then_inc(proj_made, 1)
                        at_least(pe, v_ready, m)
                        for c in range(2 * SEQ_TILE):
                            mm = pe.matmul(pv[0:NJ, c * HID:(c + 1) * HID], xn[:, 1 - k, c * NJ:(c + 1) * NJ],
                                           vw[:], start=True, stop=True)
                        mm.then_inc(v_made, 1)
                    if exists(n, NT):
                        pe_variance(pe, G, L, n)
                    if exists(m, NT):
                        for h in range(2):
                            pe.wait_ge(tanh_done, 4 * m + h + 1)
                            pe.matmul(pw[h][:, 0:COLS], w2[:], hid[:, h * COLS:(h + 1) * COLS],
                                      start=True, stop=True).then_inc(proj_made, 1)
                    if exists(r, NT):
                        at_least(pe, stream_done, r)

                        def scores(b):
                            at_least(pe, probs_ready, SEQ_TILE * r + b - 1)
                            pe.matmul(ps[b % 2][0:NJ, 0:SEQ], phik[:, k, b * SEQ:b * SEQ + NJ],
                                      phiq[:, k, b * SEQ:(b + 1) * SEQ], start=True, stop=True)
                            pe.matmul(ps[b % 2][0:NJ, SEQ:SEQ + NJ], phik[:, k, b * SEQ + NJ:(b + 1) * SEQ],
                                      phiq[:, k, b * SEQ + NJ:(b + 1) * SEQ], start=True,
                                      stop=True).then_inc(score_made, 1)

                        def retrieve(b):
                            pe.wait_ge(probs_ready, SEQ_TILE * r + b + 1)
                            for c in range(2):
                                for par in range(2):
                                    mm = pe.matmul(
                                        po[par * HID:(par + 1) * HID, b * NJ + c * (NJ // 2):(b + 1) * NJ],
                                        v[:, k, (2 * b + c) * HID:(2 * b + c + 1) * HID],
                                        probs[:, b % 2, c * SEQ:SEQ + c * NJ].rearrange("p (j o) -> p j o", o=2)[:, :, par],
                                        start=(c == 0), stop=(c == 1), skip_group_check=True)
                            mm.then_inc(out_made, 1)
                        pe.wait_ge(phi_ready, 2 * r + 2)
                        pe.wait_ge(v_ready, r + 1)
                        scores(0)
                        scores(1)
                        for b in range(2, SEQ_TILE):
                            retrieve(b - 2)
                            scores(b)
                        retrieve(SEQ_TILE - 2)
                        retrieve(SEQ_TILE - 1)
                run_steps(pe, NT, 2, step)

            @block.scalar
            def _(act):
                act.wait_ge(loads, 16 * len(weights))

                def step(t, k):
                    n, m = t, t - 1
                    if exists(n, NT):
                        act_square(act, L, n)
                    if exists(m, NT):
                        act.preload_act_table_set("silu_and_others")
                        for h in range(2):
                            act.wait_ge(proj_made, 4 * m + h + 1)
                            act.activation(hid[:, h * COLS:(h + 1) * COLS], pw[h][:, 0:COLS], ACT.Tanh,
                                           bias=vec[:, 0:1]).then_inc(tanh_done, 1)
                        at_least(act, folded_ready, m)
                        for h in range(2):
                            act.wait_ge(proj_made, 4 * m + h + 3)
                            act.activation(phase[:, h * COLS:(h + 1) * COLS], pw[h][:, 0:COLS], ACT.Tanh,
                                           bias=vec[:, 1:2]).then_inc(tanh_done, 1)
                        act.wait_ge(folded_ready, m + 1)
                        at_least(act, out_made, SEQ_TILE * (m - 1))
                        act.activation(phik[0:HID, 1 - k, :], folded[0:HID, :], ACT.Sin,
                                       bias=vec[0:HID, 4:5], scale=vec[0:HID, 3:4]).then_inc(phi_ready, 1)
                        act.activation(phiq[0:HID, 1 - k, :], folded[HID:128, :], ACT.Sin,
                                       bias=vec[HID:128, 4:5], scale=vec[HID:128, 3:4]).then_inc(phi_ready, 1)
                    if exists(n, NT):
                        act.preload_act_table_set("natural_log_exp_and_others")
                        act_rstd(act, L, n)
                run_steps(act, NT, 1, step)

            @block.vector
            def _(dve):
                dve.wait_ge(loads, 16 * len(weights))
                count = [0]

                def link(ins):
                    count[0] += 1
                    ins.then_inc(chain, 1)
                    dve.wait_ge(chain, count[0])
                link(dve.tensor_scalar(r1[:], rt[:], 0.0, None, ALU.is_ge))
                link(dve.tensor_scalar(r2[:], rt[:], float(NEXP0 - 1), None, ALU.is_le))
                link(dve.tensor_tensor(r1[:], r1[:], r2[:], ALU.mult))
                link(dve.tensor_scalar(r3[:], rt[:], float(NEXP0), None, ALU.subtract))
                link(dve.tensor_tensor(r3[:], r3[:], r1[:], ALU.mult))
                link(dve.tensor_scalar(G.expert_of[:], r3[:], float(NEXP0), None, ALU.add))

                def step(t, k):
                    n, m, r = t, t - 1, t - 2

                    def masked(b):
                        dve.wait_ge(score_made, SEQ_TILE * r + b + 1)
                        at_least(dve, out_made, SEQ_TILE * r + b - 1)
                        dve.tensor_tensor(probs[:, b % 2, :], ps[b % 2][0:NJ, 0:3 * NJ], mask[:],
                                          ALU.mult).then_inc(probs_ready, 1)
                    if exists(m, NT):
                        dve.wait_ge(v_made, m + 1)
                        at_least(dve, out_made, SEQ_TILE * (m - 1))
                        dve.tensor_tensor(v[:, 1 - k, :].rearrange("p (c h) -> p c h", h=HID),
                                          pv[0:NJ, :].rearrange("p (c h) -> p c h", h=HID),
                                          vb[:].unsqueeze(1).to_broadcast([NJ, 2 * SEQ_TILE, HID]),
                                          ALU.add).then_inc(v_ready, 1)
                    if exists(r, NT):
                        masked(0)
                        masked(1)
                    if exists(m, NT):
                        dve.wait_ge(tanh_done, 4 * m + 4)
                        at_least(dve, phi_ready, 2 * m)
                        dve.scalar_tensor_tensor(out=folded[:, :], in0=phase[:, :], scalar=vec[:, 2:3],
                                                 in1=phase[:, :], op0=ALU.mult,
                                                 op1=ALU.max).then_inc(folded_ready, 1)
                    if exists(r, NT):
                        masked(2)
                        masked(3)
                    if exists(n, NT):
                        dve.wait_ge(L.rstd_ready, n + 1)
                        at_least(dve, v_made, n - 1)
                        for par in range(2):
                            rows = slice(par * HID, (par + 1) * HID)
                            dve.tensor_tensor(xn[0:HID, k, :].rearrange("p (j o) -> p j o", o=2)[:, :, par],
                                              L.centered[rows, 0:COLS], L.rstd[rows, :],
                                              ALU.mult).then_inc(L.norm_done, 1)
                    if exists(r, NT):
                        dve.wait_ge(out_made, SEQ_TILE * r + SEQ_TILE)
                        dve.tensor_tensor(G.t_flat[:, ds(r * COLS, COLS)], po[:, 0:COLS],
                                          G.t_flat[:, ds(r * COLS, COLS)], ALU.add).then_inc(stream_done, 1)
                run_steps(dve, NT, 2, step)



def phase_routed(nc, G):
    D, NT = G.dram, SEQ_TILES
    with ExitStack() as ctx:
        sb = lambda n, s, d=F32: ctx.enter_context(nc.sbuf_tensor("r_" + n, s, d))
        pt = lambda n: ctx.enter_context(nc.psum_tensor("r_" + n, [128, 512], F32))
        sem = lambda n: G.ctx.enter_context(nc.semaphore("r_" + n))
        L = Norm(ctx, nc, sem, "r", COLS, 1e-5)
        wi, wo, vec = sb("wi", [128, 2, LH]), sb("wo", [128, HID]), sb("vec", [128, 2])
        xn = sb("xn", [128, 2, COLS])
        h0, h1, h2 = (sb(f"h{i}", [128, 2, 2, COLS]) for i in range(3))
        w = sb("w", [128, 2, 2, 2, SLOT])
        pm = [pt(f"pm{i}") for i in range(4)]
        po = pt("po")
        loads = sem("loads")
        w_here = [sem("w_here0"), sem("w_here1")]
        in_made, in_done = sem("in_made"), sem("in_done")
        a_made, a_done, b_made, b_done = sem("a_made"), sem("a_done"), sem("b_made"), sem("b_done")
        out_made, stream_done = sem("out_made"), sem("stream_done")
        weights = [(wi, D["r_wi"]), (wo, D["r_wo"]), (vec, D["r_vec"])]

        with nc.Block() as block:
            @block.sync
            def _(sp):
                for dst, src in weights:
                    sp.dma_start(dst[:], src).then_inc(loads, 16)

                def step(t, k):
                    at_least(sp, b_done, 2 * t - 2)
                    for g in range(2):
                        e = sp.value_load(G.expert_of[0:1, ds(2 * t + g, 1)], min_val=0, max_val=NEXP0)
                        for l in range(2):
                            sp.dma_start(w[:, k, l, g, :], G.expert_w[:, l, ds(e, 1), :].rearrange("p e s -> p (e s)")
                                         ).then_inc(w_here[k], 16)
                run_steps(sp, NT, 0, step)

            @block.tensor
            def _(pe):
                pe.wait_ge(loads, 16 * len(weights))

                def step(t, k):
                    n, i, a, b, o = t, t - 1, t - 2, t - 3, t - 4
                    if exists(n, NT):
                        at_least(pe, L.norm_done, n)
                        pe.matmul(L.centered[:, 0:COLS], G.center_m[:], G.t_flat[:, ds(n * COLS, COLS)],
                                  start=True, stop=True).then_inc(L.centered_ready, 1)
                    if exists(i, NT):
                        pe.wait_ge(L.norm_done, i + 1)
                        at_least(pe, b_done, 2 * (t - 3))
                        for par in range(2):
                            pe.matmul(pm[par][:, 0:COLS], wi[:, par, :], xn[:, 1 - k, :], start=True,
                                      stop=True).then_inc(in_made, 1)
                    if exists(a, NT):
                        pe.wait_ge(in_done, 2 * a + 2)
                        pe.wait_ge(w_here[k], 64 * half(a, k) + 64)
                        at_least(pe, a_done, 2 * a)
                        for g in range(2):
                            pe.matmul(pm[2 + g][:, 0:COLS].rearrange("p (o c) -> p o c", o=2), w[:, k, 0, g, 0:LH],
                                      h0[:, k, :, g * GCOLS:(g + 1) * GCOLS], start=True,
                                      stop=True).then_inc(a_made, 1)
                    if exists(n, NT):
                        pe_variance(pe, G, L, n)
                    if exists(b, NT):
                        pe.wait_ge(a_done, 2 * b + 2)
                        at_least(pe, b_done, 2 * b)
                        at_least(pe, in_done, 2 * min(t, NT) if isinstance(t, int) else 2 * t)
                        for g in range(2):
                            pe.matmul(pm[g][:, 0:COLS], w[:, 1 - k, 1, g, 0:LH], h1[:, 1 - k, g, :], start=True,
                                      stop=True).then_inc(b_made, 1)
                    if exists(o, NT):
                        pe.wait_ge(b_done, 2 * o + 2)
                        at_least(pe, stream_done, o)
                        for g in range(2):
                            for par in range(2):
                                mm = pe.matmul(po[par * HID:(par + 1) * HID, g * GCOLS:(g + 1) * GCOLS], wo[:],
                                               h2[:, k, g, par * GCOLS:(par + 1) * GCOLS], start=True, stop=True,
                                               skip_group_check=True)
                        mm.then_inc(out_made, 1)
                run_steps(pe, NT, 4, step)

            @block.scalar
            def _(act):
                act.preload_act_table_set("natural_log_exp_and_others")
                act.wait_ge(loads, 16 * len(weights))

                def step(t, k):
                    n, i, a, b = t, t - 1, t - 2, t - 3
                    if exists(n, NT):
                        act_square(act, L, n)
                    if exists(i, NT):
                        at_least(act, a_made, 2 * (i - 1))
                        for par in range(2):
                            act.wait_ge(in_made, 2 * i + par + 1)
                            act.activation(h0[:, 1 - k, par, :], pm[par][:, 0:COLS], ACT.Relu,
                                           bias=vec[:, 0:1]).then_inc(in_done, 1)
                    if exists(n, NT):
                        act_rstd(act, L, n)
                    if exists(b, NT):
                        at_least(act, out_made, b - 1)
                        for g in range(2):
                            act.wait_ge(b_made, 2 * b + g + 1)
                            act.activation(h2[:, 1 - k, g, :], pm[g][:, 0:COLS], ACT.Relu,
                                           bias=w[:, 1 - k, 1, g, LH:SLOT]).then_inc(b_done, 1)
                run_steps(act, NT, 3, step)

            @block.vector
            def _(dve):
                dve.wait_ge(loads, 16 * len(weights))

                def step(t, k):
                    n, a, o = t, t - 2, t - 4
                    if exists(a, NT):
                        at_least(dve, b_made, 2 * (a - 1))
                        for g in range(2):
                            dve.wait_ge(a_made, 2 * a + g + 1)
                            dve.tensor_scalar(h1[:, k, g, :], pm[2 + g][:, 0:COLS], w[:, k, 0, g, LH:SLOT], 0.0,
                                              ALU.add, ALU.max).then_inc(a_done, 1)
                    if exists(n, NT):
                        dve.wait_ge(L.rstd_ready, n + 1)
                        at_least(dve, in_made, 2 * (n - 1))
                        dve.tensor_tensor(xn[:, k, :], L.centered[:, 0:COLS], L.rstd[:, :],
                                          ALU.mult).then_inc(L.norm_done, 1)
                    if exists(o, NT):
                        dve.wait_ge(out_made, o + 1)
                        dve.scalar_tensor_tensor(out=G.t_flat[:, ds(o * COLS, COLS)], in0=po[:, 0:COLS],
                                                 scalar=vec[:, 1:2], in1=G.t_flat[:, ds(o * COLS, COLS)],
                                                 op0=ALU.add, op1=ALU.add).then_inc(stream_done, 1)
                run_steps(dve, NT, 4, step)



def phase_ssm(nc, G):
    D, NT = G.dram, PAIR_TILES
    P1 = HID + 1
    with ExitStack() as ctx:
        sb = lambda n, s, d=F32: ctx.enter_context(nc.sbuf_tensor("s_" + n, s, d))
        pt = lambda n: ctx.enter_context(nc.psum_tensor("s_" + n, [128, 512], F32))
        sem = lambda n: G.ctx.enter_context(nc.semaphore("s_" + n))
        L = Norm(ctx, nc, sem, "s", PCOLS, 1e-5)
        lam = sb("lam", [128, 3, P1])
        bt, crt, col = sb("bt", [128, 2, HID]), sb("crt", [128, HID]), sb("col", [128, 2])
        shift = sb("shift", [128, 128])
        T = sb("prep", [128, 20, P1])
        qi = sb("qi", [128, P1], I32)
        wut, wu = sb("wut", [128, 128]), sb("wu", [128, 128])
        bb = sb("bb", [128, 128])
        a2t, a1, gt, kt = sb("a2t", [128, 128]), sb("a1", [128, 128]), sb("gt", [128, 128]), sb("kt", [128, 128])
        xn = sb("xn", [128, 2, PCOLS])
        state = sb("state", [128, PAIR_TILE, NB])
        px, py = pt("px"), pt("py")
        pp = [pt(f"pp{i}") for i in range(3)]
        loads, chain, exp_done, sin_done = sem("loads"), sem("chain"), sem("exp_done"), sem("sin_done")
        delta_ready, angle_ready, prep_made, mats_ready = sem("delta_ready"), sem("angle_ready"), sem("prep_made"), sem("mats_ready")
        part_ready = sem("part_ready")
        x_made, x_ready, y_made, stream_done, inject_made = sem("x_made"), sem("x_ready"), sem("y_made"), sem("stream_done"), sem("inject_made")
        weights = [(lam, D["s_lam"]), (bt, D["s_bt"]), (crt, D["s_crt"]), (col, D["s_col"]), (shift, D["s_shift"])]
        stream = G.t.rearrange("p b j -> p j b")
        (MAG, ANG, RED, SIN, ABSA, COS, ARE, AIM, T0, T1, A2R, A2I, NRE, FRE, FIM, BRE, BIM, CRE, CIM, DEL) = range(20)
        c = lambda i: T[:, i, :]
        h = lambda i: T[:, i, 0:HID]
        own = lambda i: T[:, i, HID:P1]
        S4 = PAIR_TILE

        with nc.Block() as block:
            @block.sync
            def _(sp):
                for dst, src in weights:
                    sp.dma_start(dst[:], src).then_inc(loads, 16)

            @block.scalar
            def _(act):
                act.wait_ge(loads, 16 * len(weights))
                act.activation(c(DEL), lam[:, 2, :], ACT.Exp).then_inc(exp_done, 1)
                act.wait_ge(delta_ready, 1)
                act.activation(c(MAG), c(T0), ACT.Exp).then_inc(exp_done, 1)
                act.wait_ge(angle_ready, 1)
                act.activation(c(SIN), c(RED), ACT.Sin).then_inc(sin_done, 1)
                act.activation(c(COS), c(ABSA), ACT.Sin, bias=PI / 2, scale=-1.0).then_inc(sin_done, 1)
                act.preload_act_table_set("natural_log_exp_and_others")

                def step(t, k):
                    act_square(act, L, t)
                    act_rstd(act, L, t)
                run_steps(act, NT, 0, step)

            @block.tensor
            def _(pe):
                pe.wait_ge(part_ready, 1)
                pe.transpose(pp[0][:, 0:128], wut[:], G.ident[:])
                pe.matmul(pp[1][:, 0:HID], a1[:], crt[:], start=True, stop=True).then_inc(prep_made, 1)
                pe.wait_ge(part_ready, 2)
                pe.matmul(pp[2][:, 0:HID], bb[:], crt[:], start=True, stop=True)
                pe.matmul(pp[2][0:HID, HID:128], wu[:, 0:HID], crt[:], start=True, stop=True,
                          skip_group_check=True)
                pe.matmul(pp[1][:, HID:128], a1[:], gt[:, 0:HID], start=True, stop=True,
                          skip_group_check=True).then_inc(prep_made, 1)
                pe.wait_ge(mats_ready, 1)

                def step(t, k):
                    n, m = t, t - 1

                    def center():
                        if exists(n, NT):
                            at_least(pe, L.norm_done, n)
                            pe.matmul(L.centered[:, :].rearrange("p (j b) -> p j b", b=NB), G.center_m[:],
                                      stream[:, ds(n * S4, S4), :], start=True,
                                      stop=True).then_inc(L.centered_ready, 1)

                    def advance(q):
                        pe.wait_ge(x_ready, S4 * m + q + 1)
                        pe.matmul(px[:, q * NB:(q + 1) * NB], a2t[:], state[:, (q - 1) % S4, :], start=False,
                                  stop=True, skip_group_check=True).then_inc(x_made, 1)

                    def observe(q):
                        mm = pe.matmul(py[:, q * NB:(q + 1) * NB], gt[:], state[:, (q - 1) % S4, :], start=False,
                                       stop=True, skip_group_check=True)
                        if q == S4 - 1:
                            mm.then_inc(y_made, 1)
                    if not exists(m, NT):
                        center()
                        pe_variance(pe, G, L, n)
                        return
                    pe.wait_ge(L.norm_done, m + 1)
                    pe.wait_ge(x_ready, S4 * m + 1)
                    pe.matmul(px[:, :], wut[:], xn[:, 1 - k, :], start=True, stop=False, skip_group_check=True)
                    advance(0)
                    at_least(pe, stream_done, m)
                    pe.matmul(py[:, :], kt[:], xn[:, 1 - k, :], start=True, stop=False,
                              skip_group_check=True).then_inc(inject_made, 1)
                    observe(0)
                    advance(1)
                    center()
                    observe(1)
                    advance(2)
                    observe(2)
                    if exists(n, NT):
                        pe_variance(pe, G, L, n)
                    advance(3)
                    observe(3)
                run_steps(pe, NT, 1, step)

            @block.vector
            def _(dve):
                count = [0]

                def link(ins):
                    count[0] += 1
                    ins.then_inc(chain, 1)
                    dve.wait_ge(chain, count[0])

                def mul(o, a, b):
                    link(dve.tensor_tensor(o, a, b, ALU.mult))

                def addsub(o, a, b, op):
                    link(dve.tensor_tensor(o, a, b, op))

                def cmul(ore, oim, are, aim, bre, bim, t0, t1):
                    mul(t0, are, bre)
                    mul(t1, aim, bim)
                    addsub(ore, t0, t1, ALU.subtract)
                    mul(t0, are, bim)
                    mul(t1, aim, bre)
                    addsub(oim, t0, t1, ALU.add)
                dve.wait_ge(loads, 16 * len(weights))
                lre, lim = lam[:, 0, :], lam[:, 1, :]
                dve.wait_ge(exp_done, 1)
                dve.tensor_tensor(c(T0), lre, c(DEL), ALU.mult).then_inc(delta_ready, 1)
                mul(c(ANG), lim, c(DEL))
                link(dve.tensor_scalar(qi[:], c(ANG), 1.0 / (2 * PI), None, ALU.mult))
                link(dve.tensor_copy(c(T1), qi[:]))
                link(dve.scalar_tensor_tensor(out=c(RED), in0=c(T1), scalar=-6.28125, in1=c(ANG), op0=ALU.mult, op1=ALU.add))
                link(dve.scalar_tensor_tensor(out=c(RED), in0=c(T1), scalar=-(2 * PI - 6.28125), in1=c(RED), op0=ALU.mult, op1=ALU.add))
                for op, turn in ((ALU.is_gt, -2 * PI), (ALU.is_lt, 2 * PI)):
                    link(dve.tensor_scalar(c(T1), c(RED), PI if turn < 0 else -PI, turn, op, ALU.mult))
                    addsub(c(RED), c(RED), c(T1), ALU.add)
                link(dve.tensor_scalar(c(RED), c(RED), 3.1415925, -3.1415925, ALU.min, ALU.max))
                link(dve.scalar_tensor_tensor(out=c(ABSA), in0=c(RED), scalar=-1.0, in1=c(RED), op0=ALU.mult, op1=ALU.max))
                link(dve.memset(kt[:], 0.0))
                dve.tensor_scalar(crt[HID:128, :], crt[HID:128, :], -1.0, None, ALU.mult).then_inc(angle_ready, 1)
                dve.wait_ge(exp_done, 2)
                dve.wait_ge(sin_done, 2)
                mul(c(ARE), c(MAG), c(COS))
                mul(c(AIM), c(MAG), c(SIN))
                cmul(c(A2R), c(A2I), c(ARE), c(AIM), c(ARE), c(AIM), c(T0), c(T1))
                link(dve.tensor_scalar(c(NRE), c(ARE), 1.0, None, ALU.subtract))
                mul(c(T0), lre, lre)
                mul(c(T1), lim, lim)
                addsub(c(T0), c(T0), c(T1), ALU.add)
                link(dve.reciprocal(c(DEL), c(T0)))
                mul(c(T0), c(NRE), lre)
                mul(c(T1), c(AIM), lim)
                addsub(c(T0), c(T0), c(T1), ALU.add)
                mul(c(FRE), c(T0), c(DEL))
                mul(c(T0), c(AIM), lre)
                mul(c(T1), c(NRE), lim)
                addsub(c(T0), c(T0), c(T1), ALU.subtract)
                mul(c(FIM), c(T0), c(DEL))
                cmul(h(BRE), h(BIM), h(FRE), h(FIM), bt[:, 0, :], bt[:, 1, :], h(T0), h(T1))
                cmul(h(CRE), h(CIM), h(ARE), h(AIM), h(BRE), h(BIM), h(T0), h(T1))
                for half_rows, re, im in ((slice(0, HID), CRE, CIM), (slice(HID, 128), BRE, BIM)):
                    link(dve.tensor_copy(wut[half_rows, 0:HID], T[half_rows, re, 0:HID]))
                    link(dve.tensor_copy(wut[half_rows, HID:128], T[half_rows, im, 0:HID]))
                sign = col[:, 1:2]
                mul(own(T0), own(A2I), sign)
                mul(own(T1), own(AIM), sign)
                link(dve.tensor_scalar(own(T1), own(T1), -1.0, None, ALU.mult))
                link(dve.tensor_scalar(a2t[:], G.ident[:], own(A2R), None, ALU.mult))
                link(dve.scalar_tensor_tensor(out=a2t[:], in0=shift[:], scalar=own(T0), in1=a2t[:], op0=ALU.mult, op1=ALU.add))
                link(dve.tensor_scalar(a1[:], G.ident[:], own(ARE), None, ALU.mult))
                dve.scalar_tensor_tensor(out=a1[:], in0=shift[:], scalar=own(T1), in1=a1[:], op0=ALU.mult,
                                         op1=ALU.add).then_inc(part_ready, 1)
                dve.wait_ge(prep_made, 1)
                dve.tensor_copy(wu[:], pp[0][:, 0:128])
                dve.tensor_copy(bb[:, 0:HID], pp[0][:, HID:128])
                dve.tensor_copy(bb[:, HID:128], pp[0][:, HID:128])
                dve.tensor_copy(gt[:, 0:HID], pp[1][:, 0:HID]).then_inc(part_ready, 1)
                dve.wait_ge(prep_made, 2)
                dve.tensor_copy(gt[:, HID:128], pp[1][:, HID:128])
                link(dve.tensor_copy(kt[0:HID, 0:HID], pp[2][0:HID, 0:HID]))
                link(dve.tensor_copy(kt[0:HID, HID:128], pp[2][0:HID, HID:128]))
                link(dve.tensor_copy(kt[HID:128, HID:128], pp[2][HID:128, 0:HID]))
                dve.scalar_tensor_tensor(out=kt[:], in0=G.ident[:], scalar=col[:, 0:1], in1=kt[:], op0=ALU.mult,
                                         op1=ALU.add).then_inc(mats_ready, 1)
                dve.memset(state[:, S4 - 1, :], 0.0).then_inc(x_ready, 1)

                def step(t, k):
                    n, m = t, t - 1

                    def keep(q):
                        dve.wait_ge(x_made, S4 * m + q + 1)
                        dve.tensor_copy(state[:, q, :], px[:, q * NB:(q + 1) * NB]).then_inc(x_ready, 1)

                    def normalise():
                        if exists(n, NT):
                            dve.wait_ge(L.rstd_ready, n + 1)
                            at_least(dve, inject_made, n - 1)
                            dve.tensor_tensor(xn[:, k, :], L.centered[:, :], L.rstd[:, :],
                                              ALU.mult).then_inc(L.norm_done, 1)
                    if exists(m, NT):
                        for q in range(S4):
                            keep(q)
                    normalise()
                    if exists(m, NT):
                        dve.wait_ge(y_made, m + 1)
                        dve.tensor_tensor(stream[:, ds(m * S4, S4), :], py[:, :].rearrange("p (j b) -> p j b", b=NB),
                                          stream[:, ds(m * S4, S4), :], ALU.add).then_inc(stream_done, 1)
                run_steps(dve, NT, 1, step)



def phase_experts(nc, G, out):
    D, NT = G.dram, PAIR_TILES
    with ExitStack() as ctx:
        sb = lambda n, s, d=F32: ctx.enter_context(nc.sbuf_tensor("x_" + n, s, d))
        pt = lambda n, d=F32: ctx.enter_context(nc.psum_tensor("x_" + n, [128, 2048 // (4 if d is F32 else 2)], d))
        sem = lambda n: G.ctx.enter_context(nc.semaphore("x_" + n))
        L = Norm(ctx, nc, sem, "x", PCOLS, 1e-5)
        PE2 = 2 * NEXP1
        LG = PAIR_TILE * PE2
        rw, rb, tie = sb("rw", [128, PE2]), sb("rb", [NB, PE2]), sb("tie", [NB, LG])
        w1, b1, w2 = sb("w1", [128, 2, FCH, 128]), sb("b1", [128, FCH]), sb("w2", [128, FCH, HID])
        b2f, b2p = sb("b2f", [128, 2, 128]), sb("b2p", [128, 3, 128], BF16)
        maskf, maskb = sb("maskf", [128, 2, FCH, 128]), sb("maskb", [128, 2, FCH, 128], BF16)
        identb = sb("identb", [128, 128], BF16)
        xn = sb("xn", [128, 2, PCOLS])
        logit, hit = sb("logit", [NB, LG]), sb("hit", [NB, LG])
        top, first = sb("top", [NB, 2 * PAIR_TILE]), sb("first", [NB, 2 * PAIR_TILE])
        onehot = sb("onehot", [NB, LG], BF16)
        choice = sb("choice", [128, 2, PCOLS], BF16)
        hm = sb("hm", [128, 2, FCH, PCOLS])
        fin = sb("fin", [128, 2, PCOLS])
        outs = sb("outs", [NB, 2, PCOLS])
        plog, pch, pfin, po = pt("plog"), pt("pch", BF16), pt("pfin"), pt("po")
        pf = [pt("pf0"), pt("pf1")]
        loads, cleared, prep, prep_done = sem("loads"), sem("cleared"), sem("prep"), sem("prep_done")
        logit_made, logit_ready = sem("logit_made"), sem("logit_ready")
        top_ready, hit_ready, tied_ready, first_ready = sem("top_ready"), sem("hit_ready"), sem("tied_ready"), sem("first_ready")
        onehot_ready, choice_made, choice_ready = sem("onehot_ready"), sem("choice_made"), sem("choice_ready")
        up_made, relu0, relu1 = sem("up_made"), sem("relu0"), sem("relu1")
        down_made, fin_ready, fin_made, outs_ready = sem("down_made"), sem("fin_ready"), sem("fin_made"), sem("outs_ready")
        stored, turn_begun = [sem("stored0"), sem("stored1")], sem("turn_begun")
        weights = [(rw, D["x_rw"]), (rb, D["x_rb"]), (tie, D["x_tie"]), (w1, D["x_w1"]), (b1, D["x_b1"]),
                   (w2, D["x_w2"]), (maskf, D["x_mask"])]
        stream = G.t.rearrange("p b j -> p j b")
        out_rows = out.rearrange("b s c -> b (s c)")
        S4 = PAIR_TILE
        by_expert = lambda a: a.rearrange("p (g e) -> p g e", e=NEXP1)

        with nc.Block() as block:
            @block.sync
            def _(sp):
                for dst, src in weights:
                    sp.dma_start(dst[:], src).then_inc(loads, 16)
                sp.dma_start(b2f[:, 0, :], D["x_b2"]).then_inc(loads, 16)

                def step(t, k):
                    sp.wait_ge(outs_ready, t + 1)
                    sp.dma_start(out_rows[:, ds(t * PCOLS, PCOLS)], outs[:, k, :]).then_inc(stored[k], 16)
                run_steps(sp, NT, 0, step)
                sp.wait_ge(stored[0], 16 * (NT // 2 + 1))
                sp.wait_ge(stored[1], 16 * (NT // 2))

            @block.gpsimd
            def _(pool):
                pool.memset(choice[HID:128, :, :], 0.0).then_inc(cleared, 1)
                pool.wait_ge(cleared, 1)
                pool.memset(choice[HID:HID + 1, :, :], 1.0).then_inc(prep_done, 1)

            @block.tensor
            def _(pe):
                pe.wait_ge(loads, 16 * (len(weights) + 1))
                pe.wait_ge(prep_done, 2)

                def step(t, k):
                    n, i, m, f = t, t - 1, t - 2, t - 3
                    if exists(i, NT):
                        pe.wait_ge(L.norm_done, i + 1)
                        at_least(pe, logit_ready, i)
                        for q in range(S4):
                            mm = pe.matmul(plog[:, q * PE2:(q + 1) * PE2], xn[:, 1 - k, q * NB:(q + 1) * NB], rw[:],
                                           start=True, stop=True)
                        mm.then_inc(logit_made, 1)
                    if exists(n, NT):
                        at_least(pe, L.norm_done, n)
                        pe.matmul(L.centered[:, :].rearrange("p (j b) -> p j b", b=NB), G.center_m[:],
                                  stream[:, ds(n * S4, S4), :], start=True, stop=True).then_inc(L.centered_ready, 1)
                    if exists(m, NT):
                        pe.wait_ge(choice_ready, m + 1)
                        for u in range(2 * FCH):
                            ck, par = u // 2, u % 2
                            at_least(pe, (relu0, relu1)[par], FCH * m + ck)
                            pe.matmul(pf[par][:, :], maskb[:, par, ck, :], choice[:, k, :], start=True, stop=False)
                            pe.matmul(pf[par][:, :], w1[:, par, ck, :], xn[:, k, :], start=False,
                                      stop=True).then_inc(up_made, 1)
                            if u == 3 and exists(n, NT):
                                pe_variance(pe, G, L, n)
                        at_least(pe, fin_ready, m)
                        for j in range(3):
                            pe.matmul(po[:, :], b2p[:, j, :], choice[:, k, :], start=(j == 0), stop=False,
                                      skip_group_check=True)
                        for ck in range(FCH):
                            pe.wait_ge(relu0, FCH * m + ck + 1)
                            pe.wait_ge(relu1, FCH * m + ck + 1)
                            for par in range(2):
                                mm = pe.matmul(po[par * HID:(par + 1) * HID, :], w2[:, ck, :], hm[:, par, ck, :],
                                               start=False, stop=(ck == FCH - 1), skip_group_check=True)
                        mm.then_inc(down_made, 1)
                    elif exists(n, NT):
                        pe_variance(pe, G, L, n)
                    if exists(f, NT):
                        pe.wait_ge(fin_ready, f + 1)
                        at_least(pe, outs_ready, f)
                        for q in range(S4):
                            mm = pe.transpose(pfin[:, q * 128:(q + 1) * 128], fin[:, 1 - k, q * NB:(q + 1) * NB],
                                              G.ident[:])
                        mm.then_inc(fin_made, 1)
                    if exists(i, NT):
                        pe.wait_ge(onehot_ready, i + 1)
                        at_least(pe, choice_ready, i)
                        pe.sem_inc(turn_begun, 1)
                        for q in range(S4):
                            mm = pe.transpose(pch[0:PE2, q * NB:(q + 1) * NB], onehot[:, q * PE2:(q + 1) * PE2],
                                              identb[:])
                        mm.then_inc(choice_made, 1)
                run_steps(pe, NT, 3, step)

            @block.scalar
            def _(act):
                act.preload_act_table_set("natural_log_exp_and_others")
                act.wait_ge(loads, 16 * (len(weights) + 1))

                def step(t, k):
                    n, m, f = t, t - 2, t - 3
                    if exists(n, NT):
                        act_square(act, L, n)
                    if exists(m, NT):
                        at_least(act, down_made, m)
                        for ck in range(FCH):
                            act.wait_ge(up_made, 2 * FCH * m + 2 * ck + 1)
                            act.activation(hm[:, 0, ck, :], pf[0][:, :], ACT.Relu,
                                           bias=b1[:, ck:ck + 1]).then_inc(relu0, 1)
                            if ck == 2 and exists(n, NT):
                                act_rstd(act, L, n)
                    elif exists(n, NT):
                        act_rstd(act, L, n)
                    if exists(f, NT):
                        act.wait_ge(fin_made, f + 1)
                        at_least(act, stored[1 - k], 16 * half(f, 1 - k))
                        act.activation(outs[:, 1 - k, :], pfin[:, :], ACT.Identity).then_inc(outs_ready, 1)
                run_steps(act, NT, 3, step)

            @block.vector
            def _(dve):
                dve.wait_ge(loads, 16 * (len(weights) + 1))
                dve.tensor_copy(identb[:], G.ident[:])
                dve.tensor_copy(maskb[:], maskf[:])
                dve.tensor_copy(b2p[:, 0, :], b2f[:, 0, :]).then_inc(prep, 1)
                dve.wait_ge(prep, 1)
                dve.tensor_tensor(b2f[:, 1, :], b2f[:, 0, :], b2p[:, 0, :], ALU.subtract).then_inc(prep, 1)
                dve.wait_ge(prep, 2)
                dve.tensor_copy(b2p[:, 1, :], b2f[:, 1, :]).then_inc(prep, 1)
                dve.wait_ge(prep, 3)
                dve.tensor_tensor(b2f[:, 0, :], b2f[:, 1, :], b2p[:, 1, :], ALU.subtract).then_inc(prep, 1)
                dve.wait_ge(prep, 4)
                dve.tensor_copy(b2p[:, 2, :], b2f[:, 0, :]).then_inc(prep_done, 1)

                def step(t, k):
                    n, i, m = t, t - 1, t - 2

                    def relu(cks):
                        for ck in cks:
                            dve.wait_ge(up_made, 2 * FCH * m + 2 * ck + 2)
                            dve.tensor_scalar(hm[:, 1, ck, :], pf[1][:, :], b1[:, ck:ck + 1], 0.0, ALU.add,
                                              ALU.max).then_inc(relu1, 1)
                    if exists(i, NT):
                        dve.wait_ge(logit_made, i + 1)
                        dve.tensor_tensor(logit[:, :].rearrange("p (q e) -> p q e", e=PE2),
                                          plog[:, 0:LG].rearrange("p (q e) -> p q e", e=PE2),
                                          rb[:].unsqueeze(1).to_broadcast([NB, S4, PE2]), ALU.add).then_inc(logit_ready, 1)
                        dve.wait_ge(logit_ready, i + 1)
                        dve.tensor_reduce(top[:, :], by_expert(logit[:, :]), AX_X, ALU.max).then_inc(top_ready, 1)
                        dve.wait_ge(top_ready, i + 1)
                        dve.tensor_tensor(by_expert(hit[:, :]), by_expert(logit[:, :]),
                                          top[:].unsqueeze(2).to_broadcast([NB, 2 * S4, NEXP1]), ALU.is_ge).then_inc(hit_ready, 1)
                        dve.wait_ge(hit_ready, i + 1)
                    if exists(m, NT):
                        at_least(dve, down_made, m)
                        relu(range(0, 1))
                    if exists(i, NT):
                        dve.tensor_tensor(logit[:, :], hit[:, :], tie[:, :], ALU.mult).then_inc(tied_ready, 1)
                        dve.wait_ge(tied_ready, i + 1)
                        dve.tensor_reduce(first[:, :], by_expert(logit[:, :]), AX_X, ALU.max).then_inc(first_ready, 1)
                        dve.wait_ge(first_ready, i + 1)
                        at_least(dve, choice_made, i)
                        dve.tensor_tensor(by_expert(onehot[:, :]), by_expert(logit[:, :]),
                                          first[:].unsqueeze(2).to_broadcast([NB, 2 * S4, NEXP1]),
                                          ALU.is_equal).then_inc(onehot_ready, 1)
                    if exists(m, NT):
                        relu(range(1, 2))
                    if exists(m, NT):
                        relu(range(2, FCH))
                    if exists(n, NT):
                        dve.wait_ge(L.rstd_ready, n + 1)
                        at_least(dve, up_made, 2 * FCH * (n - 1))
                        dve.tensor_tensor(xn[:, k, :], L.centered[:, :], L.rstd[:, :],
                                          ALU.mult).then_inc(L.norm_done, 1)
                    if exists(m, NT):
                        dve.wait_ge(down_made, m + 1)
                        at_least(dve, fin_made, m - 1)
                        dve.scalar_tensor_tensor(out=fin[:, k, :].rearrange("p (j b) -> p j b", b=NB),
                                                 in0=po[:, :].rearrange("p (j b) -> p j b", b=NB), scalar=0.0,
                                                 in1=stream[:, ds(m * S4, S4), :], op0=ALU.max,
                                                 op1=ALU.add).then_inc(fin_ready, 1)
                    if exists(i, NT):
                        dve.wait_ge(choice_made, i + 1)
                        at_least(dve, down_made, i - 1)
                        dve.tensor_copy(choice[0:PE2, 1 - k, :], pch[0:PE2, 0:PCOLS]).then_inc(choice_ready, 1)
                run_steps(dve, NT, 2, step)

class Shared:
    pass


def build(nc, D, out):
    with ExitStack() as ctx:
        sb = lambda n, s, d=F32: ctx.enter_context(nc.sbuf_tensor(n, s, d))
        G = Shared()
        G.dram, G.ctx = D, ctx
        G.ident, G.center_m, G.mean_m = sb("ident", [128, 128]), sb("center_m", [128, 128]), sb("mean_m", [128, 128])
        G.flip = sb("flip", [NJ, NJ])
        G.vec = sb("vec", [128, 16])
        G.d1 = sb("d1", [128, LAYERS, 2, DFF])
        G.gelu_b = sb("gelu_b", [128, LAYERS, 2])
        G.d2c = sb("d2c", [128, LAYERS, 2, HID])
        G.d2bc = sb("d2bc", [128, LAYERS])
        G.lag_dram = nc.dram_tensor("lag_kernels", (LAYERS, HID, NLAG), F32).ap()
        region = sb("region", [128, PC * NB])
        G.bp = region[0:NJ, :].rearrange("p (f b) -> p f b", b=NB)
        G.t_flat = region[:, 0:NB * NJ]
        G.t = G.t_flat.rearrange("p (b j) -> p b j", j=NJ)
        with ExitStack() as early:
            y = early.enter_context(nc.sbuf_tensor("conv_out", [NJ, NB * PC], F32))
            G.y_flat = y[:, :]
            G.y = G.y_flat.rearrange("p (b f) -> p b f", f=PC)
            phase_embed(nc, G)
            for layer in range(LAYERS):
                phase_conv(nc, G, layer)
                phase_ffn(nc, G, layer)
        G.expert_w = sb("expert_w", [128, 2, NEXP0 + 1, SLOT])
        G.expert_of = sb("expert_of", [1, NGROUP], I32)
        phase_attention(nc, G)
        phase_routed(nc, G)
        phase_ssm(nc, G)
        phase_experts(nc, G, out)


def lay_out_attention(A, f):
    import numpy as np
    w1 = np.zeros((128, 128), np.float32)
    w1[0:HID, 0:HID], w1[0:HID, HID:128] = f("L0_attn_kw1").T, f("L0_attn_qw1").T
    w2 = np.zeros((128, 128), np.float32)
    vec = np.zeros((128, 8), np.float32)
    vec[:, 0] = np.concatenate([f("L0_attn_kb1"), f("L0_attn_qb1")])
    for side, (w, b) in enumerate((("L0_attn_kw2", "L0_attn_kb2"), ("L0_attn_qw2", "L0_attn_qb2"))):
        for part in range(2):
            cols = slice(side * HID + part * 32, side * HID + part * 32 + 32)
            w2[side * HID:(side + 1) * HID, cols] = f(w).T
            vec[cols, 1] = f(b)
            vec[cols, 2] = (-1.0, 1.0)[part]
            vec[cols, 3] = (-3.1415925, 3.1415925)[part]
            vec[cols, 4] = (PI / 2, 0.0)[part]
    A["a_w1"], A["a_w2"], A["a_vec"] = w1, w2, vec
    vw = np.zeros((128, HID), np.float32)
    vw[0:HID] = f("L0_attn_vw").T
    A["a_vw"] = vw
    A["a_vb"] = np.tile(f("L0_attn_vb"), (NJ, 1))
    key, query = np.arange(NJ)[:, None], np.arange(SEQ)[None, :]
    scale = 1.0 / np.sqrt((query + 1.0) * 32)
    both = [(key <= query) * scale, ((key + NJ <= query) * scale)[:, NJ:]]
    A["a_mask"] = np.concatenate(both, axis=1).astype(np.float32)


def lay_out_routed(A, f):
    import numpy as np
    w = np.zeros((128, 2, NEXP0 + 1, SLOT), np.float32)
    w[:, :, 0:NEXP0, 0:LH] = f("L0_ffn_Wr").transpose(3, 0, 1, 2)
    w[:, :, 0:NEXP0, LH] = f("L0_ffn_br").transpose(2, 0, 1)
    base = np.zeros((128, 2, SLOT), np.float32)
    base[:, :, 0:LH] = f("L0_ffn_Ws")[:, 0].transpose(2, 0, 1)
    base[:, :, LH] = f("L0_ffn_bs")[:, 0].T
    A["r_w"], A["r_base"] = w, base
    A["route"] = f("L0_ffn_route_id").reshape(1, NGROUP)
    wi = np.zeros((128, 2, LH), np.float32)
    for par in range(2):
        wi[par * HID:(par + 1) * HID, par] = f("L0_ffn_Wi").T
    A["r_wi"], A["r_wo"] = wi, np.ascontiguousarray(f("L0_ffn_Wo").T)
    bo = f("L0_ffn_bo")
    A["r_vec"] = np.stack([f("L0_ffn_bi"), np.concatenate([bo, bo])], axis=1)


def lay_out_ssm(A, f):
    import numpy as np
    rows = [f("L1_attn_Lambda_re"), f("L1_attn_Lambda_im"), f("L1_attn_log_step")]
    lam = np.zeros((128, 3, HID + 1), np.float32)
    for i, v in enumerate(rows):
        lam[:, i, 0:HID] = v[None, :]
        lam[:, i, HID] = np.concatenate([v, v])
    A["s_lam"] = lam
    b = f("L1_attn_B_ri").transpose(1, 2, 0)
    A["s_bt"] = np.concatenate([b, b], axis=0)
    A["s_crt"] = np.concatenate([f("L1_attn_C_re").T, f("L1_attn_C_im").T], axis=0)
    d = f("L1_attn_D")
    sign = np.repeat(np.array([1.0, -1.0], np.float32), HID)
    A["s_col"] = np.stack([np.concatenate([d, d]), sign], axis=1)
    A["s_shift"] = np.roll(np.eye(128, dtype=np.float32), HID, axis=1)


def lay_out_experts(A, f):
    import numpy as np
    PE2 = 2 * NEXP1
    rw, w1 = np.zeros((128, PE2), np.float32), np.zeros((128, 2, FCH * 128), np.float32)
    b2, mask = np.zeros((128, 128), np.float32), np.zeros((128, 2, FCH * 128), np.float32)
    for par in range(2):
        rows, experts = slice(par * HID, (par + 1) * HID), slice(par * NEXP1, (par + 1) * NEXP1)
        rw[rows, experts] = f("L1_ffn_router_w").T
        w1[rows, par] = f("L1_ffn_W1").transpose(1, 0, 2).reshape(HID, FCH * 128)
        b2[experts, rows] = f("L1_ffn_b2")
        mask[experts, par] = np.kron(np.eye(NEXP1), np.ones((1, EH))) * BIG
        mask[PE2, par] = -BIG
    A["x_rw"], A["x_w1"], A["x_b2"] = rw, w1.reshape(128, 2, FCH, 128), b2
    A["x_mask"] = mask.reshape(128, 2, FCH, 128)
    A["x_rb"] = np.tile(f("L1_ffn_router_b"), (NB, 2))
    A["x_tie"] = np.tile((NEXP1 - np.arange(NEXP1)).astype(np.float32), (NB, 2 * PAIR_TILE))
    A["x_b1"] = np.ascontiguousarray(f("L1_ffn_b1").reshape(FCH, 128).T)
    A["x_w2"] = np.ascontiguousarray(f("L1_ffn_W2").reshape(FCH, 128, HID).transpose(1, 0, 2))


def lay_out(inputs):
    import numpy as np
    f = lambda n: np.asarray(inputs[n])
    dup = lambda v: np.concatenate([v, v], axis=0)
    A = {}
    A["ids"] = np.ascontiguousarray(f("x").reshape(NB, NJ, 2).transpose(1, 0, 2)).reshape(NJ, 2 * NB)
    A["item_emb"] = f("L0_tok_item_emb")
    A["pos"] = np.ascontiguousarray(f("L0_tok_pos_emb").reshape(NJ, PC).T)
    A["ident"] = np.eye(128, dtype=np.float32)
    A["flip"] = np.ascontiguousarray(np.eye(NJ, dtype=np.float32)[::-1])
    half = np.eye(HID) - 1.0 / HID
    A["center_m"] = np.kron(np.eye(2), half).astype(np.float32)
    A["mean_m"] = np.kron(np.eye(2), np.full((HID, HID), 1.0 / HID)).astype(np.float32)
    vec = np.zeros((128, 16), np.float32)
    cols = [f("L0_tok_ln0_w"), f("L0_tok_ln0_b"), *f("L0_tok_fln_w"), *f("L0_tok_fln_b"),
            *f("L0_tok_iln_w"), *f("L0_tok_iln_b")]
    for i, v in enumerate(cols):
        vec[:, i] = dup(v)
    A["vec"] = vec
    A["cw"] = np.ascontiguousarray(f("L0_tok_cw").transpose(1, 0, 3, 2))
    freq = np.arange(SEQ // 2 + 1)[:, None]
    lags = (SEQ - 1) - np.arange(NLAG)[None, :]
    weight = np.where((freq == 0) | (freq == SEQ // 2), 1.0, 2.0) / SEQ
    angle = 2 * np.pi * ((freq * lags) % SEQ) / SEQ
    A["dft"] = np.stack([weight * np.cos(angle), -weight * np.sin(angle)], axis=1).astype(np.float32)
    A["d2t"] = np.ascontiguousarray(f("L0_tok_d2_w").transpose(2, 0, 1))
    A["d2b"] = dup(np.ascontiguousarray(f("L0_tok_d2_b").T))
    d1 = np.zeros((128, LAYERS, 2, DFF), np.float32)
    for par in range(2):
        d1[par * HID:(par + 1) * HID, :, par, :] = f("L0_tok_d1_w").transpose(1, 0, 2)
    A["d1"] = d1
    A["gelu_b"] = np.ascontiguousarray(f("L0_tok_d1_b").reshape(LAYERS, 2, 128).transpose(2, 0, 1))
    lay_out_attention(A, f)
    lay_out_routed(A, f)
    lay_out_ssm(A, f)
    lay_out_experts(A, f)
    return A


def kernel(**inputs):
    import numpy as _np
    import concourse.bacc as _bacc
    from concourse import mybir as _mybir
    from concourse.bass_utils import run_bass_kernel_spmd as _run

    nc = _bacc.Bacc("TRN2", target_bir_lowering=False, num_devices=1)
    arrays, D = {}, {}
    for name, a in lay_out(inputs).items():
        a = _np.ascontiguousarray(a)
        arrays[f"in_{name}_dram"] = a
        D[name] = nc.dram_tensor(f"in_{name}_dram", a.shape, _mybir.dt.from_np(a.dtype), kind="ExternalInput").ap()
    out = nc.dram_tensor("out_0_dram", (NB, SEQ, HID), F32, kind="ExternalOutput").ap()
    build(nc, D, out)
    r = _run(nc, [arrays], core_ids=[0])
    return r.results[0]["out_0_dram"]
```

```python
from contextlib import ExitStack

import concourse.bass as bass
from concourse import mybir

F32 = mybir.dt.float32
BF16 = mybir.dt.bfloat16
F32R = mybir.dt.float32r
I32 = mybir.dt.int32
ACT = mybir.ActivationFunctionType
ALU = mybir.AluOpType
AX_X = mybir.AxisListType.X

NB, SEQ, HID = 128, 200, 64
NJ = SEQ // 2
PC = 2 * HID
DFF, LAYERS = 256, 2
SEQ_TILE = 4
COLS = SEQ_TILE * NJ
SEQ_TILES = NB // SEQ_TILE
PAIR_TILE = 4
PCOLS = PAIR_TILE * NB
PAIR_TILES = NJ // PAIR_TILE
NLAG = 2 * SEQ
PHASES = 32
LH = 128
NEXP0, NGROUP = 16, 64
GCOLS = 2 * NJ
NEXP1, EH = 32, 16
FCH = NEXP1 * EH // 128
SLOT = LH + 1
PI = 3.141592653589793
BIG = 2.0 ** 100


def at_least(eng, sem, value):
    if isinstance(value, int) and value <= 0:
        return
    eng.wait_ge(sem, value)


def run_steps(eng, tiles, skew, step):
    first = skew + 2 + skew % 2
    turns = (tiles - first) // 2
    for t in range(first):
        step(t, t % 2)
    with eng.Fori(0, turns) as i:
        for u in range(2):
            step(2 * i + (first + u), u)
    for t in range(first + 2 * turns, tiles + skew):
        step(t, t % 2)


def half(t, parity):
    return (t - parity) // 2


def exists(n, tiles):
    return not isinstance(n, int) or 0 <= n < tiles


def ds(start, size):
    return bass.ds(start, size)


def clear_all(nc, sems):
    with nc.Block() as block:
        @block.sync
        def _(sp):
            for s in sems:
                sp.sem_clear(s)




def split_high(eng, split, x, done):
    for par, rows in ((0, slice(0, HID)), (1, slice(HID, 128))):
        eng.tensor_copy(split[rows, par, :], x[rows, :]).then_inc(done, 1)


def split_low(eng, split, x, done):
    for par, rows, other in ((0, slice(0, HID), slice(HID, 128)), (1, slice(HID, 128), slice(0, HID))):
        eng.tensor_tensor(split[other, par, :], x[rows, :], split[rows, par, :], ALU.subtract).then_inc(done, 1)


class Norm:

    def __init__(self, ctx, nc, sem, tag, cols, eps, parts=1, banks=1):
        self.eps, self.cols, self.parts, self.banks = eps, cols, parts, banks
        self.centered_banks = [ctx.enter_context(nc.psum_tensor(f"{tag}_centered{i}", [128, 512], F32))
                               for i in range(banks)]
        self.centered = self.centered_banks[0]
        self.variance = ctx.enter_context(nc.psum_tensor(f"{tag}_variance", [128, 512], F32))
        self.square = ctx.enter_context(nc.sbuf_tensor(f"{tag}_square", [128, cols], F32))
        self.logvar = ctx.enter_context(nc.sbuf_tensor(f"{tag}_logvar", [128, cols], F32))
        self.rstd = ctx.enter_context(nc.sbuf_tensor(f"{tag}_rstd", [128, cols], F32))
        self.centered_ready, self.square_ready = sem("n_centered_ready"), sem("n_square_ready")
        self.variance_ready, self.log_ready = sem("n_variance_ready"), sem("n_log_ready")
        self.rstd_ready, self.norm_done = sem("n_rstd_ready"), sem("n_norm_done")


def pe_variance(pe, G, L, n):
    at_least(pe, L.square_ready, n + 1)
    at_least(pe, L.log_ready, n)
    pe.matmul(L.variance[:, 0:L.cols], G.mean_m[:], L.square[:, :], start=True,
              stop=True).then_inc(L.variance_ready, 1)


def act_square(act, L, n, bias=0.0, bank=0):
    at_least(act, L.centered_ready, n + 1)
    at_least(act, L.variance_ready, n)
    act.activation(L.square[:, :], L.centered_banks[bank][:, 0:L.cols], ACT.Square,
                   bias=bias).then_inc(L.square_ready, 1)


def act_rstd(act, L, n):
    at_least(act, L.variance_ready, n + 1)
    at_least(act, L.rstd_ready, n)
    act.activation(L.logvar[:, :], L.variance[:, 0:L.cols], ACT.Ln,
                   bias=L.eps).then_inc(L.log_ready, 1)
    at_least(act, L.log_ready, n + 1)
    at_least(act, L.norm_done, L.parts * n)
    act.activation(L.rstd[:, :], L.logvar[:, :], ACT.Exp, scale=-0.5).then_inc(L.rstd_ready, 1)



class StreamParts:
    def __init__(self, ctx, nc, sem, tag, cols):
        self.cols = cols
        self.parts = ctx.enter_context(nc.sbuf_tensor(f"{tag}_stream_parts", [128, 2, 2, cols], F32R))
        self.begun, self.high_ready, self.low_ready = sem("t_begun"), sem("t_high_ready"), sem("t_low_ready")


def pool_split_stream(pool, S, L, n, k, tile, inner):
    group = lambda a: a.rearrange("p (o i) -> p o i", i=inner)
    at_least(pool, L.centered_ready, n - 1)
    pool.sem_inc(S.begun, 1)
    pool.tensor_copy(group(S.parts[:, k, 0, :]), tile).then_inc(S.high_ready, 1)
    pool.wait_ge(S.high_ready, n + 1)
    pool.sem_inc(S.begun, 1)
    pool.tensor_tensor(group(S.parts[:, k, 1, :]), tile, group(S.parts[:, k, 0, :]),
                       ALU.subtract).then_inc(S.low_ready, 1)


def pe_center(pe, G, S, L, n, k):
    bank = k if L.banks == 2 else 0
    pe.wait_ge(S.low_ready, n + 1)
    at_least(pe, L.norm_done, L.parts * (n + 1 - L.banks))
    for part in range(2):
        mm = pe.matmul(L.centered_banks[bank][:, 0:S.cols], G.center_r[:], S.parts[:, k, part, :], start=(part == 0),
                       stop=(part == 1))
    mm.then_inc(L.centered_ready, 1)



def phase_embed(nc, G):
    D, NT = G.dram, PAIR_TILES
    TILE_TOKENS = 2 * PAIR_TILE
    CHUNK = 8
    with ExitStack() as ctx:
        sb = lambda n, s, d=F32: ctx.enter_context(nc.sbuf_tensor(n, s, d))
        pt = lambda n: ctx.enter_context(nc.psum_tensor(n, [128, 512], F32))
        sem = lambda n: G.ctx.enter_context(nc.semaphore("e_" + n))
        L = Norm(ctx, nc, sem, "e", PCOLS, 1e-12)
        ids = sb("e_ids", [NB, SEQ], I32)
        ids_tile = sb("e_ids_tile", [NB, 2, TILE_TOKENS], I32)
        rows = sb("e_rows", [NB, 2, TILE_TOKENS * HID])
        z = sb("e_z", [128, PCOLS])
        y = sb("e_y", [128, PCOLS])
        x0 = sb("e_x0", [128, 2, PCOLS])
        tokens_dram = nc.dram_tensor("tokens", (NJ, PC, NB), F32).ap()
        pos = sb("e_pos", [128, NJ])
        cw = sb("e_cw", [101, LAYERS, 2, HID])
        dft = sb("e_dft", [101, 2, NLAG])
        lag = sb("e_lag", [HID, LAYERS, NLAG])
        d2t = sb("e_d2t", [HID, LAYERS, DFF])
        d2b = sb("e_d2b", [128, LAYERS])
        d1, center_f = sb("e_d1", [128, LAYERS, DFF]), sb("e_center_f", [128, 2, 128])
        pz, pk0, pk1 = pt("e_pz"), pt("e_pk0"), pt("e_pk1")
        pk = [pk0, pk1]
        ids_here, loads = sem("ids_here"), sem("loads")
        ids_copied, tile_begun = sem("ids_copied"), sem("tile_begun")
        rows_here = [sem("rows_here0"), sem("rows_here1")]
        z_turned, z_ready, x0_ready = sem("z_turned"), sem("z_ready"), sem("x0_ready")
        stored, bp_here = [sem("stored0"), sem("stored1")], sem("bp_here")
        lag_copied, d1_high = sem("lag_copied"), sem("d1_high")
        prep_made, prep_copied, prep_out = sem("prep_made"), sem("prep_copied"), sem("prep_out")
        pairs = [(ids, D["ids"])]
        weights = [(G.ident, D["ident"]), (G.flip, D["flip"]), (G.center_m, D["center_m"]), (G.mean_m, D["mean_m"]),
                   (pos, D["pos"]), (G.vec, D["vec"]), (cw, D["cw"]), (dft, D["dft"]),
                   (d2t, D["d2t"]), (d2b, D["d2b"]), (d1, D["d1"]), (center_f, D["center_s"]), (G.gelu_b, D["gelu_b"])]

        with nc.Block() as block:
            @block.sync
            def _(sp):
                for dst, src in pairs:
                    sp.dma_start(dst[:], src).then_inc(ids_here, 16)
                for dst, src in weights:
                    sp.dma_start(dst[:], src).then_inc(loads, 16)
                sp.wait_ge(prep_copied, 2)
                for l in range(LAYERS):
                    sp.dma_start(G.lag_dram[l], lag[:, l, :]).then_inc(prep_out, 16)

                def step(t, k):
                    sp.wait_ge(x0_ready, t + 1)
                    sp.dma_start(tokens_dram[ds(t * PAIR_TILE, PAIR_TILE)].rearrange("j f b -> f j b"),
                                 x0[:, k, :].rearrange("f (j b) -> f j b", b=NB)).then_inc(stored[k], 16)

                def fetch(first, tiles):
                    for k in range(2):
                        sp.wait_ge(stored[k], 16 * ((first + tiles + 1 - k) // 2))
                    rows = slice(first * PAIR_TILE, (first + tiles) * PAIR_TILE)
                    sp.dma_start(G.bp[rows], tokens_dram[rows]).then_inc(bp_here, 16)
                for c in range(NT // CHUNK):
                    with sp.Fori(0, CHUNK // 2) as i:
                        for u in range(2):
                            step(2 * i + (c * CHUNK + u), u)
                    fetch(c * CHUNK, CHUNK)
                for t in range(NT - NT % CHUNK, NT):
                    step(t, t % 2)
                fetch(NT - NT % CHUNK, NT % CHUNK)
                sp.wait_ge(bp_here, 16 * (NT // CHUNK + 1))
                sp.wait_ge(prep_out, 16 * LAYERS)

            @block.gpsimd
            def _(pool):
                pool.wait_ge(ids_here, 16)

                def step(t, k):
                    at_least(pool, z_turned, t - 1)
                    pool.tensor_copy(ids_tile[:, k, :],
                                     ids[:, ds(t * TILE_TOKENS, TILE_TOKENS)]).then_inc(ids_copied, 1)
                    pool.wait_ge(ids_copied, t + 1)
                    pool.sem_inc(tile_begun, 1)
                    for q in range(TILE_TOKENS):
                        pool.indirect_dma_start(
                            rows[:, k, q * HID:(q + 1) * HID], None, D["item_emb"],
                            bass.IndirectOffsetOnAxis(ap=ids_tile[:, k, q:q + 1], axis=0)
                        ).then_inc(rows_here[k], 16)
                run_steps(pool, NT, 0, step)

            @block.tensor
            def _(pe):
                pe.wait_ge(loads, 16 * len(weights))
                for l in range(LAYERS):
                    for c in range(2):
                        mm = pe.matmul(pk[l][0:HID, 0:NLAG], cw[:, l, c, :], dft[:, c, :],
                                       start=(c == 0), stop=(c == 1))
                    mm.then_inc(prep_made, 1)
                pe.wait_ge(prep_copied, 2)
                for l in range(LAYERS):
                    for ck in range(2):
                        mm = pe.matmul(pk0[:, (2 * l + ck) * HID:(2 * l + ck + 1) * HID],
                                       d2t[:, l, ck * 128:(ck + 1) * 128], G.center_m[0:HID, 0:HID],
                                       start=True, stop=True)
                pe.matmul(pk1[:, 0:LAYERS], G.center_m[:], d2b[:, :], start=True,
                          stop=True).then_inc(prep_made, 1)

                def step(t, k):
                    pe.wait_ge(rows_here[k], 16 * TILE_TOKENS * (half(t, k) + 1))
                    at_least(pe, z_ready, t)
                    for q in range(PAIR_TILE):
                        mm = pe.transpose(pz[:, q * NB:(q + 1) * NB], rows[:, k, q * PC:(q + 1) * PC], G.ident[:])
                    mm.then_inc(z_turned, 1)
                    pe.wait_ge(z_ready, t + 1)
                    at_least(pe, L.norm_done, t)
                    pe.matmul(L.centered[:, :], G.center_m[:], z[:, :], start=True,
                              stop=True).then_inc(L.centered_ready, 1)
                    pe_variance(pe, G, L, t)
                run_steps(pe, NT, 0, step)

            @block.scalar
            def _(act):
                act.preload_act_table_set("natural_log_exp_and_others")
                act.wait_ge(loads, 16 * len(weights))

                def step(t, k):
                    act_square(act, L, t)
                    act_rstd(act, L, t)
                    at_least(act, L.norm_done, t + 1)
                    at_least(act, stored[k], 16 * half(t, k))
                    act.activation(x0[:, k, :], y[:, :], ACT.Identity, bias=G.vec[:, 1:2],
                                   scale=G.vec[:, 0:1]).then_inc(x0_ready, 1)
                run_steps(act, NT, 0, step)

            @block.vector
            def _(dve):
                for l in range(LAYERS):
                    dve.wait_ge(prep_made, l + 1)
                    dve.tensor_copy(lag[:, l, :], pk[l][0:HID, 0:NLAG]).then_inc(lag_copied, 1)
                    dve.wait_ge(lag_copied, l + 1)
                    dve.tensor_scalar(lag[:, l, SEQ - 1:SEQ], pk[l][0:HID, SEQ - 1:SEQ], 1.0, None,
                                      ALU.add).then_inc(prep_copied, 1)
                dve.wait_ge(prep_made, 3)
                dve.tensor_copy(G.d2c[:], pk0[:, 0:4 * HID].rearrange("p (l c h) -> p l c h", l=2, c=2))
                dve.tensor_copy(G.d2bc[:], pk1[:, 0:LAYERS])
                dve.tensor_copy(G.center_s[:], center_f[:])
                dve.tensor_copy(G.center_r[:], G.center_m[:])
                dve.tensor_copy(G.d1h[:], d1[:]).then_inc(d1_high, 1)
                dve.wait_ge(d1_high, 1)
                dve.tensor_tensor(G.d1l[:], d1[:], G.d1h[:], ALU.subtract)

                def step(t, k):
                    dve.wait_ge(z_turned, t + 1)
                    at_least(dve, L.centered_ready, t)
                    dve.tensor_tensor(z[:].rearrange("p (j b) -> p j b", b=NB),
                                      pz[:, :].rearrange("p (j b) -> p j b", b=NB),
                                      pos[:, ds(t * PAIR_TILE, PAIR_TILE)].unsqueeze(2).to_broadcast([128, PAIR_TILE, NB]),
                                      ALU.add).then_inc(z_ready, 1)
                    dve.wait_ge(L.rstd_ready, t + 1)
                    at_least(dve, x0_ready, t)
                    dve.tensor_tensor(y[:, :], L.centered[:, :], L.rstd[:, :], ALU.mult).then_inc(L.norm_done, 1)
                run_steps(dve, NT, 0, step)



def phase_conv(nc, G, layer):
    with ExitStack() as ctx:
        tag = f"c{layer}_"
        sems = []

        def sem(name):
            sems.append(ctx.enter_context(nc.semaphore(tag + name)))
            return sems[-1]
        toep = ctx.enter_context(nc.sbuf_tensor(tag + "toep", [NJ, 2, 2, SEQ + 1], F32))
        po = [ctx.enter_context(nc.psum_tensor(f"{tag}po{i}", [128, 512], F32)) for i in range(2)]
        toep_here = [sem("toep_here0"), sem("toep_here1")]
        conv_made, po_out = sem("conv_made"), [sem("po_out0"), sem("po_out1")]
        steps = HID // 2

        with nc.Block() as block:
            @block.sync
            def _(sp):
                def step(t, k):
                    at_least(sp, conv_made, t - 1)
                    src = bass.AP(G.lag_dram.tensor, G.lag_dram[layer].offset + t * (2 * NLAG),
                                  [[2, NJ], [NLAG, 2], [1, SEQ + 1]])
                    sp.dma_start(toep[:, k, :, :], src).then_inc(toep_here[k], 16)
                run_steps(sp, steps, 0, step)

            @block.tensor
            def _(pe):
                def step(t, k):
                    pe.wait_ge(toep_here[k], 16 * half(t, k) + 16)
                    at_least(pe, po_out[k], half(t, k))
                    for ch in range(2):
                        for po_par in range(2):
                            for in_par in range(2):
                                a = 1 - po_par + in_par
                                mm = pe.matmul(
                                    po[k][0:NJ, (2 * po_par + ch) * NB:(2 * po_par + ch + 1) * NB],
                                    toep[:, k, ch, a:a + SEQ - 1:2],
                                    G.bp[:, ds(2 * t + (in_par * HID + ch), 1), :].rearrange("p f b -> p (f b)"),
                                    start=(in_par == 0), stop=(in_par == 1))
                    mm.then_inc(conv_made, 1)
                run_steps(pe, steps, 0, step)

            def out_ap(t):
                return G.y.rearrange("p b (o c) -> p o c b", o=2)[:, :, ds(2 * t, 2), :]

            def in_ap(k):
                return po[k][0:NJ, :].rearrange("p (o c b) -> p o c b", o=2, c=2)

            @block.vector
            def _(dve):
                def step(t, k):
                    if k == 0:
                        dve.wait_ge(conv_made, t + 1)
                        dve.tensor_copy(out_ap(t), in_ap(0)).then_inc(po_out[0], 1)
                run_steps(dve, steps, 0, step)

            @block.scalar
            def _(act):
                def step(t, k):
                    if k == 1:
                        act.wait_ge(conv_made, t + 1)
                        act.activation(out_ap(t), in_ap(1), ACT.Identity).then_inc(po_out[1], 1)
                run_steps(act, steps, 0, step)
        clear_all(nc, sems)



def phase_ffn(nc, G, layer):
    last = layer == LAYERS - 1
    NT = SEQ_TILES
    with ExitStack() as ctx:
        tag = f"f{layer}_"
        sb = lambda n, s, d=F32: ctx.enter_context(nc.sbuf_tensor(tag + n, s, d))
        pt = lambda n: ctx.enter_context(nc.psum_tensor(tag + n, [128, 512], F32))
        sems = []

        def sem(name):
            sems.append(ctx.enter_context(nc.semaphore(tag + name)))
            return sems[-1]
        L1 = Norm(ctx, nc, lambda n: sem("1" + n), tag + "n1", COLS, 1e-12)
        L2 = Norm(ctx, nc, lambda n: sem("2" + n), tag + "n2", COLS, 1e-12)
        rows = sb("rows", [NJ, 2, SEQ_TILE * PC])
        z = sb("z", [128, COLS])
        y1 = sb("y1", [128, COLS])
        c1, x1 = sb("c1", [128, COLS]), sb("x1", [128, COLS])
        x1s = sb("x1s", [128, 2, 2, COLS], F32R)
        y2 = sb("y2", [128, COLS])
        x2 = sb("x2", [128, 2, COLS])
        g = sb("g", [128, 2, 4, COLS])
        pz, pback = pt("pz"), pt("pback")
        pf = [pt("pf0"), pt("pf1")]
        rows_here = [sem("rows_here0"), sem("rows_here1")]
        z_turned, z_ready, x1_ready = sem("z_turned"), sem("z_ready"), sem("x1_ready")
        up_made, gelu_done, begun = sem("up_made"), sem("gelu_done"), sem("begun")
        high_ready, low_ready, c1_ready = sem("high_ready"), sem("low_ready"), sem("c1_ready")
        x2_ready, back_turned, back_done = sem("x2_ready"), sem("back_turned"), sem("back_done")
        w = lambda i: G.vec[:, i:i + 1]
        fw, fb, iw, ib = w(2 + layer), w(4 + layer), w(6 + layer), w(8 + layer)

        with nc.Block() as block:
            @block.sync
            def _(sp):
                def step(t, k):
                    at_least(sp, z_turned, t - 1)
                    sp.dma_start(rows[:, k, :], G.y_flat[:, ds(t * (SEQ_TILE * PC), SEQ_TILE * PC)]
                                 ).then_inc(rows_here[k], 16)
                run_steps(sp, NT, 0, step)

            @block.tensor
            def _(pe):
                def step(t, k):
                    n, m, u, v = t, t - 2, t - 3, t - 4

                    def up(q):
                        at_least(pe, gelu_done, 4 * m + q - 1)
                        par, ck = q // 2, q % 2
                        for part, w in enumerate((G.d1h, G.d1l)):
                            mm = pe.matmul(pf[q % 2][:, 0:COLS], w[:, layer, ck * 128:(ck + 1) * 128],
                                           x1s[:, k, par, :], start=(part == 0), stop=(part == 1))
                        mm.then_inc(up_made, 1)
                    if exists(m, NT):
                        pe.wait_ge(low_ready, 2 * m + 2)
                        up(0)
                        up(1)
                    if exists(n, NT):
                        pe.wait_ge(rows_here[k], 16 * half(n, k) + 16)
                        at_least(pe, z_ready, n)
                        for q in range(SEQ_TILE):
                            mm = pe.transpose(pz[:, q * NJ:(q + 1) * NJ], rows[:, k, q * PC:(q + 1) * PC],
                                              G.flip[:])
                        mm.then_inc(z_turned, 1)
                    if exists(u, NT):
                        at_least(pe, L2.norm_done, u)
                        for par in range(2):
                            pe.matmul(L2.centered[:, 0:COLS], G.center_s[:, par, :], x1s[:, 1 - k, par, :],
                                      start=(par == 0), stop=False, skip_group_check=True)
                        pe.wait_ge(gelu_done, 4 * u + 4)
                        for ck in range(2):
                            for par in range(2):
                                mm = pe.matmul(L2.centered[par * HID:(par + 1) * HID, 0:COLS],
                                               G.d2c[:, layer, ck, :], g[:, 1 - k, 2 * par + ck, :],
                                               start=False, stop=(ck == 1), skip_group_check=True)
                        mm.then_inc(L2.centered_ready, 1)
                    if exists(n, NT):
                        pe.wait_ge(z_ready, n + 1)
                        at_least(pe, c1_ready, n)
                        pe.matmul(L1.centered[:, 0:COLS], G.center_m[:], z[:, :], start=True,
                                  stop=True).then_inc(L1.centered_ready, 1)
                    if exists(m, NT):
                        up(2)
                        up(3)
                    if exists(u, NT):
                        pe_variance(pe, G, L2, u)
                    if exists(n, NT):
                        pe_variance(pe, G, L1, n)
                    if exists(v, NT) and not last:
                        pe.wait_ge(x2_ready, v + 1)
                        at_least(pe, back_done, v)
                        for q in range(SEQ_TILE):
                            mm = pe.transpose(pback[0:NJ, q * PC:(q + 1) * PC],
                                              x2[:, k, q * NJ:(q + 1) * NJ], G.ident[:])
                        mm.then_inc(back_turned, 1)
                run_steps(pe, NT, 4, step)

            @block.scalar
            def _(act):
                def step(t, k):
                    n, m, u = t, t - 2, t - 3

                    def gelu(q):
                        act.wait_ge(up_made, 4 * m + q + 1)
                        act.activation(g[:, k, q, :], pf[q % 2][:, 0:COLS], ACT.Gelu,
                                       bias=G.gelu_b[:, layer, q % 2:q % 2 + 1]).then_inc(gelu_done, 1)
                    if exists(m, NT):
                        at_least(act, L2.centered_ready, m - 1)
                        gelu(0)
                        gelu(1)
                    if exists(u, NT):
                        act_square(act, L2, u, bias=G.d2bc[:, layer:layer + 1])
                    if exists(m, NT):
                        gelu(2)
                        gelu(3)
                    act.preload_act_table_set("natural_log_exp_and_others")
                    if exists(u, NT):
                        act_rstd(act, L2, u)
                    if exists(n, NT):
                        act_rstd(act, L1, n)
                run_steps(act, NT, 3, step)

            @block.vector
            def _(dve):
                def step(t, k):
                    n, p, v, w = t, t - 1, t - 4, t - 5
                    if exists(v, NT):
                        dve.wait_ge(L2.rstd_ready, v + 1)
                        at_least(dve, x2_ready, v)
                        dve.scalar_tensor_tensor(out=y2[:, :], in0=L2.centered[:, 0:COLS],
                                                 scalar=G.d2bc[:, layer:layer + 1], in1=L2.rstd[:, :],
                                                 op0=ALU.add, op1=ALU.mult).then_inc(L2.norm_done, 1)
                    if exists(n, NT):
                        dve.wait_ge(z_turned, n + 1)
                        at_least(dve, L1.centered_ready, n)
                        dve.tensor_copy(z[:, :], pz[:, 0:COLS]).then_inc(z_ready, 1)
                    if exists(p, NT):
                        dve.wait_ge(L1.rstd_ready, p + 1)
                        at_least(dve, x1_ready, p)
                        dve.tensor_tensor(y1[:, :], c1[:, :], L1.rstd[:, :], ALU.mult).then_inc(L1.norm_done, 1)
                    if exists(v, NT) and last:
                        dve.wait_ge(L2.norm_done, v + 1)
                        dve.tensor_scalar(G.t_flat[:, ds(v * COLS, COLS)], y2[:, :], iw, ib, ALU.mult,
                                          ALU.add).then_inc(x2_ready, 1)
                    if exists(w, NT) and not last:
                        dve.wait_ge(back_turned, w + 1)
                        dve.tensor_copy(G.bp[:, :, ds(w * SEQ_TILE, SEQ_TILE)].rearrange("p f b -> p b f"),
                                        pback[0:NJ, :].rearrange("p (b f) -> p b f", f=PC)
                                        ).then_inc(back_done, 1)
                    if exists(p, NT):
                        dve.wait_ge(x1_ready, p + 1)
                        at_least(dve, L2.centered_ready, p - 1)
                        split_high(dve, x1s[:, 1 - k], x1, high_ready)
                        dve.wait_ge(high_ready, 2 * p + 2)
                    if exists(n, NT):
                        dve.wait_ge(L1.centered_ready, n + 1)
                        at_least(dve, L1.norm_done, n)
                        at_least(dve, L1.variance_ready, n)
                        dve.tensor_copy(c1[:, :], L1.centered[:, 0:COLS]).then_inc(c1_ready, 1)
                        dve.wait_ge(c1_ready, n + 1)
                        dve.tensor_tensor(L1.square[:, :], c1[:, :], c1[:, :], ALU.mult).then_inc(L1.square_ready, 1)
                    if exists(p, NT):
                        split_low(dve, x1s[:, 1 - k], x1, low_ready)
                run_steps(dve, NT, 4 if last else 5, step)

            @block.gpsimd
            def _(pool):
                def step(t, k):
                    p, v = t - 1, t - 4
                    if exists(v, NT) and not last:
                        pool.wait_ge(L2.norm_done, v + 1)
                        at_least(pool, back_turned, v - 1)
                        pool.sem_inc(begun, 1)
                        pool.tensor_scalar(x2[:, k, :], y2[:, :], iw, ib, ALU.mult, ALU.add).then_inc(x2_ready, 1)
                    if exists(p, NT):
                        pool.wait_ge(L1.norm_done, p + 1)
                        at_least(pool, low_ready, 2 * p)
                        pool.sem_inc(begun, 1)
                        pool.tensor_scalar(x1[:, :], y1[:, :], fw, fb, ALU.mult, ALU.add).then_inc(x1_ready, 1)
                run_steps(pool, NT, 4, step)
        clear_all(nc, sems)



def phase_attention(nc, G):
    D, NT = G.dram, SEQ_TILES
    with ExitStack() as ctx:
        sb = lambda n, s, d=F32: ctx.enter_context(nc.sbuf_tensor("a_" + n, s, d))
        pt = lambda n: ctx.enter_context(nc.psum_tensor("a_" + n, [128, 512], F32))
        sem = lambda n: G.ctx.enter_context(nc.semaphore("a_" + n))
        L = Norm(ctx, nc, sem, "a", COLS, 1e-5, parts=2)
        S = StreamParts(ctx, nc, sem, "a", COLS)
        TOK = SEQ_TILE * SEQ
        w1, w2, vw = sb("w1", [128, 128]), sb("w2", [128, 128]), sb("vw", [128, HID])
        mask, vb, vec = sb("mask", [NJ, 3 * NJ]), sb("vb", [NJ, HID]), sb("vec", [128, 8])
        xn = sb("xn", [128, 2, TOK])
        hid, phase, folded = sb("hid", [128, TOK]), sb("phase", [128, TOK]), sb("folded", [128, TOK])
        phik, phiq = sb("phik", [128, 2, TOK]), sb("phiq", [128, 2, TOK])
        v = sb("v", [NJ, 2, 2 * SEQ_TILE * HID])
        probs = sb("probs", [NJ, 2, 3 * NJ])
        wbase, rt = sb("wbase", [128, 2, SLOT]), sb("rt", [1, NGROUP], I32)
        r1, r2, r3 = (sb(f"r{i}", [1, NGROUP]) for i in range(3))
        pw = [pt("pw0"), pt("pw1")]
        pv, po = pt("pv"), pt("po")
        ps = [pt("ps0"), pt("ps1")]
        loads, cleared, table_ready = sem("loads"), sem("cleared"), sem("table_ready")
        chain = sem("chain")
        proj_made, tanh_done, folded_ready, phi_ready = sem("proj_made"), sem("tanh_done"), sem("folded_ready"), sem("phi_ready")
        v_made, v_ready = sem("v_made"), sem("v_ready")
        score_made, probs_ready, out_made, stream_done = sem("score_made"), sem("probs_ready"), sem("out_made"), sem("stream_done")
        weights = [(w1, D["a_w1"]), (w2, D["a_w2"]), (vw, D["a_vw"]), (mask, D["a_mask"]), (vb, D["a_vb"]),
                   (vec, D["a_vec"]), (G.expert_w, D["r_w"]), (wbase, D["r_base"]), (rt, D["route"])]

        with nc.Block() as block:
            @block.sync
            def _(sp):
                for dst, src in weights:
                    sp.dma_start(dst[:], src).then_inc(loads, 16)

            @block.gpsimd
            def _(pool):
                pool.memset(xn[HID:128, :, :], 0.0).then_inc(cleared, 1)
                pool.memset(phik[HID:128, :, :], 0.0).then_inc(cleared, 1)
                pool.memset(phiq[HID:128, :, :], 0.0).then_inc(cleared, 1)
                pool.wait_ge(cleared, 3)

                def step(t, k):
                    pool_split_stream(pool, S, L, t, k, G.t[:, ds(t * SEQ_TILE, SEQ_TILE), :], NJ)
                run_steps(pool, NT, 0, step)
                pool.wait_ge(loads, 16 * len(weights))
                for l in range(2):
                    pool.tensor_tensor(wbase[:, l, 0:LH], wbase[:, l, 0:LH], G.ident[:],
                                       ALU.add).then_inc(table_ready, 1)
                pool.wait_ge(table_ready, 2)
                for l in range(2):
                    pool.tensor_tensor(G.expert_w[:, l, :, :], G.expert_w[:, l, :, :],
                                       wbase[:, l, :].unsqueeze(1).to_broadcast([128, NEXP0 + 1, SLOT]),
                                       ALU.add)

            @block.tensor
            def _(pe):
                pe.wait_ge(loads, 16 * len(weights))
                pe.wait_ge(cleared, 3)

                def step(t, k):
                    n, m, s, r = t, t - 2, t - 3, t - 4
                    if exists(s, NT):
                        at_least(pe, v_ready, s)
                        for c in range(2 * SEQ_TILE):
                            mm = pe.matmul(pv[0:NJ, c * HID:(c + 1) * HID], xn[:, 1 - k, c * NJ:(c + 1) * NJ],
                                           vw[:], start=True, stop=True)
                        mm.then_inc(v_made, 1)
                    if exists(m, NT):
                        pe.wait_ge(L.norm_done, 2 * m + 2)
                        for h in range(2):
                            at_least(pe, tanh_done, 4 * m - 2 + h + 1)
                            pe.matmul(pw[h][:, 0:COLS], w1[:], xn[:, k, h * COLS:(h + 1) * COLS],
                                      start=True, stop=True).then_inc(proj_made, 1)

                    def center_and_project():
                        if exists(n, NT):
                            pe_center(pe, G, S, L, n, k)
                        if exists(m, NT):
                            for h in range(2):
                                pe.wait_ge(tanh_done, 4 * m + h + 1)
                                pe.matmul(pw[h][:, 0:COLS], w2[:], hid[:, h * COLS:(h + 1) * COLS],
                                          start=True, stop=True).then_inc(proj_made, 1)
                        if exists(n, NT):
                            pe_variance(pe, G, L, n)
                    if not exists(r, NT):
                        center_and_project()
                    else:
                        at_least(pe, stream_done, r)

                        def scores(b):
                            at_least(pe, probs_ready, SEQ_TILE * r + b - 1)
                            pe.matmul(ps[b % 2][0:NJ, 0:SEQ], phik[:, k, b * SEQ:b * SEQ + NJ],
                                      phiq[:, k, b * SEQ:(b + 1) * SEQ], start=True, stop=True)
                            pe.matmul(ps[b % 2][0:NJ, SEQ:SEQ + NJ], phik[:, k, b * SEQ + NJ:(b + 1) * SEQ],
                                      phiq[:, k, b * SEQ + NJ:(b + 1) * SEQ], start=True,
                                      stop=True).then_inc(score_made, 1)

                        def retrieve(b):
                            pe.wait_ge(probs_ready, SEQ_TILE * r + b + 1)
                            for c in range(2):
                                for par in range(2):
                                    mm = pe.matmul(
                                        po[par * HID:(par + 1) * HID, b * NJ + c * (NJ // 2):(b + 1) * NJ],
                                        v[:, k, (2 * b + c) * HID:(2 * b + c + 1) * HID],
                                        probs[:, b % 2, c * SEQ:SEQ + c * NJ].rearrange("p (j o) -> p j o", o=2)[:, :, par],
                                        start=(c == 0), stop=(c == 1), skip_group_check=True)
                            mm.then_inc(out_made, 1)
                        pe.wait_ge(phi_ready, 2 * r + 2)
                        pe.wait_ge(v_ready, r + 1)
                        scores(0)
                        scores(1)
                        center_and_project()
                        for b in range(2, SEQ_TILE):
                            retrieve(b - 2)
                            scores(b)
                        retrieve(SEQ_TILE - 2)
                        retrieve(SEQ_TILE - 1)
                run_steps(pe, NT, 4, step)

            @block.scalar
            def _(act):
                act.wait_ge(loads, 16 * len(weights))

                def step(t, k):
                    n, m, s = t, t - 2, t - 3
                    act.preload_act_table_set("silu_and_others")
                    if exists(m, NT):
                        for h in range(2):
                            act.wait_ge(proj_made, 4 * m + h + 1)
                            act.activation(hid[:, h * COLS:(h + 1) * COLS], pw[h][:, 0:COLS], ACT.Tanh,
                                           bias=vec[:, 0:1]).then_inc(tanh_done, 1)
                    if exists(s, NT):
                        act.wait_ge(folded_ready, s + 1)
                        at_least(act, out_made, SEQ_TILE * (s - 1))
                        act.activation(phik[0:HID, 1 - k, :], folded[0:HID, :], ACT.Sin,
                                       bias=vec[0:HID, 4:5], scale=vec[0:HID, 3:4]).then_inc(phi_ready, 1)
                    if exists(n, NT):
                        act_square(act, L, n)
                    if exists(s, NT):
                        act.activation(phiq[0:HID, 1 - k, :], folded[HID:128, :], ACT.Sin,
                                       bias=vec[HID:128, 4:5], scale=vec[HID:128, 3:4]).then_inc(phi_ready, 1)
                    if exists(m, NT):
                        at_least(act, folded_ready, m)
                        for h in range(2):
                            act.wait_ge(proj_made, 4 * m + h + 3)
                            act.activation(phase[:, h * COLS:(h + 1) * COLS], pw[h][:, 0:COLS], ACT.Tanh,
                                           bias=vec[:, 1:2]).then_inc(tanh_done, 1)
                    if exists(n, NT):
                        act.preload_act_table_set("natural_log_exp_and_others")
                        act_rstd(act, L, n)
                run_steps(act, NT, 3, step)

            @block.vector
            def _(dve):
                dve.wait_ge(loads, 16 * len(weights))
                count = [0]

                def link(ins):
                    count[0] += 1
                    ins.then_inc(chain, 1)
                    dve.wait_ge(chain, count[0])
                link(dve.tensor_scalar(r1[:], rt[:], 0.0, None, ALU.is_ge))
                link(dve.tensor_scalar(r2[:], rt[:], float(NEXP0 - 1), None, ALU.is_le))
                link(dve.tensor_tensor(r1[:], r1[:], r2[:], ALU.mult))
                link(dve.tensor_scalar(r3[:], rt[:], float(NEXP0), None, ALU.subtract))
                link(dve.tensor_tensor(r3[:], r3[:], r1[:], ALU.mult))
                link(dve.tensor_scalar(G.expert_of[:], r3[:], float(NEXP0), None, ALU.add))

                def step(t, k):
                    p, m, s, r = t - 1, t - 2, t - 3, t - 4

                    def masked(b):
                        dve.wait_ge(score_made, SEQ_TILE * r + b + 1)
                        at_least(dve, out_made, SEQ_TILE * r + b - 1)
                        dve.tensor_tensor(probs[:, b % 2, :], ps[b % 2][0:NJ, 0:3 * NJ], mask[:],
                                          ALU.mult).then_inc(probs_ready, 1)
                    if exists(s, NT):
                        dve.wait_ge(v_made, s + 1)
                        at_least(dve, out_made, SEQ_TILE * (s - 1))
                        dve.tensor_tensor(v[:, 1 - k, :].rearrange("p (c h) -> p c h", h=HID),
                                          pv[0:NJ, :].rearrange("p (c h) -> p c h", h=HID),
                                          vb[:].unsqueeze(1).to_broadcast([NJ, 2 * SEQ_TILE, HID]),
                                          ALU.add).then_inc(v_ready, 1)
                    if exists(p, NT):
                        dve.wait_ge(L.rstd_ready, p + 1)
                        at_least(dve, v_made, p - 1)
                        for par in range(2):
                            rows = slice(par * HID, (par + 1) * HID)
                            dve.tensor_tensor(xn[0:HID, 1 - k, :].rearrange("p (j o) -> p j o", o=2)[:, :, par],
                                              L.centered[rows, 0:COLS], L.rstd[rows, :],
                                              ALU.mult).then_inc(L.norm_done, 1)
                    if exists(r, NT):
                        for b in range(SEQ_TILE):
                            masked(b)
                    if exists(m, NT):
                        dve.wait_ge(tanh_done, 4 * m + 4)
                        at_least(dve, phi_ready, 2 * m)
                        dve.scalar_tensor_tensor(out=folded[:, :], in0=phase[:, :], scalar=vec[:, 2:3],
                                                 in1=phase[:, :], op0=ALU.mult,
                                                 op1=ALU.max).then_inc(folded_ready, 1)
                    if exists(r, NT):
                        dve.wait_ge(out_made, SEQ_TILE * r + SEQ_TILE)
                        dve.tensor_tensor(G.t_flat[:, ds(r * COLS, COLS)], po[:, 0:COLS],
                                          G.t_flat[:, ds(r * COLS, COLS)], ALU.add).then_inc(stream_done, 1)
                run_steps(dve, NT, 4, step)



def phase_routed(nc, G):
    D, NT = G.dram, SEQ_TILES
    with ExitStack() as ctx:
        sb = lambda n, s, d=F32: ctx.enter_context(nc.sbuf_tensor("r_" + n, s, d))
        pt = lambda n: ctx.enter_context(nc.psum_tensor("r_" + n, [128, 512], F32))
        sem = lambda n: G.ctx.enter_context(nc.semaphore("r_" + n))
        L = Norm(ctx, nc, sem, "r", COLS, 1e-5)
        wi, wo, vec = sb("wi", [128, LH]), sb("wo", [128, HID]), sb("vec", [128, 2])
        S = StreamParts(ctx, nc, sem, "r", COLS)
        wih, wil = sb("wih", [128, LH], F32R), sb("wil", [128, LH], F32R)
        xn = sb("xn", [128, COLS])
        xs = sb("xs", [128, 2, 2, COLS], F32R)
        high_ready, low_ready, prepared = sem("high_ready"), sem("low_ready"), sem("prepared")
        h0, h1, h2 = (sb(f"h{i}", [128, 2, 2, COLS]) for i in range(3))
        wa, wb = (sb(f"w{i}", [128, 2, 2, SLOT]) for i in "ab")
        pm = [pt(f"pm{i}") for i in range(4)]
        po = pt("po")
        loads = sem("loads")
        wa_here, wb_here = ([sem(f"w{i}_here{k}") for k in range(2)] for i in "ab")
        in_made, in_done = sem("in_made"), sem("in_done")
        a_made, a_done, b_made, b_done = sem("a_made"), sem("a_done"), sem("b_made"), sem("b_done")
        out_made, stream_done = sem("out_made"), sem("stream_done")
        weights = [(wi, D["r_wi"]), (wo, D["r_wo"]), (vec, D["r_vec"])]

        with nc.Block() as block:
            @block.sync
            def _(sp):
                for dst, src in weights:
                    sp.dma_start(dst[:], src).then_inc(loads, 16)

                def step(t, k):
                    for l, n, kn, w, here, done in ((0, t, k, wa, wa_here, a_done),
                                                    (1, t - 1, 1 - k, wb, wb_here, b_done)):
                        if not exists(n, NT):
                            continue
                        for g in range(2):
                            e = sp.value_load(G.expert_of[0:1, ds(2 * n + g, 1)], min_val=0, max_val=NEXP0)
                            if g == 0:
                                at_least(sp, done, 2 * n - 2)
                            sp.dma_start(w[:, kn, g, :], G.expert_w[:, l, ds(e, 1), :].rearrange("p e s -> p (e s)")
                                         ).then_inc(here[kn], 16)
                run_steps(sp, NT, 1, step)

            @block.gpsimd
            def _(pool):
                def step(t, k):
                    pool_split_stream(pool, S, L, t, k, G.t[:, ds(t * SEQ_TILE, SEQ_TILE), :], NJ)
                run_steps(pool, NT, 0, step)

            @block.tensor
            def _(pe):
                pe.wait_ge(loads, 16 * len(weights))
                pe.wait_ge(prepared, 2)

                def step(t, k):
                    n, i, a, b, o = t, t - 2, t - 3, t - 4, t - 5
                    if exists(n, NT):
                        pe_center(pe, G, S, L, n, k)
                    if exists(i, NT):
                        pe.wait_ge(low_ready, 2 * i + 2)
                        at_least(pe, b_done, 2 * (t - 4))
                        for par in range(2):
                            pe.matmul(pm[par][:, 0:COLS], wih[:], xs[:, k, par, :], start=True, stop=False)
                            pe.matmul(pm[par][:, 0:COLS], wil[:], xs[:, k, par, :], start=False,
                                      stop=True).then_inc(in_made, 1)
                    if exists(a, NT):
                        pe.wait_ge(in_done, 2 * a + 2)
                        pe.wait_ge(wa_here[1 - k], 32 * half(a, 1 - k) + 32)
                        at_least(pe, a_done, 2 * a)
                        for g in range(2):
                            pe.matmul(pm[2 + g][:, 0:COLS].rearrange("p (o c) -> p o c", o=2), wa[:, 1 - k, g, 0:LH],
                                      h0[:, 1 - k, :, g * GCOLS:(g + 1) * GCOLS], start=True,
                                      stop=True).then_inc(a_made, 1)
                    if exists(n, NT):
                        pe_variance(pe, G, L, n)
                    if exists(b, NT):
                        pe.wait_ge(a_done, 2 * b + 2)
                        at_least(pe, b_done, 2 * b)
                        at_least(pe, in_done, 2 * min(t - 1, NT) if isinstance(t, int) else 2 * t - 2)
                        pe.wait_ge(wb_here[k], 32 * half(b, k) + 32)
                        for g in range(2):
                            pe.matmul(pm[g][:, 0:COLS], wb[:, k, g, 0:LH], h1[:, k, g, :], start=True,
                                      stop=True).then_inc(b_made, 1)
                    if exists(o, NT):
                        pe.wait_ge(b_done, 2 * o + 2)
                        at_least(pe, stream_done, o)
                        for g in range(2):
                            for par in range(2):
                                mm = pe.matmul(po[par * HID:(par + 1) * HID, g * GCOLS:(g + 1) * GCOLS], wo[:],
                                               h2[:, 1 - k, g, par * GCOLS:(par + 1) * GCOLS], start=True, stop=True,
                                               skip_group_check=True)
                        mm.then_inc(out_made, 1)
                run_steps(pe, NT, 5, step)

            @block.scalar
            def _(act):
                act.preload_act_table_set("natural_log_exp_and_others")
                act.wait_ge(loads, 16 * len(weights))

                def step(t, k):
                    n, i, a, b = t, t - 2, t - 3, t - 4
                    if exists(n, NT):
                        act_square(act, L, n)
                    if exists(i, NT):
                        at_least(act, a_made, 2 * (i - 1))
                        for par in range(2):
                            act.wait_ge(in_made, 2 * i + par + 1)
                            act.activation(h0[:, k, par, :], pm[par][:, 0:COLS], ACT.Relu,
                                           bias=vec[:, 0:1]).then_inc(in_done, 1)
                    if exists(n, NT):
                        act_rstd(act, L, n)
                    if exists(b, NT):
                        at_least(act, out_made, b - 1)
                        for g in range(2):
                            act.wait_ge(b_made, 2 * b + g + 1)
                            act.activation(h2[:, k, g, :], pm[g][:, 0:COLS], ACT.Relu,
                                           bias=wb[:, k, g, LH:SLOT]).then_inc(b_done, 1)
                run_steps(act, NT, 4, step)

            @block.vector
            def _(dve):
                dve.wait_ge(loads, 16 * len(weights))
                dve.tensor_copy(wih[:], wi[:]).then_inc(prepared, 1)
                dve.wait_ge(prepared, 1)
                dve.tensor_tensor(wil[:], wi[:], wih[:], ALU.subtract).then_inc(prepared, 1)

                def step(t, k):
                    n, a, o = t, t - 3, t - 5
                    if exists(a, NT):
                        at_least(dve, b_made, 2 * (a - 1))
                        for g in range(2):
                            dve.wait_ge(a_made, 2 * a + g + 1)
                            dve.tensor_scalar(h1[:, 1 - k, g, :], pm[2 + g][:, 0:COLS], wa[:, 1 - k, g, LH:SLOT], 0.0,
                                              ALU.add, ALU.max).then_inc(a_done, 1)
                    if exists(n, NT):
                        dve.wait_ge(L.rstd_ready, n + 1)
                        at_least(dve, low_ready, 2 * n)
                        dve.tensor_tensor(xn[:, :], L.centered[:, 0:COLS], L.rstd[:, :],
                                          ALU.mult).then_inc(L.norm_done, 1)
                        dve.wait_ge(L.norm_done, n + 1)
                        at_least(dve, in_made, 2 * (n - 1))
                        split_high(dve, xs[:, k], xn, high_ready)
                    if exists(o, NT):
                        dve.wait_ge(out_made, o + 1)
                        dve.scalar_tensor_tensor(out=G.t_flat[:, ds(o * COLS, COLS)], in0=po[:, 0:COLS],
                                                 scalar=vec[:, 1:2], in1=G.t_flat[:, ds(o * COLS, COLS)],
                                                 op0=ALU.add, op1=ALU.add).then_inc(stream_done, 1)
                    if exists(n, NT):
                        dve.wait_ge(high_ready, 2 * n + 2)
                        split_low(dve, xs[:, k], xn, low_ready)
                run_steps(dve, NT, 5, step)



def phase_ssm(nc, G):
    D, NT = G.dram, PAIR_TILES
    P1 = HID + 1
    with ExitStack() as ctx:
        sb = lambda n, s, d=F32: ctx.enter_context(nc.sbuf_tensor("s_" + n, s, d))
        pt = lambda n: ctx.enter_context(nc.psum_tensor("s_" + n, [128, 512], F32))
        sem = lambda n: G.ctx.enter_context(nc.semaphore("s_" + n))
        L = Norm(ctx, nc, sem, "s", PCOLS, 1e-5, banks=2)
        S = StreamParts(ctx, nc, sem, "s", PCOLS)
        lam = sb("lam", [128, 3, P1])
        bt, crt, col = sb("bt", [128, 2, HID]), sb("crt", [128, HID]), sb("col", [128, 2])
        shift = sb("shift", [128, 128])
        T = sb("prep", [128, 20, P1])
        qi = sb("qi", [128, P1], I32)
        wut, wu = sb("wut", [128, 128]), sb("wu", [128, 128])
        bb = sb("bb", [128, 128])
        a2t, a1, gt, kt = sb("a2t", [128, 128]), sb("a1", [128, 128]), sb("gt", [128, 128]), sb("kt", [128, 128])
        xn = sb("xn", [128, 2, PCOLS])
        state = sb("state", [128, PAIR_TILE, NB])
        px, py = [pt("px0"), pt("px1")], [pt("py0"), pt("py1")]
        pp = [px[0], px[1], py[0]]
        loads, chain, exp_done, sin_done = sem("loads"), sem("chain"), sem("exp_done"), sem("sin_done")
        delta_ready, angle_ready, prep_made, mats_ready = sem("delta_ready"), sem("angle_ready"), sem("prep_made"), sem("mats_ready")
        part_ready = sem("part_ready")
        x_made, x_ready, y_made, stream_done, inject_made = sem("x_made"), sem("x_ready"), sem("y_made"), sem("stream_done"), sem("inject_made")
        weights = [(lam, D["s_lam"]), (bt, D["s_bt"]), (crt, D["s_crt"]), (col, D["s_col"]), (shift, D["s_shift"])]
        stream = G.t.rearrange("p b j -> p j b")
        (MAG, ANG, RED, SIN, ABSA, COS, ARE, AIM, T0, T1, A2R, A2I, NRE, FRE, FIM, BRE, BIM, CRE, CIM, DEL) = range(20)
        c = lambda i: T[:, i, :]
        h = lambda i: T[:, i, 0:HID]
        own = lambda i: T[:, i, HID:P1]
        S4 = PAIR_TILE

        with nc.Block() as block:
            @block.sync
            def _(sp):
                for dst, src in weights:
                    sp.dma_start(dst[:], src).then_inc(loads, 16)

            @block.gpsimd
            def _(pool):
                def step(t, k):
                    pool_split_stream(pool, S, L, t, k, stream[:, ds(t * PAIR_TILE, PAIR_TILE), :], NB)
                run_steps(pool, NT, 0, step)

            @block.scalar
            def _(act):
                act.wait_ge(loads, 16 * len(weights))
                act.activation(c(DEL), lam[:, 2, :], ACT.Exp).then_inc(exp_done, 1)
                act.wait_ge(delta_ready, 1)
                act.activation(c(MAG), c(T0), ACT.Exp).then_inc(exp_done, 1)
                act.wait_ge(angle_ready, 1)
                act.activation(c(SIN), c(RED), ACT.Sin).then_inc(sin_done, 1)
                act.activation(c(COS), c(ABSA), ACT.Sin, bias=PI / 2, scale=-1.0).then_inc(sin_done, 1)
                act.preload_act_table_set("natural_log_exp_and_others")

                def step(t, k):
                    act_square(act, L, t, bank=k)
                    act_rstd(act, L, t)
                run_steps(act, NT, 0, step)

            @block.tensor
            def _(pe):
                pe.wait_ge(part_ready, 1)
                pe.transpose(pp[0][:, 0:128], wut[:], G.ident[:])
                pe.matmul(pp[1][:, 0:HID], a1[:], crt[:], start=True, stop=True).then_inc(prep_made, 1)
                pe.wait_ge(part_ready, 2)
                pe.matmul(pp[2][:, 0:HID], bb[:], crt[:], start=True, stop=True)
                pe.matmul(pp[2][0:HID, HID:128], wu[:, 0:HID], crt[:], start=True, stop=True,
                          skip_group_check=True)
                pe.matmul(pp[1][:, HID:128], a1[:], gt[:, 0:HID], start=True, stop=True,
                          skip_group_check=True).then_inc(prep_made, 1)
                pe.wait_ge(mats_ready, 1)

                def step(t, k):
                    n, i, m = t, t - 1, t - 2

                    def inject():
                        if exists(i, NT):
                            pe.wait_ge(L.norm_done, i + 1)
                            at_least(pe, x_ready, S4 * (i - 1) + 1)
                            pe.matmul(px[1 - k][:, :], wut[:], xn[:, 1 - k, :], start=True, stop=False,
                                      skip_group_check=True)

                    def center():
                        if exists(n, NT):
                            pe_center(pe, G, S, L, n, k)

                    def advance(q):
                        pe.wait_ge(x_ready, S4 * m + q + 1)
                        pe.matmul(px[k][:, q * NB:(q + 1) * NB], a2t[:], state[:, (q - 1) % S4, :], start=False,
                                  stop=True, skip_group_check=True).then_inc(x_made, 1)

                    def observe(q):
                        mm = pe.matmul(py[k][:, q * NB:(q + 1) * NB], gt[:], state[:, (q - 1) % S4, :], start=False,
                                       stop=True, skip_group_check=True)
                        if q == S4 - 1:
                            mm.then_inc(y_made, 1)
                    if not exists(m, NT):
                        center()
                        inject()
                        pe_variance(pe, G, L, n)
                        return
                    advance(0)
                    at_least(pe, stream_done, m - 1)
                    pe.matmul(py[k][:, :], kt[:], xn[:, k, :], start=True, stop=False,
                              skip_group_check=True).then_inc(inject_made, 1)
                    observe(0)
                    advance(1)
                    center()
                    observe(1)
                    advance(2)
                    inject()
                    observe(2)
                    advance(3)
                    if exists(n, NT):
                        pe_variance(pe, G, L, n)
                    observe(3)
                run_steps(pe, NT, 2, step)

            @block.vector
            def _(dve):
                count = [0]

                def link(ins):
                    count[0] += 1
                    ins.then_inc(chain, 1)
                    dve.wait_ge(chain, count[0])

                def mul(o, a, b):
                    link(dve.tensor_tensor(o, a, b, ALU.mult))

                def addsub(o, a, b, op):
                    link(dve.tensor_tensor(o, a, b, op))

                def cmul(ore, oim, are, aim, bre, bim, t0, t1):
                    mul(t0, are, bre)
                    mul(t1, aim, bim)
                    addsub(ore, t0, t1, ALU.subtract)
                    mul(t0, are, bim)
                    mul(t1, aim, bre)
                    addsub(oim, t0, t1, ALU.add)
                dve.wait_ge(loads, 16 * len(weights))
                lre, lim = lam[:, 0, :], lam[:, 1, :]
                dve.wait_ge(exp_done, 1)
                dve.tensor_tensor(c(T0), lre, c(DEL), ALU.mult).then_inc(delta_ready, 1)
                mul(c(ANG), lim, c(DEL))
                link(dve.tensor_scalar(qi[:], c(ANG), 1.0 / (2 * PI), None, ALU.mult))
                link(dve.tensor_copy(c(T1), qi[:]))
                link(dve.scalar_tensor_tensor(out=c(RED), in0=c(T1), scalar=-6.28125, in1=c(ANG), op0=ALU.mult, op1=ALU.add))
                link(dve.scalar_tensor_tensor(out=c(RED), in0=c(T1), scalar=-(2 * PI - 6.28125), in1=c(RED), op0=ALU.mult, op1=ALU.add))
                for op, turn in ((ALU.is_gt, -2 * PI), (ALU.is_lt, 2 * PI)):
                    link(dve.tensor_scalar(c(T1), c(RED), PI if turn < 0 else -PI, turn, op, ALU.mult))
                    addsub(c(RED), c(RED), c(T1), ALU.add)
                link(dve.tensor_scalar(c(RED), c(RED), 3.1415925, -3.1415925, ALU.min, ALU.max))
                link(dve.scalar_tensor_tensor(out=c(ABSA), in0=c(RED), scalar=-1.0, in1=c(RED), op0=ALU.mult, op1=ALU.max))
                link(dve.memset(kt[:], 0.0))
                dve.tensor_scalar(crt[HID:128, :], crt[HID:128, :], -1.0, None, ALU.mult).then_inc(angle_ready, 1)
                dve.wait_ge(exp_done, 2)
                dve.wait_ge(sin_done, 2)
                mul(c(ARE), c(MAG), c(COS))
                mul(c(AIM), c(MAG), c(SIN))
                cmul(c(A2R), c(A2I), c(ARE), c(AIM), c(ARE), c(AIM), c(T0), c(T1))
                link(dve.tensor_scalar(c(NRE), c(ARE), 1.0, None, ALU.subtract))
                mul(c(T0), lre, lre)
                mul(c(T1), lim, lim)
                addsub(c(T0), c(T0), c(T1), ALU.add)
                link(dve.reciprocal(c(DEL), c(T0)))
                mul(c(T0), c(NRE), lre)
                mul(c(T1), c(AIM), lim)
                addsub(c(T0), c(T0), c(T1), ALU.add)
                mul(c(FRE), c(T0), c(DEL))
                mul(c(T0), c(AIM), lre)
                mul(c(T1), c(NRE), lim)
                addsub(c(T0), c(T0), c(T1), ALU.subtract)
                mul(c(FIM), c(T0), c(DEL))
                cmul(h(BRE), h(BIM), h(FRE), h(FIM), bt[:, 0, :], bt[:, 1, :], h(T0), h(T1))
                cmul(h(CRE), h(CIM), h(ARE), h(AIM), h(BRE), h(BIM), h(T0), h(T1))
                for half_rows, re, im in ((slice(0, HID), CRE, CIM), (slice(HID, 128), BRE, BIM)):
                    link(dve.tensor_copy(wut[half_rows, 0:HID], T[half_rows, re, 0:HID]))
                    link(dve.tensor_copy(wut[half_rows, HID:128], T[half_rows, im, 0:HID]))
                sign = col[:, 1:2]
                mul(own(T0), own(A2I), sign)
                mul(own(T1), own(AIM), sign)
                link(dve.tensor_scalar(own(T1), own(T1), -1.0, None, ALU.mult))
                link(dve.tensor_scalar(a2t[:], G.ident[:], own(A2R), None, ALU.mult))
                link(dve.scalar_tensor_tensor(out=a2t[:], in0=shift[:], scalar=own(T0), in1=a2t[:], op0=ALU.mult, op1=ALU.add))
                link(dve.tensor_scalar(a1[:], G.ident[:], own(ARE), None, ALU.mult))
                dve.scalar_tensor_tensor(out=a1[:], in0=shift[:], scalar=own(T1), in1=a1[:], op0=ALU.mult,
                                         op1=ALU.add).then_inc(part_ready, 1)
                dve.wait_ge(prep_made, 1)
                dve.tensor_copy(wu[:], pp[0][:, 0:128])
                dve.tensor_copy(bb[:, 0:HID], pp[0][:, HID:128])
                dve.tensor_copy(bb[:, HID:128], pp[0][:, HID:128])
                dve.tensor_copy(gt[:, 0:HID], pp[1][:, 0:HID]).then_inc(part_ready, 1)
                dve.wait_ge(prep_made, 2)
                dve.tensor_copy(gt[:, HID:128], pp[1][:, HID:128])
                link(dve.tensor_copy(kt[0:HID, 0:HID], pp[2][0:HID, 0:HID]))
                link(dve.tensor_copy(kt[0:HID, HID:128], pp[2][0:HID, HID:128]))
                link(dve.tensor_copy(kt[HID:128, HID:128], pp[2][HID:128, 0:HID]))
                dve.scalar_tensor_tensor(out=kt[:], in0=G.ident[:], scalar=col[:, 0:1], in1=kt[:], op0=ALU.mult,
                                         op1=ALU.add).then_inc(mats_ready, 1)
                dve.memset(state[:, S4 - 1, :], 0.0).then_inc(x_ready, 1)

                def step(t, k):
                    p, m, o = t - 1, t - 2, t - 3

                    def keep(q):
                        if exists(m, NT):
                            dve.wait_ge(x_made, S4 * m + q + 1)
                            dve.tensor_copy(state[:, q, :], px[k][:, q * NB:(q + 1) * NB]).then_inc(x_ready, 1)
                    keep(0)
                    if exists(p, NT):
                        dve.wait_ge(L.rstd_ready, p + 1)
                        at_least(dve, inject_made, p - 1)
                        dve.tensor_tensor(xn[:, 1 - k, :], L.centered_banks[1 - k][:, :], L.rstd[:, :],
                                          ALU.mult).then_inc(L.norm_done, 1)
                    keep(1)
                    if exists(o, NT):
                        dve.wait_ge(y_made, o + 1)
                        dve.tensor_tensor(stream[:, ds(o * S4, S4), :],
                                          py[1 - k][:, :].rearrange("p (j b) -> p j b", b=NB),
                                          stream[:, ds(o * S4, S4), :], ALU.add).then_inc(stream_done, 1)
                    keep(2)
                    keep(3)
                run_steps(dve, NT, 3, step)



def phase_experts(nc, G, out):
    D, NT = G.dram, PAIR_TILES
    with ExitStack() as ctx:
        sb = lambda n, s, d=F32: ctx.enter_context(nc.sbuf_tensor("x_" + n, s, d))
        pt = lambda n, d=F32: ctx.enter_context(nc.psum_tensor("x_" + n, [128, 2048 // (4 if d is F32 else 2)], d))
        sem = lambda n: G.ctx.enter_context(nc.semaphore("x_" + n))
        L = Norm(ctx, nc, sem, "x", PCOLS, 1e-5)
        S = StreamParts(ctx, nc, sem, "x", PCOLS)
        PE2 = 2 * NEXP1
        LG = PAIR_TILE * PE2
        rw, rb, tie = sb("rw", [128, PE2]), sb("rb", [NB, PE2]), sb("tie", [NB, LG])
        w1, w1h, w1l = sb("w1", [128, FCH * 128]), sb("w1h", [128, FCH * 128], F32R), sb("w1l", [128, FCH * 128], F32R)
        b1, w2 = sb("b1", [128, FCH]), sb("w2", [128, FCH, HID])
        b2f, b2p = sb("b2f", [128, 2, 128]), sb("b2p", [128, 3, 128], BF16)
        maskf, maskb = sb("maskf", [128, 2, FCH, 128]), sb("maskb", [128, 2, FCH, 128], BF16)
        identb = sb("identb", [128, 128], BF16)
        xn = sb("xn", [128, 2, PCOLS])
        xs = sb("xs", [128, 2, 2, PCOLS], F32R)
        high_ready, low_ready = sem("high_ready"), sem("low_ready")
        logit, hit = sb("logit", [NB, LG]), sb("hit", [NB, LG])
        top, first = sb("top", [NB, 2 * PAIR_TILE]), sb("first", [NB, 2 * PAIR_TILE])
        onehot = sb("onehot", [NB, LG], BF16)
        choice = sb("choice", [128, 2, PCOLS], BF16)
        hm = sb("hm", [128, 2, FCH, PCOLS])
        fin = sb("fin", [128, 2, PCOLS])
        outs = sb("outs", [NB, 2, PCOLS])
        plog, pch, pfin, po = pt("plog"), pt("pch", BF16), pt("pfin"), pt("po")
        pf = [pt("pf0"), pt("pf1")]
        loads, cleared, prep, prep_done = sem("loads"), sem("cleared"), sem("prep"), sem("prep_done")
        logit_made, logit_ready = sem("logit_made"), sem("logit_ready")
        top_ready, hit_ready, tied_ready, first_ready = sem("top_ready"), sem("hit_ready"), sem("tied_ready"), sem("first_ready")
        onehot_ready, choice_made, choice_ready = sem("onehot_ready"), sem("choice_made"), sem("choice_ready")
        up_made, relu0, relu1 = sem("up_made"), sem("relu0"), sem("relu1")
        down_made, fin_ready, fin_made, outs_ready = sem("down_made"), sem("fin_ready"), sem("fin_made"), sem("outs_ready")
        stored, turn_begun = [sem("stored0"), sem("stored1")], sem("turn_begun")
        split_begun = sem("split_begun")
        weights = [(rw, D["x_rw"]), (rb, D["x_rb"]), (tie, D["x_tie"]), (w1, D["x_w1"]), (b1, D["x_b1"]),
                   (w2, D["x_w2"]), (maskf, D["x_mask"])]
        stream = G.t.rearrange("p b j -> p j b")
        out_rows = out.rearrange("b s c -> b (s c)")
        S4 = PAIR_TILE
        by_expert = lambda a: a.rearrange("p (g e) -> p g e", e=NEXP1)

        with nc.Block() as block:
            @block.sync
            def _(sp):
                for dst, src in weights:
                    sp.dma_start(dst[:], src).then_inc(loads, 16)
                sp.dma_start(b2f[:, 0, :], D["x_b2"]).then_inc(loads, 16)

                def step(t, k):
                    sp.wait_ge(outs_ready, t + 1)
                    sp.dma_start(out_rows[:, ds(t * PCOLS, PCOLS)], outs[:, k, :]).then_inc(stored[k], 16)
                run_steps(sp, NT, 0, step)
                sp.wait_ge(stored[0], 16 * (NT // 2 + 1))
                sp.wait_ge(stored[1], 16 * (NT // 2))

            @block.gpsimd
            def _(pool):
                pool.memset(choice[HID:128, :, :], 0.0).then_inc(cleared, 1)
                pool.wait_ge(cleared, 1)
                pool.memset(choice[HID:HID + 1, :, :], 1.0).then_inc(prep_done, 1)
                pool.wait_ge(prep_done, 2)

                def step(t, k):
                    i = t - 1
                    if exists(t, NT):
                        at_least(pool, high_ready, 2 * (t - 1))
                        pool_split_stream(pool, S, L, t, k, stream[:, ds(t * S4, S4), :], NB)
                    if exists(i, NT):
                        at_least(pool, S.low_ready, t + 1 if exists(t, NT) else NT)
                        pool.wait_ge(L.norm_done, i + 1)
                        at_least(pool, up_made, 2 * FCH * (i - 1))
                        pool.sem_inc(split_begun, 1)
                        split_high(pool, xs[:, 1 - k], xn[:, 1 - k, :], high_ready)
                run_steps(pool, NT, 1, step)

            @block.tensor
            def _(pe):
                pe.wait_ge(loads, 16 * (len(weights) + 1))
                pe.wait_ge(prep_done, 2)

                def step(t, k):
                    n, i, m, f = t, t - 1, t - 2, t - 3
                    if exists(i, NT):
                        pe.wait_ge(L.norm_done, i + 1)
                        at_least(pe, logit_ready, i)
                        for q in range(S4):
                            mm = pe.matmul(plog[:, q * PE2:(q + 1) * PE2], xn[:, 1 - k, q * NB:(q + 1) * NB], rw[:],
                                           start=True, stop=True)
                        mm.then_inc(logit_made, 1)
                    if exists(n, NT):
                        pe_center(pe, G, S, L, n, k)
                    if exists(m, NT):
                        pe.wait_ge(choice_ready, m + 1)
                        pe.wait_ge(low_ready, 2 * m + 2)
                        for u in range(2 * FCH):
                            ck, par = u // 2, u % 2
                            at_least(pe, (relu0, relu1)[par], FCH * m + ck)
                            pe.matmul(pf[par][:, :], maskb[:, par, ck, :], choice[:, k, :], start=True, stop=False)
                            pe.matmul(pf[par][:, :], w1h[:, ck * 128:(ck + 1) * 128], xs[:, k, par, :], start=False,
                                      stop=False)
                            pe.matmul(pf[par][:, :], w1l[:, ck * 128:(ck + 1) * 128], xs[:, k, par, :], start=False,
                                      stop=True).then_inc(up_made, 1)
                            if u == 3 and exists(n, NT):
                                pe_variance(pe, G, L, n)
                        at_least(pe, fin_ready, m)
                        for j in range(3):
                            pe.matmul(po[:, :], b2p[:, j, :], choice[:, k, :], start=(j == 0), stop=False,
                                      skip_group_check=True)
                        for ck in range(FCH):
                            pe.wait_ge(relu0, FCH * m + ck + 1)
                            pe.wait_ge(relu1, FCH * m + ck + 1)
                            for par in range(2):
                                mm = pe.matmul(po[par * HID:(par + 1) * HID, :], w2[:, ck, :], hm[:, par, ck, :],
                                               start=False, stop=(ck == FCH - 1), skip_group_check=True)
                        mm.then_inc(down_made, 1)
                    elif exists(n, NT):
                        pe_variance(pe, G, L, n)
                    if exists(f, NT):
                        pe.wait_ge(fin_ready, f + 1)
                        at_least(pe, outs_ready, f)
                        for q in range(S4):
                            mm = pe.transpose(pfin[:, q * 128:(q + 1) * 128], fin[:, 1 - k, q * NB:(q + 1) * NB],
                                              G.ident[:])
                        mm.then_inc(fin_made, 1)
                    if exists(i, NT):
                        pe.wait_ge(onehot_ready, i + 1)
                        at_least(pe, choice_ready, i)
                        pe.sem_inc(turn_begun, 1)
                        for q in range(S4):
                            mm = pe.transpose(pch[0:PE2, q * NB:(q + 1) * NB], onehot[:, q * PE2:(q + 1) * PE2],
                                              identb[:])
                        mm.then_inc(choice_made, 1)
                run_steps(pe, NT, 3, step)

            @block.scalar
            def _(act):
                act.preload_act_table_set("natural_log_exp_and_others")
                act.wait_ge(loads, 16 * (len(weights) + 1))

                def step(t, k):
                    n, m, f = t, t - 2, t - 3
                    if exists(n, NT):
                        act_square(act, L, n)
                    if exists(m, NT):
                        at_least(act, down_made, m)
                        for ck in range(FCH):
                            act.wait_ge(up_made, 2 * FCH * m + 2 * ck + 1)
                            act.activation(hm[:, 0, ck, :], pf[0][:, :], ACT.Relu,
                                           bias=b1[:, ck:ck + 1]).then_inc(relu0, 1)
                            if ck == 2 and exists(n, NT):
                                act_rstd(act, L, n)
                    elif exists(n, NT):
                        act_rstd(act, L, n)
                    if exists(f, NT):
                        act.wait_ge(fin_made, f + 1)
                        at_least(act, stored[1 - k], 16 * half(f, 1 - k))
                        act.activation(outs[:, 1 - k, :], pfin[:, :], ACT.Identity).then_inc(outs_ready, 1)
                run_steps(act, NT, 3, step)

            @block.vector
            def _(dve):
                dve.wait_ge(loads, 16 * (len(weights) + 1))
                dve.tensor_copy(identb[:], G.ident[:])
                dve.tensor_copy(maskb[:], maskf[:])
                dve.tensor_copy(w1h[:], w1[:]).then_inc(prep, 1)
                dve.wait_ge(prep, 1)
                dve.tensor_tensor(w1l[:], w1[:], w1h[:], ALU.subtract).then_inc(prep, 1)
                dve.tensor_copy(b2p[:, 0, :], b2f[:, 0, :]).then_inc(prep, 1)
                dve.wait_ge(prep, 3)
                dve.tensor_tensor(b2f[:, 1, :], b2f[:, 0, :], b2p[:, 0, :], ALU.subtract).then_inc(prep, 1)
                dve.wait_ge(prep, 4)
                dve.tensor_copy(b2p[:, 1, :], b2f[:, 1, :]).then_inc(prep, 1)
                dve.wait_ge(prep, 5)
                dve.tensor_tensor(b2f[:, 0, :], b2f[:, 1, :], b2p[:, 1, :], ALU.subtract).then_inc(prep, 1)
                dve.wait_ge(prep, 6)
                dve.tensor_copy(b2p[:, 2, :], b2f[:, 0, :]).then_inc(prep_done, 1)

                def step(t, k):
                    n, i, m = t, t - 1, t - 2

                    def relu(cks):
                        for ck in cks:
                            dve.wait_ge(up_made, 2 * FCH * m + 2 * ck + 2)
                            dve.tensor_scalar(hm[:, 1, ck, :], pf[1][:, :], b1[:, ck:ck + 1], 0.0, ALU.add,
                                              ALU.max).then_inc(relu1, 1)
                    if exists(i, NT):
                        dve.wait_ge(logit_made, i + 1)
                        dve.tensor_tensor(logit[:, :].rearrange("p (q e) -> p q e", e=PE2),
                                          plog[:, 0:LG].rearrange("p (q e) -> p q e", e=PE2),
                                          rb[:].unsqueeze(1).to_broadcast([NB, S4, PE2]), ALU.add).then_inc(logit_ready, 1)
                        dve.wait_ge(logit_ready, i + 1)
                        dve.tensor_reduce(top[:, :], by_expert(logit[:, :]), AX_X, ALU.max).then_inc(top_ready, 1)
                        dve.wait_ge(top_ready, i + 1)
                        dve.tensor_tensor(by_expert(hit[:, :]), by_expert(logit[:, :]),
                                          top[:].unsqueeze(2).to_broadcast([NB, 2 * S4, NEXP1]), ALU.is_ge).then_inc(hit_ready, 1)
                        dve.wait_ge(hit_ready, i + 1)
                    if exists(m, NT):
                        at_least(dve, down_made, m)
                        relu(range(0, 1))
                    if exists(i, NT):
                        dve.tensor_tensor(logit[:, :], hit[:, :], tie[:, :], ALU.mult).then_inc(tied_ready, 1)
                        dve.wait_ge(tied_ready, i + 1)
                        dve.tensor_reduce(first[:, :], by_expert(logit[:, :]), AX_X, ALU.max).then_inc(first_ready, 1)
                        dve.wait_ge(first_ready, i + 1)
                        at_least(dve, choice_made, i)
                        dve.tensor_tensor(by_expert(onehot[:, :]), by_expert(logit[:, :]),
                                          first[:].unsqueeze(2).to_broadcast([NB, 2 * S4, NEXP1]),
                                          ALU.is_equal).then_inc(onehot_ready, 1)
                    if exists(m, NT):
                        relu(range(1, 3))
                    if exists(i, NT):
                        dve.wait_ge(high_ready, 2 * i + 2)
                        split_low(dve, xs[:, 1 - k], xn[:, 1 - k, :], low_ready)
                    if exists(m, NT):
                        relu(range(3, FCH))
                    if exists(n, NT):
                        dve.wait_ge(L.rstd_ready, n + 1)
                        at_least(dve, logit_made, n - 1)
                        dve.tensor_tensor(xn[:, k, :], L.centered[:, :], L.rstd[:, :],
                                          ALU.mult).then_inc(L.norm_done, 1)
                    if exists(m, NT):
                        dve.wait_ge(down_made, m + 1)
                        at_least(dve, fin_made, m - 1)
                        dve.scalar_tensor_tensor(out=fin[:, k, :].rearrange("p (j b) -> p j b", b=NB),
                                                 in0=po[:, :].rearrange("p (j b) -> p j b", b=NB), scalar=0.0,
                                                 in1=stream[:, ds(m * S4, S4), :], op0=ALU.max,
                                                 op1=ALU.add).then_inc(fin_ready, 1)
                    if exists(i, NT):
                        dve.wait_ge(choice_made, i + 1)
                        at_least(dve, down_made, i - 1)
                        dve.tensor_copy(choice[0:PE2, 1 - k, :], pch[0:PE2, 0:PCOLS]).then_inc(choice_ready, 1)
                run_steps(dve, NT, 2, step)

class Shared:
    pass


def build(nc, D, out):
    with ExitStack() as ctx:
        sb = lambda n, s, d=F32: ctx.enter_context(nc.sbuf_tensor(n, s, d))
        G = Shared()
        G.dram, G.ctx = D, ctx
        G.ident, G.center_m, G.mean_m = sb("ident", [128, 128]), sb("center_m", [128, 128]), sb("mean_m", [128, 128])
        G.center_r = sb("center_r", [128, 128], F32R)
        G.flip = sb("flip", [NJ, NJ])
        G.vec = sb("vec", [128, 16])
        G.d1h, G.d1l = (sb(f"d1_{i}", [128, LAYERS, DFF], F32R) for i in ("high", "low"))
        G.center_s = sb("center_s", [128, 2, 128], F32R)
        G.gelu_b = sb("gelu_b", [128, LAYERS, 2])
        G.d2c = sb("d2c", [128, LAYERS, 2, HID])
        G.d2bc = sb("d2bc", [128, LAYERS])
        G.lag_dram = nc.dram_tensor("lag_kernels", (LAYERS, HID, NLAG), F32).ap()
        region = sb("region", [128, PC * NB])
        G.bp = region[0:NJ, :].rearrange("p (f b) -> p f b", b=NB)
        G.t_flat = region[:, 0:NB * NJ]
        G.t = G.t_flat.rearrange("p (b j) -> p b j", j=NJ)
        with ExitStack() as early:
            y = early.enter_context(nc.sbuf_tensor("conv_out", [NJ, NB * PC], F32))
            G.y_flat = y[:, :]
            G.y = G.y_flat.rearrange("p (b f) -> p b f", f=PC)
            phase_embed(nc, G)
            for layer in range(LAYERS):
                phase_conv(nc, G, layer)
                phase_ffn(nc, G, layer)
        G.expert_w = sb("expert_w", [128, 2, NEXP0 + 1, SLOT])
        G.expert_of = sb("expert_of", [1, NGROUP], I32)
        phase_attention(nc, G)
        phase_routed(nc, G)
        phase_ssm(nc, G)
        phase_experts(nc, G, out)


def lay_out_attention(A, f):
    import numpy as np
    w1 = np.zeros((128, 128), np.float32)
    w1[0:HID, 0:HID], w1[0:HID, HID:128] = f("L0_attn_kw1").T, f("L0_attn_qw1").T
    w2 = np.zeros((128, 128), np.float32)
    vec = np.zeros((128, 8), np.float32)
    vec[:, 0] = np.concatenate([f("L0_attn_kb1"), f("L0_attn_qb1")])
    for side, (w, b) in enumerate((("L0_attn_kw2", "L0_attn_kb2"), ("L0_attn_qw2", "L0_attn_qb2"))):
        for part in range(2):
            cols = slice(side * HID + part * 32, side * HID + part * 32 + 32)
            w2[side * HID:(side + 1) * HID, cols] = f(w).T
            vec[cols, 1] = f(b)
            vec[cols, 2] = (-1.0, 1.0)[part]
            vec[cols, 3] = (-3.1415925, 3.1415925)[part]
            vec[cols, 4] = (PI / 2, 0.0)[part]
    A["a_w1"], A["a_w2"], A["a_vec"] = w1, w2, vec
    vw = np.zeros((128, HID), np.float32)
    vw[0:HID] = f("L0_attn_vw").T
    A["a_vw"] = vw
    A["a_vb"] = np.tile(f("L0_attn_vb"), (NJ, 1))
    key, query = np.arange(NJ)[:, None], np.arange(SEQ)[None, :]
    scale = 1.0 / np.sqrt((query + 1.0) * 32)
    both = [(key <= query) * scale, ((key + NJ <= query) * scale)[:, NJ:]]
    A["a_mask"] = np.concatenate(both, axis=1).astype(np.float32)


def lay_out_routed(A, f):
    import numpy as np
    w = np.zeros((128, 2, NEXP0 + 1, SLOT), np.float32)
    w[:, :, 0:NEXP0, 0:LH] = f("L0_ffn_Wr").transpose(3, 0, 1, 2)
    w[:, :, 0:NEXP0, LH] = f("L0_ffn_br").transpose(2, 0, 1)
    base = np.zeros((128, 2, SLOT), np.float32)
    base[:, :, 0:LH] = f("L0_ffn_Ws")[:, 0].transpose(2, 0, 1)
    base[:, :, LH] = f("L0_ffn_bs")[:, 0].T
    A["r_w"], A["r_base"] = w, base
    A["route"] = f("L0_ffn_route_id").reshape(1, NGROUP)
    A["r_wi"] = np.tile(f("L0_ffn_Wi").T, (2, 1))
    A["r_wo"] = np.ascontiguousarray(f("L0_ffn_Wo").T)
    bo = f("L0_ffn_bo")
    A["r_vec"] = np.stack([f("L0_ffn_bi"), np.concatenate([bo, bo])], axis=1)


def lay_out_ssm(A, f):
    import numpy as np
    rows = [f("L1_attn_Lambda_re"), f("L1_attn_Lambda_im"), f("L1_attn_log_step")]
    lam = np.zeros((128, 3, HID + 1), np.float32)
    for i, v in enumerate(rows):
        lam[:, i, 0:HID] = v[None, :]
        lam[:, i, HID] = np.concatenate([v, v])
    A["s_lam"] = lam
    b = f("L1_attn_B_ri").transpose(1, 2, 0)
    A["s_bt"] = np.concatenate([b, b], axis=0)
    A["s_crt"] = np.concatenate([f("L1_attn_C_re").T, f("L1_attn_C_im").T], axis=0)
    d = f("L1_attn_D")
    sign = np.repeat(np.array([1.0, -1.0], np.float32), HID)
    A["s_col"] = np.stack([np.concatenate([d, d]), sign], axis=1)
    A["s_shift"] = np.roll(np.eye(128, dtype=np.float32), HID, axis=1)


def lay_out_experts(A, f):
    import numpy as np
    PE2 = 2 * NEXP1
    rw = np.zeros((128, PE2), np.float32)
    b2, mask = np.zeros((128, 128), np.float32), np.zeros((128, 2, FCH * 128), np.float32)
    for par in range(2):
        rows, experts = slice(par * HID, (par + 1) * HID), slice(par * NEXP1, (par + 1) * NEXP1)
        rw[rows, experts] = f("L1_ffn_router_w").T
        b2[experts, rows] = f("L1_ffn_b2")
        mask[experts, par] = np.kron(np.eye(NEXP1), np.ones((1, EH))) * BIG
        mask[PE2, par] = -BIG
    A["x_rw"], A["x_b2"] = rw, b2
    A["x_w1"] = np.tile(f("L1_ffn_W1").transpose(1, 0, 2).reshape(HID, FCH * 128), (2, 1))
    A["x_mask"] = mask.reshape(128, 2, FCH, 128)
    A["x_rb"] = np.tile(f("L1_ffn_router_b"), (NB, 2))
    A["x_tie"] = np.tile((NEXP1 - np.arange(NEXP1)).astype(np.float32), (NB, 2 * PAIR_TILE))
    A["x_b1"] = np.ascontiguousarray(f("L1_ffn_b1").reshape(FCH, 128).T)
    A["x_w2"] = np.ascontiguousarray(f("L1_ffn_W2").reshape(FCH, 128, HID).transpose(1, 0, 2))


def lay_out(inputs):
    import numpy as np
    f = lambda n: np.asarray(inputs[n])
    dup = lambda v: np.concatenate([v, v], axis=0)
    A = {}
    A["ids"] = f("x")
    A["item_emb"] = f("L0_tok_item_emb")
    A["pos"] = np.ascontiguousarray(f("L0_tok_pos_emb").reshape(NJ, PC).T)
    A["ident"] = np.eye(128, dtype=np.float32)
    A["flip"] = np.ascontiguousarray(np.eye(NJ, dtype=np.float32)[::-1])
    half = np.eye(HID) - 1.0 / HID
    A["center_m"] = np.kron(np.eye(2), half).astype(np.float32)
    A["mean_m"] = np.kron(np.eye(2), np.full((HID, HID), 1.0 / HID)).astype(np.float32)
    vec = np.zeros((128, 16), np.float32)
    cols = [f("L0_tok_ln0_w"), f("L0_tok_ln0_b"), *f("L0_tok_fln_w"), *f("L0_tok_fln_b"),
            *f("L0_tok_iln_w"), *f("L0_tok_iln_b")]
    for i, v in enumerate(cols):
        vec[:, i] = dup(v)
    A["vec"] = vec
    A["cw"] = np.ascontiguousarray(f("L0_tok_cw").transpose(1, 0, 3, 2))
    freq = np.arange(SEQ // 2 + 1)[:, None]
    lags = (SEQ - 1) - np.arange(NLAG)[None, :]
    weight = np.where((freq == 0) | (freq == SEQ // 2), 1.0, 2.0) / SEQ
    angle = 2 * np.pi * ((freq * lags) % SEQ) / SEQ
    A["dft"] = np.stack([weight * np.cos(angle), -weight * np.sin(angle)], axis=1).astype(np.float32)
    A["d2t"] = np.ascontiguousarray(f("L0_tok_d2_w").transpose(2, 0, 1))
    A["d2b"] = dup(np.ascontiguousarray(f("L0_tok_d2_b").T))
    A["d1"] = np.ascontiguousarray(dup(f("L0_tok_d1_w").transpose(1, 0, 2)))
    center_s = np.zeros((128, 2, 128), np.float32)
    for par in range(2):
        center_s[:, par, par * HID:(par + 1) * HID] = dup(half)
    A["center_s"] = center_s
    A["gelu_b"] = np.ascontiguousarray(f("L0_tok_d1_b").reshape(LAYERS, 2, 128).transpose(2, 0, 1))
    lay_out_attention(A, f)
    lay_out_routed(A, f)
    lay_out_ssm(A, f)
    lay_out_experts(A, f)
    return A


def kernel(**inputs):
    import numpy as _np
    import concourse.bacc as _bacc
    from concourse import mybir as _mybir
    from concourse.bass_utils import run_bass_kernel_spmd as _run

    nc = _bacc.Bacc("TRN2", target_bir_lowering=False, num_devices=1)
    arrays, D = {}, {}
    for name, a in lay_out(inputs).items():
        a = _np.ascontiguousarray(a)
        arrays[f"in_{name}_dram"] = a
        D[name] = nc.dram_tensor(f"in_{name}_dram", a.shape, _mybir.dt.from_np(a.dtype), kind="ExternalInput").ap()
    out = nc.dram_tensor("out_0_dram", (NB, SEQ, HID), F32, kind="ExternalOutput").ap()
    build(nc, D, out)
    r = _run(nc, [arrays], core_ids=[0])
    return r.results[0]["out_0_dram"]
```

```python
from contextlib import ExitStack

import concourse.bass as bass
from concourse import mybir

F32 = mybir.dt.float32
BF16 = mybir.dt.bfloat16
F32R = mybir.dt.float32r
I32 = mybir.dt.int32
ACT = mybir.ActivationFunctionType
ALU = mybir.AluOpType
AX_X = mybir.AxisListType.X

NB, SEQ, HID = 128, 200, 64
NJ = SEQ // 2
PC = 2 * HID
DFF, LAYERS = 256, 2
SEQ_TILE = 4
COLS = SEQ_TILE * NJ
SEQ_TILES = NB // SEQ_TILE
PAIR_TILE = 4
PCOLS = PAIR_TILE * NB
PAIR_TILES = NJ // PAIR_TILE
NLAG = 2 * SEQ
PHASES = 32
LH = 128
NEXP0, NGROUP = 16, 64
GCOLS = 2 * NJ
NEXP1, EH = 32, 16
FCH = NEXP1 * EH // 128
SLOT = LH + 1
PI = 3.141592653589793
BIG = 2.0 ** 100


def at_least(eng, sem, value):
    if isinstance(value, int) and value <= 0:
        return
    eng.wait_ge(sem, value)


def run_steps(eng, tiles, skew, step):
    first = skew + 2 + skew % 2
    turns = (tiles - first) // 2
    for t in range(first):
        step(t, t % 2)
    with eng.Fori(0, turns) as i:
        for u in range(2):
            step(2 * i + (first + u), u)
    for t in range(first + 2 * turns, tiles + skew):
        step(t, t % 2)


def half(t, parity):
    return (t - parity) // 2


def exists(n, tiles):
    return not isinstance(n, int) or 0 <= n < tiles


def ds(start, size):
    return bass.ds(start, size)


def clear_all(nc, sems):
    with nc.Block() as block:
        @block.sync
        def _(sp):
            for s in sems:
                sp.sem_clear(s)




def split_high(eng, split, x, done):
    for par, rows in ((0, slice(0, HID)), (1, slice(HID, 128))):
        eng.tensor_copy(split[rows, par, :], x[rows, :]).then_inc(done, 1)


def split_low(eng, split, x, done):
    for par, rows, other in ((0, slice(0, HID), slice(HID, 128)), (1, slice(HID, 128), slice(0, HID))):
        eng.tensor_tensor(split[other, par, :], x[rows, :], split[rows, par, :], ALU.subtract).then_inc(done, 1)


class Norm:

    def __init__(self, ctx, nc, sem, tag, cols, eps, parts=1, banks=1, slots=1):
        self.eps, self.cols, self.parts, self.banks = eps, cols, parts, banks
        self.centered_banks = [ctx.enter_context(nc.psum_tensor(f"{tag}_centered{i}", [128, 512], F32))
                               for i in range(banks)]
        self.centered = self.centered_banks[0]
        self.variance = ctx.enter_context(nc.psum_tensor(f"{tag}_variance", [128, 512], F32))
        sb = lambda n, i: ctx.enter_context(nc.sbuf_tensor(f"{tag}_{n}{i}", [128, cols], F32))
        self.slots = slots
        self.squares, self.rstds = [sb("square", i) for i in range(slots)], [sb("rstd", i) for i in range(slots)]
        self.square, self.rstd = self.squares[0], self.rstds[0]
        self.logvar = sb("logvar", "")
        self.centered_ready, self.square_ready = sem("n_centered_ready"), sem("n_square_ready")
        self.variance_ready, self.log_ready = sem("n_variance_ready"), sem("n_log_ready")
        self.rstd_ready, self.norm_done = sem("n_rstd_ready"), sem("n_norm_done")


def pe_variance(pe, G, L, n, slot=0):
    at_least(pe, L.square_ready, n + 1)
    at_least(pe, L.log_ready, n)
    pe.matmul(L.variance[:, 0:L.cols], G.mean_m[:], L.squares[slot][:, :], start=True,
              stop=True).then_inc(L.variance_ready, 1)


def act_square(act, L, n, bias=0.0, bank=0):
    at_least(act, L.centered_ready, n + 1)
    at_least(act, L.variance_ready, n)
    act.activation(L.square[:, :], L.centered_banks[bank][:, 0:L.cols], ACT.Square,
                   bias=bias).then_inc(L.square_ready, 1)


def act_log(act, L, n, slot=0):
    at_least(act, L.variance_ready, n + 1)
    at_least(act, L.rstd_ready, n)
    act.activation(L.logvar[:, :], L.variance[:, 0:L.cols], ACT.Ln,
                   bias=L.eps).then_inc(L.log_ready, 1)


def act_exp(act, L, n, slot=0):
    at_least(act, L.log_ready, n + 1)
    at_least(act, L.norm_done, L.parts * (n + 1 - L.slots))
    act.activation(L.rstds[slot][:, :], L.logvar[:, :], ACT.Exp, scale=-0.5).then_inc(L.rstd_ready, 1)


def act_rstd(act, L, n, slot=0):
    act_log(act, L, n, slot)
    act_exp(act, L, n, slot)



class StreamParts:
    def __init__(self, ctx, nc, sem, tag, cols):
        self.cols = cols
        self.parts = ctx.enter_context(nc.sbuf_tensor(f"{tag}_stream_parts", [128, 2, 2, cols], F32R))
        self.begun, self.high_ready, self.low_ready = sem("t_begun"), sem("t_high_ready"), sem("t_low_ready")


def pool_split_stream(pool, S, L, n, k, tile, inner):
    group = lambda a: a.rearrange("p (o i) -> p o i", i=inner)
    at_least(pool, L.centered_ready, n - 1)
    pool.sem_inc(S.begun, 1)
    pool.tensor_copy(group(S.parts[:, k, 0, :]), tile).then_inc(S.high_ready, 1)
    pool.wait_ge(S.high_ready, n + 1)
    pool.sem_inc(S.begun, 1)
    pool.tensor_tensor(group(S.parts[:, k, 1, :]), tile, group(S.parts[:, k, 0, :]),
                       ALU.subtract).then_inc(S.low_ready, 1)


def pe_center(pe, G, S, L, n, k):
    bank = k if L.banks == 2 else 0
    pe.wait_ge(S.low_ready, n + 1)
    at_least(pe, L.norm_done, L.parts * (n + 1 - L.banks))
    for part in range(2):
        mm = pe.matmul(L.centered_banks[bank][:, 0:S.cols], G.center_r[:], S.parts[:, k, part, :], start=(part == 0),
                       stop=(part == 1))
    mm.then_inc(L.centered_ready, 1)



def ssm_matrices(nc, ctx, G, pp):
    D = G.dram
    P1 = HID + 1
    sb = lambda n, s, d=F32: ctx.enter_context(nc.sbuf_tensor("m_" + n, s, d))
    sem = lambda n: G.ctx.enter_context(nc.semaphore("m_" + n))
    lam = sb("lam", [128, 3, P1])
    bt, crt, col = sb("bt", [128, 2, HID]), sb("crt", [128, HID]), sb("col", [128, 2])
    shift = sb("shift", [128, 128])
    T = sb("prep", [128, 20, P1])
    qi = sb("qi", [128, P1], I32)
    wu, a1 = sb("wu", [128, 128]), sb("a1", [128, 128])
    bb = sb("bb", [128, 128])
    wut, a2t, gt, kt = G.ssm
    loads, chain, exp_done, sin_done = sem("loads"), sem("chain"), sem("exp_done"), sem("sin_done")
    delta_ready, angle_ready, part_ready, prep_made = sem("delta_ready"), sem("angle_ready"), sem("part_ready"), sem("prep_made")
    weights = [(lam, D["s_lam"]), (bt, D["s_bt"]), (crt, D["s_crt"]), (col, D["s_col"]), (shift, D["s_shift"])]
    (MAG, ANG, RED, SIN, ABSA, COS, ARE, AIM, T0, T1, A2R, A2I, NRE, FRE, FIM, BRE, BIM, CRE, CIM, DEL) = range(20)
    c = lambda i: T[:, i, :]
    h = lambda i: T[:, i, 0:HID]
    own = lambda i: T[:, i, HID:P1]
    lre, lim = lam[:, 0, :], lam[:, 1, :]

    def on_scalar(act):
        act.wait_ge(loads, 16 * len(weights))
        act.activation(c(DEL), lam[:, 2, :], ACT.Exp).then_inc(exp_done, 1)
        act.wait_ge(delta_ready, 1)
        act.activation(c(MAG), c(T0), ACT.Exp).then_inc(exp_done, 1)
        act.wait_ge(angle_ready, 1)
        act.activation(c(SIN), c(RED), ACT.Sin).then_inc(sin_done, 1)
        act.activation(c(COS), c(ABSA), ACT.Sin, bias=PI / 2, scale=-1.0).then_inc(sin_done, 1)

    def on_tensor(pe):
        pe.wait_ge(part_ready, 1)
        pe.transpose(pp[0][:, 0:128], wut[:], G.ident[:])
        pe.matmul(pp[1][:, 0:HID], a1[:], crt[:], start=True, stop=True).then_inc(prep_made, 1)
        pe.wait_ge(part_ready, 2)
        pe.matmul(pp[2][:, 0:HID], bb[:], crt[:], start=True, stop=True)
        pe.matmul(pp[2][0:HID, HID:128], wu[:, 0:HID], crt[:], start=True, stop=True,
                  skip_group_check=True)
        pe.matmul(pp[1][:, HID:128], a1[:], gt[:, 0:HID], start=True, stop=True,
                  skip_group_check=True).then_inc(prep_made, 1)


    dve = nc.vector
    count = [0]

    def link(*instructions):
        for ins in instructions:
            ins.then_inc(chain, 1)
        count[0] += len(instructions)
        dve.wait_ge(chain, count[0])

    def mul(*products):
        link(*[dve.tensor_tensor(o, a, b, ALU.mult) for o, a, b in products])

    def addsub(o, a, b, op):
        link(dve.tensor_tensor(o, a, b, op))

    def cmul(ore, oim, are, aim, bre, bim, t0, t1):
        mul((t0, are, bre), (t1, aim, bim))
        addsub(ore, t0, t1, ALU.subtract)
        mul((t0, are, bim), (t1, aim, bre))
        addsub(oim, t0, t1, ALU.add)

    def angles():
        dve.wait_ge(loads, 16 * len(weights))
        dve.wait_ge(exp_done, 1)
        dve.tensor_tensor(c(T0), lre, c(DEL), ALU.mult).then_inc(delta_ready, 1)
        mul((c(ANG), lim, c(DEL)))
        link(dve.tensor_scalar(qi[:], c(ANG), 1.0 / (2 * PI), None, ALU.mult))
        link(dve.tensor_copy(c(T1), qi[:]))
        link(dve.scalar_tensor_tensor(out=c(RED), in0=c(T1), scalar=-6.28125, in1=c(ANG), op0=ALU.mult, op1=ALU.add))
        link(dve.scalar_tensor_tensor(out=c(RED), in0=c(T1), scalar=-(2 * PI - 6.28125), in1=c(RED), op0=ALU.mult, op1=ALU.add))
        for op, turn in ((ALU.is_gt, -2 * PI), (ALU.is_lt, 2 * PI)):
            link(dve.tensor_scalar(c(T1), c(RED), PI if turn < 0 else -PI, turn, op, ALU.mult))
            addsub(c(RED), c(RED), c(T1), ALU.add)
        link(dve.tensor_scalar(c(RED), c(RED), 3.1415925, -3.1415925, ALU.min, ALU.max))
        link(dve.scalar_tensor_tensor(out=c(ABSA), in0=c(RED), scalar=-1.0, in1=c(RED), op0=ALU.mult, op1=ALU.max))
        dve.memset(kt[:], 0.0)
        dve.tensor_scalar(crt[HID:128, :], crt[HID:128, :], -1.0, None, ALU.mult).then_inc(angle_ready, 1)

    def factors():
        dve.wait_ge(exp_done, 2)
        dve.wait_ge(sin_done, 2)
        mul((c(ARE), c(MAG), c(COS)), (c(AIM), c(MAG), c(SIN)))
        cmul(c(A2R), c(A2I), c(ARE), c(AIM), c(ARE), c(AIM), c(T0), c(T1))
        dve.tensor_scalar(c(NRE), c(ARE), 1.0, None, ALU.subtract)
        mul((c(T0), lre, lre), (c(T1), lim, lim))
        addsub(c(T0), c(T0), c(T1), ALU.add)
        link(dve.reciprocal(c(DEL), c(T0)))
        mul((c(T0), c(NRE), lre), (c(T1), c(AIM), lim))
        addsub(c(T0), c(T0), c(T1), ALU.add)
        mul((c(FRE), c(T0), c(DEL)))
        mul((c(T0), c(AIM), lre), (c(T1), c(NRE), lim))
        addsub(c(T0), c(T0), c(T1), ALU.subtract)
        mul((c(FIM), c(T0), c(DEL)))

    def inputs():
        cmul(h(BRE), h(BIM), h(FRE), h(FIM), bt[:, 0, :], bt[:, 1, :], h(T0), h(T1))
        cmul(h(CRE), h(CIM), h(ARE), h(AIM), h(BRE), h(BIM), h(T0), h(T1))
        for half_rows, re, im in ((slice(0, HID), CRE, CIM), (slice(HID, 128), BRE, BIM)):
            dve.tensor_copy(wut[half_rows, 0:HID], T[half_rows, re, 0:HID])
            dve.tensor_copy(wut[half_rows, HID:128], T[half_rows, im, 0:HID])
        sign = col[:, 1:2]
        mul((own(T0), own(A2I), sign), (own(T1), own(AIM), sign))
        link(dve.tensor_scalar(own(T1), own(T1), -1.0, None, ALU.mult))

    def outputs():
        link(dve.tensor_scalar(a2t[:], G.ident[:], own(A2R), None, ALU.mult),
             dve.tensor_scalar(a1[:], G.ident[:], own(ARE), None, ALU.mult))
        dve.scalar_tensor_tensor(out=a2t[:], in0=shift[:], scalar=own(T0), in1=a2t[:], op0=ALU.mult, op1=ALU.add)
        dve.scalar_tensor_tensor(out=a1[:], in0=shift[:], scalar=own(T1), in1=a1[:], op0=ALU.mult,
                                 op1=ALU.add).then_inc(part_ready, 1)
        dve.wait_ge(prep_made, 1)
        dve.tensor_copy(wu[:], pp[0][:, 0:128])
        dve.tensor_copy(bb[:, 0:HID], pp[0][:, HID:128])
        dve.tensor_copy(bb[:, HID:128], pp[0][:, HID:128])
        dve.tensor_copy(gt[:, 0:HID], pp[1][:, 0:HID]).then_inc(part_ready, 1)
        dve.wait_ge(prep_made, 2)
        dve.tensor_copy(gt[:, HID:128], pp[1][:, HID:128])
        link(dve.tensor_copy(kt[0:HID, 0:HID], pp[2][0:HID, 0:HID]),
             dve.tensor_copy(kt[0:HID, HID:128], pp[2][0:HID, HID:128]),
             dve.tensor_copy(kt[HID:128, HID:128], pp[2][HID:128, 0:HID]))
        dve.scalar_tensor_tensor(out=kt[:], in0=G.ident[:], scalar=col[:, 0:1], in1=kt[:], op0=ALU.mult,
                                 op1=ALU.add)

    return weights, loads, on_scalar, on_tensor, (angles, factors, inputs, outputs)



def phase_embed(nc, G):
    D, NT = G.dram, PAIR_TILES
    TILE_TOKENS = 2 * PAIR_TILE
    CHUNK = 8
    with ExitStack() as ctx:
        sb = lambda n, s, d=F32: ctx.enter_context(nc.sbuf_tensor(n, s, d))
        pt = lambda n: ctx.enter_context(nc.psum_tensor(n, [128, 512], F32))
        sem = lambda n: G.ctx.enter_context(nc.semaphore("e_" + n))
        L = Norm(ctx, nc, sem, "e", PCOLS, 1e-12)
        ids = sb("e_ids", [NB, SEQ], I32)
        ids_tile = sb("e_ids_tile", [NB, 2, TILE_TOKENS], I32)
        rows = sb("e_rows", [NB, 2, TILE_TOKENS * HID])
        z = sb("e_z", [128, PCOLS])
        y = sb("e_y", [128, PCOLS])
        x0 = sb("e_x0", [128, 2, PCOLS])
        tokens_dram = nc.dram_tensor("tokens", (NJ, PC, NB), F32).ap()
        pos = sb("e_pos", [128, NJ])
        cw = sb("e_cw", [101, LAYERS, 2, HID])
        dft = sb("e_dft", [101, 2, NLAG])
        lag = sb("e_lag", [HID, LAYERS, NLAG])
        d2t = sb("e_d2t", [HID, LAYERS, DFF])
        d2b = sb("e_d2b", [128, LAYERS])
        d1, center_f = sb("e_d1", [128, LAYERS, DFF]), sb("e_center_f", [128, 2, 128])
        pz, pk0, pk1 = pt("e_pz"), pt("e_pk0"), pt("e_pk1")
        pk = [pk0, pk1]
        ids_here, loads = sem("ids_here"), sem("loads")
        ids_copied, tile_begun = sem("ids_copied"), sem("tile_begun")
        rows_here = [sem("rows_here0"), sem("rows_here1")]
        z_turned, z_ready, x0_ready = sem("z_turned"), sem("z_ready"), sem("x0_ready")
        stored, bp_here = [sem("stored0"), sem("stored1")], sem("bp_here")
        lag_copied, d1_high = sem("lag_copied"), sem("d1_high")
        prep_made, prep_copied, prep_out = sem("prep_made"), sem("prep_copied"), sem("prep_out")
        pairs = [(ids, D["ids"])]
        weights = [(G.ident, D["ident"]), (G.flip, D["flip"]), (G.center_m, D["center_m"]), (G.mean_m, D["mean_m"]),
                   (pos, D["pos"]), (G.vec, D["vec"]), (cw, D["cw"]), (dft, D["dft"]),
                   (d2t, D["d2t"]), (d2b, D["d2b"]), (d1, D["d1"]), (center_f, D["center_s"]), (G.gelu_b, D["gelu_b"])]

        ssm_banks = [pt(f"e_ssm{i}") for i in range(3)]
        ssm_weights, ssm_loads, ssm_on_scalar, ssm_on_tensor, ssm_on_vector = ssm_matrices(nc, ctx, G, ssm_banks)

        with nc.Block() as block:
            @block.sync
            def _(sp):
                for dst, src in pairs:
                    sp.dma_start(dst[:], src).then_inc(ids_here, 16)
                for dst, src in weights:
                    sp.dma_start(dst[:], src).then_inc(loads, 16)
                for dst, src in ssm_weights:
                    sp.dma_start(dst[:], src).then_inc(ssm_loads, 16)
                for dst, src in G.attention_weights:
                    sp.dma_start(dst[:], src).then_inc(G.attention_loads, 16)
                sp.wait_ge(prep_copied, 2)
                for l in range(LAYERS):
                    sp.dma_start(G.lag_dram[l], lag[:, l, :]).then_inc(prep_out, 16)

                def step(t, k):
                    sp.wait_ge(x0_ready, t + 1)
                    sp.dma_start(tokens_dram[ds(t * PAIR_TILE, PAIR_TILE)].rearrange("j f b -> f j b"),
                                 x0[:, k, :].rearrange("f (j b) -> f j b", b=NB)).then_inc(stored[k], 16)

                def fetch(first, tiles):
                    for k in range(2):
                        sp.wait_ge(stored[k], 16 * ((first + tiles + 1 - k) // 2))
                    rows = slice(first * PAIR_TILE, (first + tiles) * PAIR_TILE)
                    sp.dma_start(G.bp[rows], tokens_dram[rows]).then_inc(bp_here, 16)
                for c in range(NT // CHUNK):
                    with sp.Fori(0, CHUNK // 2) as i:
                        for u in range(2):
                            step(2 * i + (c * CHUNK + u), u)
                    fetch(c * CHUNK, CHUNK)
                for t in range(NT - NT % CHUNK, NT):
                    step(t, t % 2)
                fetch(NT - NT % CHUNK, NT % CHUNK)
                sp.wait_ge(bp_here, 16 * (NT // CHUNK + 1))
                sp.wait_ge(prep_out, 16 * LAYERS)

            @block.gpsimd
            def _(pool):
                pool.wait_ge(ids_here, 16)

                def step(t, k):
                    at_least(pool, z_turned, t - 1)
                    pool.tensor_copy(ids_tile[:, k, :],
                                     ids[:, ds(t * TILE_TOKENS, TILE_TOKENS)]).then_inc(ids_copied, 1)
                    pool.wait_ge(ids_copied, t + 1)
                    pool.sem_inc(tile_begun, 1)
                    for q in range(TILE_TOKENS):
                        pool.indirect_dma_start(
                            rows[:, k, q * HID:(q + 1) * HID], None, D["item_emb"],
                            bass.IndirectOffsetOnAxis(ap=ids_tile[:, k, q:q + 1], axis=0)
                        ).then_inc(rows_here[k], 16)
                run_steps(pool, NT, 0, step)

            @block.tensor
            def _(pe):
                pe.wait_ge(loads, 16 * len(weights))
                for l in range(LAYERS):
                    for c in range(2):
                        mm = pe.matmul(pk[l][0:HID, 0:NLAG], cw[:, l, c, :], dft[:, c, :],
                                       start=(c == 0), stop=(c == 1))
                    mm.then_inc(prep_made, 1)
                pe.wait_ge(prep_copied, 2)
                for l in range(LAYERS):
                    for ck in range(2):
                        mm = pe.matmul(pk0[:, (2 * l + ck) * HID:(2 * l + ck + 1) * HID],
                                       d2t[:, l, ck * 128:(ck + 1) * 128], G.center_m[0:HID, 0:HID],
                                       start=True, stop=True)
                pe.matmul(pk1[:, 0:LAYERS], G.center_m[:], d2b[:, :], start=True,
                          stop=True).then_inc(prep_made, 1)

                def step(t, k):
                    m = t - 1
                    if exists(t, NT):
                        pe.wait_ge(rows_here[k], 16 * TILE_TOKENS * (half(t, k) + 1))
                        at_least(pe, z_ready, t)
                        for q in range(PAIR_TILE):
                            mm = pe.transpose(pz[:, q * NB:(q + 1) * NB], rows[:, k, q * PC:(q + 1) * PC],
                                              G.ident[:])
                        mm.then_inc(z_turned, 1)
                    if exists(m, NT):
                        pe.wait_ge(z_ready, m + 1)
                        at_least(pe, L.norm_done, m)
                        pe.matmul(L.centered[:, :], G.center_m[:], z[:, :], start=True,
                                  stop=True).then_inc(L.centered_ready, 1)
                        pe_variance(pe, G, L, m)
                run_steps(pe, NT, 1, step)
                ssm_on_tensor(pe)

            @block.scalar
            def _(act):
                ssm_on_scalar(act)
                act.preload_act_table_set("natural_log_exp_and_others")
                act.wait_ge(loads, 16 * len(weights))

                def step(t, k):
                    act_square(act, L, t)
                    act_rstd(act, L, t)
                    at_least(act, L.norm_done, t + 1)
                    at_least(act, stored[k], 16 * half(t, k))
                    act.activation(x0[:, k, :], y[:, :], ACT.Identity, bias=G.vec[:, 1:2],
                                   scale=G.vec[:, 0:1]).then_inc(x0_ready, 1)
                run_steps(act, NT, 0, step)

            @block.vector
            def _(dve):
                for l in range(LAYERS):
                    dve.wait_ge(prep_made, l + 1)
                    dve.tensor_copy(lag[:, l, :], pk[l][0:HID, 0:NLAG]).then_inc(lag_copied, 1)
                    dve.wait_ge(lag_copied, l + 1)
                    dve.tensor_scalar(lag[:, l, SEQ - 1:SEQ], pk[l][0:HID, SEQ - 1:SEQ], 1.0, None,
                                      ALU.add).then_inc(prep_copied, 1)
                dve.wait_ge(prep_made, 3)
                dve.tensor_copy(G.d2c[:], pk0[:, 0:4 * HID].rearrange("p (l c h) -> p l c h", l=2, c=2))
                dve.tensor_copy(G.d2bc[:], pk1[:, 0:LAYERS])
                dve.tensor_copy(G.center_s[:], center_f[:])
                dve.tensor_copy(G.center_r[:], G.center_m[:])
                dve.tensor_copy(G.d1h[:], d1[:]).then_inc(d1_high, 1)
                dve.wait_ge(d1_high, 1)
                dve.tensor_tensor(G.d1l[:], d1[:], G.d1h[:], ALU.subtract)

                def step(t, k):
                    m = t - 1
                    if exists(t, NT):
                        dve.wait_ge(z_turned, t + 1)
                        at_least(dve, L.centered_ready, t)
                        dve.tensor_tensor(z[:].rearrange("p (j b) -> p j b", b=NB),
                                          pz[:, :].rearrange("p (j b) -> p j b", b=NB),
                                          pos[:, ds(t * PAIR_TILE, PAIR_TILE)].unsqueeze(2).to_broadcast([128, PAIR_TILE, NB]),
                                          ALU.add).then_inc(z_ready, 1)
                    if exists(m, NT):
                        dve.wait_ge(L.rstd_ready, m + 1)
                        at_least(dve, x0_ready, m)
                        dve.tensor_tensor(y[:, :], L.centered[:, :], L.rstd[:, :], ALU.mult).then_inc(L.norm_done, 1)
                    if isinstance(t, int) and t < 3:
                        ssm_on_vector[t]()
                run_steps(dve, NT, 1, step)
                ssm_on_vector[3]()



def phase_conv(nc, G, layer):
    with ExitStack() as ctx:
        tag = f"c{layer}_"
        sems = []

        def sem(name):
            sems.append(ctx.enter_context(nc.semaphore(tag + name)))
            return sems[-1]
        CH = 4
        toep = ctx.enter_context(nc.sbuf_tensor(tag + "toep", [NJ, 2, CH, SEQ + 1], F32))
        po = [[ctx.enter_context(nc.psum_tensor(f"{tag}po{k}{i}", [128, 512], F32)) for i in range(2)] for k in range(2)]
        toep_here = [sem("toep_here0"), sem("toep_here1")]
        conv_made, po_out = [sem("conv_made0"), sem("conv_made1")], [sem("po_out0"), sem("po_out1")]
        steps = HID // CH

        with nc.Block() as block:
            @block.sync
            def _(sp):
                def step(t, k):
                    at_least(sp, conv_made[1], t - 1)
                    src = bass.AP(G.lag_dram.tensor, G.lag_dram[layer].offset + t * (CH * NLAG),
                                  [[2, NJ], [NLAG, CH], [1, SEQ + 1]])
                    sp.dma_start(toep[:, k, :, :], src).then_inc(toep_here[k], 16)
                run_steps(sp, steps, 0, step)

            @block.tensor
            def _(pe):
                def step(t, k):
                    pe.wait_ge(toep_here[k], 16 * half(t, k) + 16)
                    for bank in range(2):
                        at_least(pe, po_out[bank], t - 1)
                        for ch in range(2):
                            for po_par in range(2):
                                for in_par in range(2):
                                    a = 1 - po_par + in_par
                                    row = CH * t + (in_par * HID + 2 * bank + ch)
                                    mm = pe.matmul(
                                        po[k][bank][0:NJ, (2 * po_par + ch) * NB:(2 * po_par + ch + 1) * NB],
                                        toep[:, k, 2 * bank + ch, a:a + SEQ - 1:2],
                                        G.bp[:, ds(row, 1), :].rearrange("p f b -> p (f b)"),
                                        start=(in_par == 0), stop=(in_par == 1))
                        mm.then_inc(conv_made[bank], 1)
                run_steps(pe, steps, 0, step)

            def out_ap(t, bank):
                return G.y.rearrange("p b (o c) -> p o c b", o=2)[:, :, ds(CH * t + 2 * bank, 2), :]

            def in_ap(k, bank):
                return po[k][bank][0:NJ, :].rearrange("p (o c b) -> p o c b", o=2, c=2)

            @block.vector
            def _(dve):
                def step(t, k):
                    dve.wait_ge(conv_made[0], t + 1)
                    dve.tensor_copy(out_ap(t, 0), in_ap(k, 0)).then_inc(po_out[0], 1)
                run_steps(dve, steps, 0, step)

            @block.scalar
            def _(act):
                def step(t, k):
                    act.wait_ge(conv_made[1], t + 1)
                    act.activation(out_ap(t, 1), in_ap(k, 1), ACT.Identity).then_inc(po_out[1], 1)
                run_steps(act, steps, 0, step)
        clear_all(nc, sems)



def phase_ffn(nc, G, layer):
    last = layer == LAYERS - 1
    NT = SEQ_TILES
    with ExitStack() as ctx:
        tag = f"f{layer}_"
        sb = lambda n, s, d=F32: ctx.enter_context(nc.sbuf_tensor(tag + n, s, d))
        pt = lambda n: ctx.enter_context(nc.psum_tensor(tag + n, [128, 512], F32))
        sems = []

        def sem(name):
            sems.append(ctx.enter_context(nc.semaphore(tag + name)))
            return sems[-1]
        L1 = Norm(ctx, nc, lambda n: sem("1" + n), tag + "n1", COLS, 1e-12, slots=2)
        L2 = Norm(ctx, nc, lambda n: sem("2" + n), tag + "n2", COLS, 1e-12, slots=2)
        rows = sb("rows", [NJ, 2, SEQ_TILE * PC])
        z = sb("z", [128, COLS])
        c1, c2 = sb("c1", [128, 2, COLS]), sb("c2", [128, 2, COLS])
        y1, x1 = sb("y1", [128, COLS]), sb("x1", [128, COLS])
        x1s = sb("x1s", [128, 2, 2, COLS], F32R)
        y2 = sb("y2", [128, COLS])
        x2 = sb("x2", [128, 2, COLS])
        g = sb("g", [128, 2, 4, COLS])
        pz, pback = pt("pz"), pt("pback")
        pf = [pt("pf0"), pt("pf1")]
        rows_here = [sem("rows_here0"), sem("rows_here1")]
        z_turned, z_ready, x1_ready = sem("z_turned"), sem("z_ready"), sem("x1_ready")
        up_made, gelu_done, begun = sem("up_made"), sem("gelu_done"), sem("begun")
        high_ready, low_ready, x1s_used = sem("high_ready"), sem("low_ready"), sem("x1s_used")
        c1_ready, c2_ready = sem("c1_ready"), sem("c2_ready")
        x2_ready, back_turned, back_done = sem("x2_ready"), sem("back_turned"), sem("back_done")
        w = lambda i: G.vec[:, i:i + 1]
        fw, fb, iw, ib = w(2 + layer), w(4 + layer), w(6 + layer), w(8 + layer)

        with nc.Block() as block:
            @block.sync
            def _(sp):
                def step(t, k):
                    at_least(sp, z_turned, t - 1)
                    sp.dma_start(rows[:, k, :], G.y_flat[:, ds(t * (SEQ_TILE * PC), SEQ_TILE * PC)]
                                 ).then_inc(rows_here[k], 16)
                run_steps(sp, NT, 0, step)

            @block.tensor
            def _(pe):
                def step(t, k):
                    n, m, u, v = t, t - 3, t - 4, t - 6

                    def up(q):
                        at_least(pe, gelu_done, 4 * m + q - 1)
                        par, ck = q // 2, q % 2
                        for part, w in enumerate((G.d1h, G.d1l)):
                            mm = pe.matmul(pf[q % 2][:, 0:COLS], w[:, layer, ck * 128:(ck + 1) * 128],
                                           x1s[:, 1 - k, par, :], start=(part == 0), stop=(part == 1))
                        mm.then_inc(up_made, 1)

                    def center():
                        if exists(n, NT):
                            pe.wait_ge(z_ready, n + 1)
                            at_least(pe, c1_ready, n)
                            pe.matmul(L1.centered[:, 0:COLS], G.center_m[:], z[:, :], start=True,
                                      stop=True).then_inc(L1.centered_ready, 1)
                    if exists(m, NT):
                        pe.wait_ge(low_ready, 2 * m + 2)
                        up(0)
                        up(1)
                    if exists(n, NT):
                        pe.wait_ge(rows_here[k], 16 * half(n, k) + 16)
                        at_least(pe, z_ready, n)
                        for q in range(SEQ_TILE):
                            mm = pe.transpose(pz[:, q * NJ:(q + 1) * NJ], rows[:, k, q * PC:(q + 1) * PC],
                                              G.flip[:])
                        mm.then_inc(z_turned, 1)
                    if exists(u, NT):
                        at_least(pe, c2_ready, u)
                        for par in range(2):
                            mm = pe.matmul(L2.centered[:, 0:COLS], G.center_s[:, par, :], x1s[:, k, par, :],
                                           start=(par == 0), stop=False, skip_group_check=True)
                        mm.then_inc(x1s_used, 1)
                    if k == 1:
                        if exists(u - 1, NT):
                            pe_variance(pe, G, L2, u - 1, 0)
                        if exists(n - 1, NT):
                            pe_variance(pe, G, L1, n - 1, 0)
                        if exists(m, NT):
                            up(2)
                            up(3)
                        center()
                    if exists(u, NT):
                        pe.wait_ge(gelu_done, 4 * u + 4)
                        for ck in range(2):
                            for par in range(2):
                                mm = pe.matmul(L2.centered[par * HID:(par + 1) * HID, 0:COLS],
                                               G.d2c[:, layer, ck, :], g[:, k, 2 * par + ck, :],
                                               start=False, stop=(ck == 1), skip_group_check=True)
                        mm.then_inc(L2.centered_ready, 1)
                    if k == 0:
                        center()
                        if exists(m, NT):
                            up(2)
                            up(3)
                    if exists(v, NT) and not last:
                        pe.wait_ge(x2_ready, v + 1)
                        at_least(pe, back_done, v)
                        for q in range(SEQ_TILE):
                            mm = pe.transpose(pback[0:NJ, q * PC:(q + 1) * PC],
                                              x2[:, k, q * NJ:(q + 1) * NJ], G.ident[:])
                        mm.then_inc(back_turned, 1)
                    if k == 1:
                        if exists(n, NT):
                            pe_variance(pe, G, L1, n, 1)
                        if exists(u, NT):
                            pe_variance(pe, G, L2, u, 1)
                run_steps(pe, NT, 6, step)

            @block.scalar
            def _(act):
                def step(t, k):
                    n, m, u = t, t - 3, t - 4

                    def gelu(q):
                        act.wait_ge(up_made, 4 * m + q + 1)
                        act.activation(g[:, 1 - k, q, :], pf[q % 2][:, 0:COLS], ACT.Gelu,
                                       bias=G.gelu_b[:, layer, q % 2:q % 2 + 1]).then_inc(gelu_done, 1)
                    if exists(m, NT):
                        at_least(act, L2.centered_ready, m - 1)
                        gelu(0)
                        gelu(1)

                    def rstds(*norms):
                        for part in (act_log, act_exp):
                            for L, tile, slot in norms:
                                if exists(tile, NT):
                                    part(act, L, tile, slot)

                    def square():
                        if exists(u, NT):
                            act.wait_ge(c2_ready, u + 1)
                            at_least(act, L2.variance_ready, u - 1)
                            act.activation(L2.squares[k][:, :], c2[:, k, :], ACT.Square).then_inc(L2.square_ready, 1)
                    if k == 0:
                        square()
                    if exists(m, NT):
                        gelu(2)
                        gelu(3)
                    if k == 1:
                        act.preload_act_table_set("natural_log_exp_and_others")
                        rstds((L2, u - 1, 0), (L1, n - 1, 0))
                        square()
                        rstds((L1, n, 1), (L2, u, 1))
                run_steps(act, NT, 4, step)

            @block.vector
            def _(dve):
                def step(t, k):
                    n, p, u, v, w = t, t - 2, t - 4, t - 6, t - 7
                    if exists(p, NT):
                        dve.wait_ge(L1.rstd_ready, p + 1)
                        at_least(dve, x1_ready, p)
                        dve.tensor_tensor(y1[:, :], c1[:, k, :], L1.rstds[k][:, :], ALU.mult).then_inc(L1.norm_done, 1)
                    if exists(v, NT):
                        dve.wait_ge(L2.rstd_ready, v + 1)
                        at_least(dve, x2_ready, v)
                        dve.tensor_tensor(y2[:, :], c2[:, k, :], L2.rstds[k][:, :], ALU.mult).then_inc(L2.norm_done, 1)
                    if exists(w, NT) and not last:
                        dve.wait_ge(back_turned, w + 1)
                        dve.tensor_copy(G.bp[:, :, ds(w * SEQ_TILE, SEQ_TILE)].rearrange("p f b -> p b f"),
                                        pback[0:NJ, :].rearrange("p (b f) -> p b f", f=PC)
                                        ).then_inc(back_done, 1)
                    if exists(n, NT):
                        dve.wait_ge(z_turned, n + 1)
                        at_least(dve, L1.centered_ready, n)
                        dve.tensor_copy(z[:, :], pz[:, 0:COLS]).then_inc(z_ready, 1)
                    if exists(v, NT) and last:
                        dve.wait_ge(L2.norm_done, v + 1)
                        dve.tensor_scalar(G.t_flat[:, ds(v * COLS, COLS)], y2[:, :], iw, ib, ALU.mult,
                                          ALU.add).then_inc(x2_ready, 1)
                    if exists(p, NT):
                        dve.wait_ge(x1_ready, p + 1)
                        at_least(dve, x1s_used, p - 1)
                        split_high(dve, x1s[:, k], x1, high_ready)
                    if exists(p, NT):
                        dve.wait_ge(high_ready, 2 * p + 2)
                        split_low(dve, x1s[:, k], x1, low_ready)

                    def keep1():
                        if exists(n, NT):
                            dve.wait_ge(L1.centered_ready, n + 1)
                            at_least(dve, L1.norm_done, n - 1)
                            at_least(dve, L1.square_ready, n - 1)
                            dve.tensor_copy(c1[:, k, :], L1.centered[:, 0:COLS]).then_inc(c1_ready, 1)

                    def keep2():
                        if exists(u, NT):
                            dve.wait_ge(L2.centered_ready, u + 1)
                            at_least(dve, L2.norm_done, u - 1)
                            at_least(dve, L2.square_ready, u - 1)
                            dve.tensor_scalar(c2[:, k, :], L2.centered[:, 0:COLS], G.d2bc[:, layer:layer + 1], None,
                                              ALU.add).then_inc(c2_ready, 1)
                    for keep in ((keep2, keep1), (keep1, keep2))[k]:
                        keep()
                run_steps(dve, NT, 6 if last else 7, step)

            @block.gpsimd
            def _(pool):
                def step(t, k):
                    n, p, v = t, t - 2, t - 6
                    if exists(p, NT):
                        pool.wait_ge(L1.norm_done, p + 1)
                        at_least(pool, low_ready, 2 * p)
                        pool.sem_inc(begun, 1)
                        pool.tensor_scalar(x1[:, :], y1[:, :], fw, fb, ALU.mult, ALU.add).then_inc(x1_ready, 1)
                    if exists(v, NT) and not last:
                        pool.wait_ge(L2.norm_done, v + 1)
                        at_least(pool, back_turned, v - 1)
                        pool.sem_inc(begun, 1)
                        pool.tensor_scalar(x2[:, k, :], y2[:, :], iw, ib, ALU.mult, ALU.add).then_inc(x2_ready, 1)
                    if exists(n, NT):
                        pool.wait_ge(c1_ready, n + 1)
                        at_least(pool, L1.variance_ready, n - 1)
                        pool.sem_inc(begun, 1)
                        pool.tensor_tensor(L1.squares[k][:, :], c1[:, k, :], c1[:, k, :],
                                           ALU.mult).then_inc(L1.square_ready, 1)
                run_steps(pool, NT, 6, step)
        clear_all(nc, sems)



def phase_attention(nc, G):
    D, NT = G.dram, SEQ_TILES
    with ExitStack() as ctx:
        sb = lambda n, s, d=F32: ctx.enter_context(nc.sbuf_tensor("a_" + n, s, d))
        pt = lambda n: ctx.enter_context(nc.psum_tensor("a_" + n, [128, 512], F32))
        sem = lambda n: G.ctx.enter_context(nc.semaphore("a_" + n))
        L = Norm(ctx, nc, sem, "a", COLS, 1e-5, parts=2)
        S = StreamParts(ctx, nc, sem, "a", COLS)
        TOK = SEQ_TILE * SEQ
        w1, w2, vw, mask, vb, vec, rt = (tile for tile, _ in G.attention_weights)
        xn = sb("xn", [128, 2, TOK])
        xs = sb("xs", [128, 2, TOK], F32R)
        w1h, w1l = sb("w1h", [128, 128], F32R), sb("w1l", [128, 128], F32R)
        high_ready, low_ready, prepared = sem("high_ready"), sem("low_ready"), sem("prepared")
        hid, phase, folded = sb("hid", [128, TOK]), sb("phase", [128, TOK]), sb("folded", [128, TOK])
        phik, phiq = sb("phik", [128, 2, TOK]), sb("phiq", [128, 2, TOK])
        v = sb("v", [NJ, 2, 2 * SEQ_TILE * HID])
        probs = sb("probs", [NJ, 2, 3 * NJ])
        wbase = sb("wbase", [128, 2, SLOT])
        r1, r2, r3 = (sb(f"r{i}", [1, NGROUP]) for i in range(3))
        pw = [pt("pw0"), pt("pw1")]
        pv, po = pt("pv"), pt("po")
        ps = [pt("ps0"), pt("ps1")]
        loads, cleared, table_ready = sem("loads"), sem("cleared"), sem("table_ready")
        chain = sem("chain")
        proj_made, tanh_done, folded_ready, phi_ready = sem("proj_made"), sem("tanh_done"), sem("folded_ready"), sem("phi_ready")
        v_made, v_ready = sem("v_made"), sem("v_ready")
        score_made, probs_ready, out_made, stream_done = sem("score_made"), sem("probs_ready"), sem("out_made"), sem("stream_done")
        tables = [(G.expert_w, D["r_w"]), (wbase, D["r_base"])]

        with nc.Block() as block:
            @block.sync
            def _(sp):
                for dst, src in tables:
                    sp.dma_start(dst[:], src).then_inc(loads, 16)
                for dst, src in G.routed_weights + G.experts_weights:
                    sp.dma_start(dst[:], src).then_inc(G.later_loads, 16)
                sp.wait_ge(G.later_loads, 16 * len(G.routed_weights + G.experts_weights))

            @block.gpsimd
            def _(pool):
                def step(t, k):
                    pool_split_stream(pool, S, L, t, k, G.t[:, ds(t * SEQ_TILE, SEQ_TILE), :], NJ)
                run_steps(pool, NT, 0, step)
                pool.wait_ge(loads, 16 * len(tables))
                for l in range(2):
                    pool.tensor_tensor(wbase[:, l, 0:LH], wbase[:, l, 0:LH], G.ident[:],
                                       ALU.add).then_inc(table_ready, 1)
                pool.wait_ge(table_ready, 2)
                for l in range(2):
                    pool.tensor_tensor(G.expert_w[:, l, :, :], G.expert_w[:, l, :, :],
                                       wbase[:, l, :].unsqueeze(1).to_broadcast([128, NEXP0 + 1, SLOT]),
                                       ALU.add)

            @block.tensor
            def _(pe):
                pe.wait_ge(G.attention_loads, 16 * len(G.attention_weights))

                def step(t, k):
                    n, m, s, r = t, t - 2, t - 3, t - 4
                    if exists(s, NT):
                        at_least(pe, v_ready, s)
                        for c in range(2 * SEQ_TILE):
                            mm = pe.matmul(pv[0:NJ, c * HID:(c + 1) * HID], xn[:, 1 - k, c * NJ:(c + 1) * NJ],
                                           vw[:], start=True, stop=True)
                        mm.then_inc(v_made, 1)
                    if exists(m, NT):
                        if isinstance(t, int) and m == 0:
                            pe.wait_ge(cleared, 3)
                            pe.wait_ge(prepared, 2)
                        pe.wait_ge(low_ready, m + 1)
                        for h in range(2):
                            at_least(pe, tanh_done, 4 * m - 2 + h + 1)
                            for part, w in enumerate((w1h, w1l)):
                                mm = pe.matmul(pw[h][:, 0:COLS], w[:], xs[:, k, h * COLS:(h + 1) * COLS],
                                               start=(part == 0), stop=(part == 1))
                            mm.then_inc(proj_made, 1)

                    def center_and_project():
                        if exists(n, NT):
                            pe_center(pe, G, S, L, n, k)
                        if exists(m, NT):
                            for h in range(2):
                                pe.wait_ge(tanh_done, 4 * m + h + 1)
                                pe.matmul(pw[h][:, 0:COLS], w2[:], hid[:, h * COLS:(h + 1) * COLS],
                                          start=True, stop=True).then_inc(proj_made, 1)
                        if exists(n, NT):
                            pe_variance(pe, G, L, n)
                    if not exists(r, NT):
                        center_and_project()
                    else:
                        at_least(pe, stream_done, r)

                        def scores(b):
                            at_least(pe, probs_ready, SEQ_TILE * r + b - 1)
                            pe.matmul(ps[b % 2][0:NJ, 0:SEQ], phik[:, k, b * SEQ:b * SEQ + NJ],
                                      phiq[:, k, b * SEQ:(b + 1) * SEQ], start=True, stop=True)
                            pe.matmul(ps[b % 2][0:NJ, SEQ:SEQ + NJ], phik[:, k, b * SEQ + NJ:(b + 1) * SEQ],
                                      phiq[:, k, b * SEQ + NJ:(b + 1) * SEQ], start=True,
                                      stop=True).then_inc(score_made, 1)

                        def retrieve(b):
                            pe.wait_ge(probs_ready, SEQ_TILE * r + b + 1)
                            for c in range(2):
                                for par in range(2):
                                    mm = pe.matmul(
                                        po[par * HID:(par + 1) * HID, b * NJ + c * (NJ // 2):(b + 1) * NJ],
                                        v[:, k, (2 * b + c) * HID:(2 * b + c + 1) * HID],
                                        probs[:, b % 2, c * SEQ:SEQ + c * NJ].rearrange("p (j o) -> p j o", o=2)[:, :, par],
                                        start=(c == 0), stop=(c == 1), skip_group_check=True)
                            mm.then_inc(out_made, 1)
                        pe.wait_ge(phi_ready, 2 * r + 2)
                        pe.wait_ge(v_ready, r + 1)
                        scores(0)
                        scores(1)
                        center_and_project()
                        for b in range(2, SEQ_TILE):
                            retrieve(b - 2)
                            scores(b)
                        retrieve(SEQ_TILE - 2)
                        retrieve(SEQ_TILE - 1)
                run_steps(pe, NT, 4, step)

            @block.scalar
            def _(act):
                act.wait_ge(G.attention_loads, 16 * len(G.attention_weights))

                def step(t, k):
                    n, m, s = t, t - 2, t - 3
                    act.preload_act_table_set("silu_and_others")
                    if exists(m, NT):
                        for h in range(2):
                            act.wait_ge(proj_made, 4 * m + h + 1)
                            act.activation(hid[:, h * COLS:(h + 1) * COLS], pw[h][:, 0:COLS], ACT.Tanh,
                                           bias=vec[:, 0:1]).then_inc(tanh_done, 1)
                    if exists(s, NT):
                        act.wait_ge(folded_ready, s + 1)
                        at_least(act, out_made, SEQ_TILE * (s - 1))
                        act.activation(phik[0:HID, 1 - k, :], folded[0:HID, :], ACT.Sin,
                                       bias=vec[0:HID, 4:5], scale=vec[0:HID, 3:4]).then_inc(phi_ready, 1)
                    if exists(n, NT):
                        act_square(act, L, n)
                    if exists(s, NT):
                        act.activation(phiq[0:HID, 1 - k, :], folded[HID:128, :], ACT.Sin,
                                       bias=vec[HID:128, 4:5], scale=vec[HID:128, 3:4]).then_inc(phi_ready, 1)
                    if exists(m, NT):
                        at_least(act, folded_ready, m)
                        for h in range(2):
                            act.wait_ge(proj_made, 4 * m + h + 3)
                            act.activation(phase[:, h * COLS:(h + 1) * COLS], pw[h][:, 0:COLS], ACT.Tanh,
                                           bias=vec[:, 1:2]).then_inc(tanh_done, 1)
                    if exists(n, NT):
                        act.preload_act_table_set("natural_log_exp_and_others")
                        act_rstd(act, L, n)
                run_steps(act, NT, 3, step)

            @block.vector
            def _(dve):
                dve.wait_ge(G.attention_loads, 16 * len(G.attention_weights))
                dve.memset(xn[HID:128, :, :], 0.0).then_inc(cleared, 1)
                dve.memset(phik[HID:128, :, :], 0.0).then_inc(cleared, 1)
                dve.memset(phiq[HID:128, :, :], 0.0).then_inc(cleared, 1)
                dve.tensor_copy(w1h[:], w1[:]).then_inc(prepared, 1)
                dve.wait_ge(prepared, 1)
                dve.tensor_tensor(w1l[:], w1[:], w1h[:], ALU.subtract).then_inc(prepared, 1)
                count = [0]

                def link(ins):
                    count[0] += 1
                    ins.then_inc(chain, 1)
                    dve.wait_ge(chain, count[0])
                link(dve.tensor_scalar(r1[:], rt[:], 0.0, None, ALU.is_ge))
                link(dve.tensor_scalar(r2[:], rt[:], float(NEXP0 - 1), None, ALU.is_le))
                link(dve.tensor_tensor(r1[:], r1[:], r2[:], ALU.mult))
                link(dve.tensor_scalar(r3[:], rt[:], float(NEXP0), None, ALU.subtract))
                link(dve.tensor_tensor(r3[:], r3[:], r1[:], ALU.mult))
                link(dve.tensor_scalar(G.expert_of[:], r3[:], float(NEXP0), None, ALU.add))

                def step(t, k):
                    p, m, s, r = t - 1, t - 2, t - 3, t - 4

                    def masked(b):
                        dve.wait_ge(score_made, SEQ_TILE * r + b + 1)
                        at_least(dve, out_made, SEQ_TILE * r + b - 1)
                        dve.tensor_tensor(probs[:, b % 2, :], ps[b % 2][0:NJ, 0:3 * NJ], mask[:],
                                          ALU.mult).then_inc(probs_ready, 1)
                    if exists(s, NT):
                        dve.wait_ge(v_made, s + 1)
                        at_least(dve, out_made, SEQ_TILE * (s - 1))
                        dve.tensor_tensor(v[:, 1 - k, :].rearrange("p (c h) -> p c h", h=HID),
                                          pv[0:NJ, :].rearrange("p (c h) -> p c h", h=HID),
                                          vb[:].unsqueeze(1).to_broadcast([NJ, 2 * SEQ_TILE, HID]),
                                          ALU.add).then_inc(v_ready, 1)
                    if exists(p, NT):
                        dve.wait_ge(L.rstd_ready, p + 1)
                        at_least(dve, v_made, p - 1)
                        for par in range(2):
                            rows = slice(par * HID, (par + 1) * HID)
                            dve.tensor_tensor(xn[0:HID, 1 - k, :].rearrange("p (j o) -> p j o", o=2)[:, :, par],
                                              L.centered[rows, 0:COLS], L.rstd[rows, :],
                                              ALU.mult).then_inc(L.norm_done, 1)
                    if exists(r, NT):
                        masked(0)
                        masked(1)
                    if exists(p, NT):
                        dve.wait_ge(L.norm_done, 2 * p + 2)
                        at_least(dve, proj_made, 4 * p - 6)
                        dve.tensor_copy(xs[0:HID, 1 - k, :], xn[0:HID, 1 - k, :]).then_inc(high_ready, 1)
                        dve.wait_ge(high_ready, p + 1)
                        dve.tensor_tensor(xs[HID:128, 1 - k, :], xn[0:HID, 1 - k, :], xs[0:HID, 1 - k, :],
                                          ALU.subtract).then_inc(low_ready, 1)
                    if exists(r, NT):
                        masked(2)
                        masked(3)
                    if exists(m, NT):
                        dve.wait_ge(tanh_done, 4 * m + 4)
                        at_least(dve, phi_ready, 2 * m)
                        dve.scalar_tensor_tensor(out=folded[:, :], in0=phase[:, :], scalar=vec[:, 2:3],
                                                 in1=phase[:, :], op0=ALU.mult,
                                                 op1=ALU.max).then_inc(folded_ready, 1)
                    if exists(r, NT):
                        dve.wait_ge(out_made, SEQ_TILE * r + SEQ_TILE)
                        dve.tensor_tensor(G.t_flat[:, ds(r * COLS, COLS)], po[:, 0:COLS],
                                          G.t_flat[:, ds(r * COLS, COLS)], ALU.add).then_inc(stream_done, 1)
                run_steps(dve, NT, 4, step)



def phase_routed(nc, G):
    D, NT = G.dram, SEQ_TILES
    with ExitStack() as ctx:
        sb = lambda n, s, d=F32: ctx.enter_context(nc.sbuf_tensor("r_" + n, s, d))
        pt = lambda n: ctx.enter_context(nc.psum_tensor("r_" + n, [128, 512], F32))
        sem = lambda n: G.ctx.enter_context(nc.semaphore("r_" + n))
        L = Norm(ctx, nc, sem, "r", COLS, 1e-5)
        wi, wo, vec = (tile for tile, _ in G.routed_weights)
        S = StreamParts(ctx, nc, sem, "r", COLS)
        wih, wil = sb("wih", [128, LH], F32R), sb("wil", [128, LH], F32R)
        xn = sb("xn", [128, COLS])
        xs = sb("xs", [128, 2, 2, COLS], F32R)
        high_ready, low_ready, prepared = sem("high_ready"), sem("low_ready"), sem("prepared")
        h0, h1, h2 = (sb(f"h{i}", [128, 2, 2, COLS]) for i in range(3))
        wa, wb = (sb(f"w{i}", [128, 2, 2, SLOT]) for i in "ab")
        pm = [pt(f"pm{i}") for i in range(4)]
        po = pt("po")
        wa_here, wb_here = ([sem(f"w{i}_here{k}") for k in range(2)] for i in "ab")
        in_made, in_done = sem("in_made"), sem("in_done")
        a_made, a_done, b_made, b_done = sem("a_made"), sem("a_done"), sem("b_made"), sem("b_done")
        out_made, stream_done = sem("out_made"), sem("stream_done")

        with nc.Block() as block:
            @block.sync
            def _(sp):
                def step(t, k):
                    for l, n, kn, w, here, done in ((0, t, k, wa, wa_here, a_done),
                                                    (1, t - 1, 1 - k, wb, wb_here, b_done)):
                        if not exists(n, NT):
                            continue
                        for g in range(2):
                            e = sp.value_load(G.expert_of[0:1, ds(2 * n + g, 1)], min_val=0, max_val=NEXP0)
                            if g == 0:
                                at_least(sp, done, 2 * n - 2)
                            sp.dma_start(w[:, kn, g, :], G.expert_w[:, l, ds(e, 1), :].rearrange("p e s -> p (e s)")
                                         ).then_inc(here[kn], 16)
                run_steps(sp, NT, 1, step)

            @block.gpsimd
            def _(pool):
                def step(t, k):
                    pool_split_stream(pool, S, L, t, k, G.t[:, ds(t * SEQ_TILE, SEQ_TILE), :], NJ)
                run_steps(pool, NT, 0, step)

            @block.tensor
            def _(pe):
                pe.wait_ge(prepared, 2)

                def step(t, k):
                    n, i, a, b, o = t, t - 2, t - 3, t - 4, t - 5
                    if exists(n, NT):
                        pe_center(pe, G, S, L, n, k)
                    if exists(i, NT):
                        pe.wait_ge(low_ready, 2 * i + 2)
                        at_least(pe, b_done, 2 * (t - 4))
                        for par in range(2):
                            pe.matmul(pm[par][:, 0:COLS], wih[:], xs[:, k, par, :], start=True, stop=False)
                            pe.matmul(pm[par][:, 0:COLS], wil[:], xs[:, k, par, :], start=False,
                                      stop=True).then_inc(in_made, 1)
                    if exists(a, NT):
                        pe.wait_ge(in_done, 2 * a + 2)
                        pe.wait_ge(wa_here[1 - k], 32 * half(a, 1 - k) + 32)
                        at_least(pe, a_done, 2 * a)
                        for g in range(2):
                            pe.matmul(pm[2 + g][:, 0:COLS].rearrange("p (o c) -> p o c", o=2), wa[:, 1 - k, g, 0:LH],
                                      h0[:, 1 - k, :, g * GCOLS:(g + 1) * GCOLS], start=True,
                                      stop=True).then_inc(a_made, 1)
                    if exists(n, NT):
                        pe_variance(pe, G, L, n)
                    if exists(b, NT):
                        pe.wait_ge(a_done, 2 * b + 2)
                        at_least(pe, b_done, 2 * b)
                        at_least(pe, in_done, 2 * min(t - 1, NT) if isinstance(t, int) else 2 * t - 2)
                        pe.wait_ge(wb_here[k], 32 * half(b, k) + 32)
                        for g in range(2):
                            pe.matmul(pm[g][:, 0:COLS], wb[:, k, g, 0:LH], h1[:, k, g, :], start=True,
                                      stop=True).then_inc(b_made, 1)
                    if exists(o, NT):
                        pe.wait_ge(b_done, 2 * o + 2)
                        at_least(pe, stream_done, o)
                        for g in range(2):
                            for par in range(2):
                                mm = pe.matmul(po[par * HID:(par + 1) * HID, g * GCOLS:(g + 1) * GCOLS], wo[:],
                                               h2[:, 1 - k, g, par * GCOLS:(par + 1) * GCOLS], start=True, stop=True,
                                               skip_group_check=True)
                        mm.then_inc(out_made, 1)
                run_steps(pe, NT, 5, step)

            @block.scalar
            def _(act):
                act.preload_act_table_set("natural_log_exp_and_others")

                def step(t, k):
                    n, i, a, b = t, t - 2, t - 3, t - 4
                    if exists(n, NT):
                        act_square(act, L, n)
                    if exists(i, NT):
                        at_least(act, a_made, 2 * (i - 1))
                        for par in range(2):
                            act.wait_ge(in_made, 2 * i + par + 1)
                            act.activation(h0[:, k, par, :], pm[par][:, 0:COLS], ACT.Relu,
                                           bias=vec[:, 0:1]).then_inc(in_done, 1)
                    if exists(n, NT):
                        act_rstd(act, L, n)
                    if exists(b, NT):
                        at_least(act, out_made, b - 1)
                        for g in range(2):
                            act.wait_ge(b_made, 2 * b + g + 1)
                            act.activation(h2[:, k, g, :], pm[g][:, 0:COLS], ACT.Relu,
                                           bias=wb[:, k, g, LH:SLOT]).then_inc(b_done, 1)
                run_steps(act, NT, 4, step)

            @block.vector
            def _(dve):
                dve.tensor_copy(wih[:], wi[:]).then_inc(prepared, 1)
                dve.wait_ge(prepared, 1)
                dve.tensor_tensor(wil[:], wi[:], wih[:], ALU.subtract).then_inc(prepared, 1)

                def step(t, k):
                    n, a, o = t, t - 3, t - 5
                    if exists(a, NT):
                        at_least(dve, b_made, 2 * (a - 1))
                        for g in range(2):
                            dve.wait_ge(a_made, 2 * a + g + 1)
                            dve.tensor_scalar(h1[:, 1 - k, g, :], pm[2 + g][:, 0:COLS], wa[:, 1 - k, g, LH:SLOT], 0.0,
                                              ALU.add, ALU.max).then_inc(a_done, 1)
                    if exists(n, NT):
                        dve.wait_ge(L.rstd_ready, n + 1)
                        at_least(dve, low_ready, 2 * n)
                        dve.tensor_tensor(xn[:, :], L.centered[:, 0:COLS], L.rstd[:, :],
                                          ALU.mult).then_inc(L.norm_done, 1)
                        dve.wait_ge(L.norm_done, n + 1)
                        at_least(dve, in_made, 2 * (n - 1))
                        split_high(dve, xs[:, k], xn, high_ready)
                    if exists(o, NT):
                        dve.wait_ge(out_made, o + 1)
                        dve.scalar_tensor_tensor(out=G.t_flat[:, ds(o * COLS, COLS)], in0=po[:, 0:COLS],
                                                 scalar=vec[:, 1:2], in1=G.t_flat[:, ds(o * COLS, COLS)],
                                                 op0=ALU.add, op1=ALU.add).then_inc(stream_done, 1)
                    if exists(n, NT):
                        dve.wait_ge(high_ready, 2 * n + 2)
                        split_low(dve, xs[:, k], xn, low_ready)
                run_steps(dve, NT, 5, step)



def phase_ssm(nc, G):
    D, NT = G.dram, PAIR_TILES
    wut, a2t, gt, kt = G.ssm
    with ExitStack() as ctx:
        sb = lambda n, s, d=F32: ctx.enter_context(nc.sbuf_tensor("s_" + n, s, d))
        pt = lambda n: ctx.enter_context(nc.psum_tensor("s_" + n, [128, 512], F32))
        sem = lambda n: G.ctx.enter_context(nc.semaphore("s_" + n))
        L = Norm(ctx, nc, sem, "s", PCOLS, 1e-5, banks=2)
        S = StreamParts(ctx, nc, sem, "s", PCOLS)
        xn = sb("xn", [128, 2, PCOLS])
        state = sb("state", [128, PAIR_TILE, NB])
        px, py = [pt("px0"), pt("px1")], [pt("py0"), pt("py1")]
        x_made, x_ready, y_made, stream_done, inject_made = sem("x_made"), sem("x_ready"), sem("y_made"), sem("stream_done"), sem("inject_made")
        stream = G.t.rearrange("p b j -> p j b")
        S4 = PAIR_TILE

        with nc.Block() as block:
            @block.gpsimd
            def _(pool):
                def step(t, k):
                    pool_split_stream(pool, S, L, t, k, stream[:, ds(t * PAIR_TILE, PAIR_TILE), :], NB)
                run_steps(pool, NT, 0, step)

            @block.scalar
            def _(act):
                act.preload_act_table_set("natural_log_exp_and_others")

                def step(t, k):
                    act_square(act, L, t, bank=k)
                    act_rstd(act, L, t)
                run_steps(act, NT, 0, step)

            @block.tensor
            def _(pe):
                def step(t, k):
                    n, i, m = t, t - 1, t - 2

                    def inject():
                        if exists(i, NT):
                            pe.wait_ge(L.norm_done, i + 1)
                            at_least(pe, x_ready, S4 * (i - 1) + 1)
                            pe.matmul(px[1 - k][:, :], wut[:], xn[:, 1 - k, :], start=True, stop=False,
                                      skip_group_check=True)

                    def center():
                        if exists(n, NT):
                            pe_center(pe, G, S, L, n, k)

                    def advance(q):
                        pe.wait_ge(x_ready, S4 * m + q + 1)
                        pe.matmul(px[k][:, q * NB:(q + 1) * NB], a2t[:], state[:, (q - 1) % S4, :], start=False,
                                  stop=True, skip_group_check=True).then_inc(x_made, 1)

                    def observe(q):
                        mm = pe.matmul(py[k][:, q * NB:(q + 1) * NB], gt[:], state[:, (q - 1) % S4, :], start=False,
                                       stop=True, skip_group_check=True)
                        if q == S4 - 1:
                            mm.then_inc(y_made, 1)
                    if not exists(m, NT):
                        center()
                        inject()
                        pe_variance(pe, G, L, n)
                        return
                    advance(0)
                    at_least(pe, stream_done, m - 1)
                    pe.matmul(py[k][:, :], kt[:], xn[:, k, :], start=True, stop=False,
                              skip_group_check=True).then_inc(inject_made, 1)
                    observe(0)
                    advance(1)
                    center()
                    observe(1)
                    advance(2)
                    inject()
                    observe(2)
                    advance(3)
                    if exists(n, NT):
                        pe_variance(pe, G, L, n)
                    observe(3)
                run_steps(pe, NT, 2, step)

            @block.vector
            def _(dve):
                dve.memset(state[:, PAIR_TILE - 1, :], 0.0).then_inc(x_ready, 1)

                def step(t, k):
                    p, m, o = t - 1, t - 2, t - 3

                    def keep(q):
                        if exists(m, NT):
                            dve.wait_ge(x_made, S4 * m + q + 1)
                            dve.tensor_copy(state[:, q, :], px[k][:, q * NB:(q + 1) * NB]).then_inc(x_ready, 1)
                    keep(0)
                    if exists(p, NT):
                        dve.wait_ge(L.rstd_ready, p + 1)
                        at_least(dve, inject_made, p - 1)
                        dve.tensor_tensor(xn[:, 1 - k, :], L.centered_banks[1 - k][:, :], L.rstd[:, :],
                                          ALU.mult).then_inc(L.norm_done, 1)
                    keep(1)
                    if exists(o, NT):
                        dve.wait_ge(y_made, o + 1)
                        dve.tensor_tensor(stream[:, ds(o * S4, S4), :],
                                          py[1 - k][:, :].rearrange("p (j b) -> p j b", b=NB),
                                          stream[:, ds(o * S4, S4), :], ALU.add).then_inc(stream_done, 1)
                    keep(2)
                    keep(3)
                run_steps(dve, NT, 3, step)



def phase_experts(nc, G, out):
    D, NT = G.dram, PAIR_TILES
    with ExitStack() as ctx:
        sb = lambda n, s, d=F32: ctx.enter_context(nc.sbuf_tensor("x_" + n, s, d))
        pt = lambda n, d=F32: ctx.enter_context(nc.psum_tensor("x_" + n, [128, 2048 // (4 if d is F32 else 2)], d))
        sem = lambda n: G.ctx.enter_context(nc.semaphore("x_" + n))
        L = Norm(ctx, nc, sem, "x", PCOLS, 1e-5)
        S = StreamParts(ctx, nc, sem, "x", PCOLS)
        PE2 = 2 * NEXP1
        LG = PAIR_TILE * PE2
        rw, rb, tie, w1, b1, w2, b2, maskf = (tile for tile, _ in G.experts_weights)
        w1h, w1l = sb("w1h", [128, FCH * 128], F32R), sb("w1l", [128, FCH * 128], F32R)
        b2f, b2p = sb("b2f", [128, 2, 128]), sb("b2p", [128, 3, 128], BF16)
        maskb = sb("maskb", [128, 2, FCH, 128], BF16)
        identb = sb("identb", [128, 128], BF16)
        xn = sb("xn", [128, 2, PCOLS])
        xs = sb("xs", [128, 2, 2, PCOLS], F32R)
        high_ready, low_ready = sem("high_ready"), sem("low_ready")
        logit, hit = sb("logit", [NB, LG]), sb("hit", [NB, LG])
        top, first = sb("top", [NB, 2 * PAIR_TILE]), sb("first", [NB, 2 * PAIR_TILE])
        onehot = sb("onehot", [NB, LG], BF16)
        choice = sb("choice", [128, 2, PCOLS], BF16)
        hm = sb("hm", [128, 2, FCH, PCOLS])
        fin = sb("fin", [128, 2, PCOLS])
        outs = sb("outs", [NB, 2, PCOLS])
        plog, pch, pfin, po = pt("plog"), pt("pch", BF16), pt("pfin"), pt("po")
        pf = [pt("pf0"), pt("pf1")]
        cleared, prep, prep_done = sem("cleared"), sem("prep"), sem("prep_done")
        logit_made, logit_ready = sem("logit_made"), sem("logit_ready")
        top_ready, hit_ready, tied_ready, first_ready = sem("top_ready"), sem("hit_ready"), sem("tied_ready"), sem("first_ready")
        onehot_ready, choice_made, choice_ready = sem("onehot_ready"), sem("choice_made"), sem("choice_ready")
        up_made, relu0, relu1 = sem("up_made"), sem("relu0"), sem("relu1")
        down_made, fin_ready, fin_made, outs_ready = sem("down_made"), sem("fin_ready"), sem("fin_made"), sem("outs_ready")
        stored, turn_begun = [sem("stored0"), sem("stored1")], sem("turn_begun")
        split_begun = sem("split_begun")
        stream = G.t.rearrange("p b j -> p j b")
        out_rows = out.rearrange("b s c -> b (s c)")
        S4 = PAIR_TILE
        by_expert = lambda a: a.rearrange("p (g e) -> p g e", e=NEXP1)

        with nc.Block() as block:
            @block.sync
            def _(sp):
                def step(t, k):
                    sp.wait_ge(outs_ready, t + 1)
                    sp.dma_start(out_rows[:, ds(t * PCOLS, PCOLS)], outs[:, k, :]).then_inc(stored[k], 16)
                run_steps(sp, NT, 0, step)
                sp.wait_ge(stored[0], 16 * (NT // 2 + 1))
                sp.wait_ge(stored[1], 16 * (NT // 2))

            @block.gpsimd
            def _(pool):
                pool.memset(choice[HID:128, :, :], 0.0).then_inc(cleared, 1)
                pool.wait_ge(cleared, 1)
                pool.memset(choice[HID:HID + 1, :, :], 1.0).then_inc(prep_done, 1)
                pool.wait_ge(prep_done, 2)

                def step(t, k):
                    i = t - 1
                    if exists(t, NT):
                        at_least(pool, high_ready, 2 * (t - 1))
                        pool_split_stream(pool, S, L, t, k, stream[:, ds(t * S4, S4), :], NB)
                    if exists(i, NT):
                        at_least(pool, S.low_ready, t + 1 if exists(t, NT) else NT)
                        pool.wait_ge(L.norm_done, i + 1)
                        at_least(pool, up_made, 2 * FCH * (i - 1))
                        pool.sem_inc(split_begun, 1)
                        split_high(pool, xs[:, 1 - k], xn[:, 1 - k, :], high_ready)
                run_steps(pool, NT, 1, step)

            @block.tensor
            def _(pe):
                def step(t, k):
                    n, i, m, f = t, t - 1, t - 2, t - 3
                    if exists(i, NT):
                        pe.wait_ge(L.norm_done, i + 1)
                        at_least(pe, logit_ready, i)
                        for q in range(S4):
                            mm = pe.matmul(plog[:, q * PE2:(q + 1) * PE2], xn[:, 1 - k, q * NB:(q + 1) * NB], rw[:],
                                           start=True, stop=True)
                        mm.then_inc(logit_made, 1)
                    if exists(n, NT):
                        pe_center(pe, G, S, L, n, k)
                    if exists(m, NT):
                        if isinstance(t, int) and m == 0:
                            pe.wait_ge(prep_done, 2)
                        pe.wait_ge(choice_ready, m + 1)
                        pe.wait_ge(low_ready, 2 * m + 2)

                        def up(ck):
                            for par in range(2):
                                at_least(pe, (relu0, relu1)[par], FCH * m + ck)
                                pe.matmul(pf[par][:, :], maskb[:, par, ck, :], choice[:, k, :], start=True, stop=False)
                                pe.matmul(pf[par][:, :], w1h[:, ck * 128:(ck + 1) * 128], xs[:, k, par, :],
                                          start=False, stop=False)
                                pe.matmul(pf[par][:, :], w1l[:, ck * 128:(ck + 1) * 128], xs[:, k, par, :],
                                          start=False, stop=True).then_inc(up_made, 1)

                        def down(ck):
                            pe.wait_ge(relu0, FCH * m + ck + 1)
                            pe.wait_ge(relu1, FCH * m + ck + 1)
                            for par in range(2):
                                mm = pe.matmul(po[par * HID:(par + 1) * HID, :], w2[:, ck, :], hm[:, par, ck, :],
                                               start=False, stop=(ck == FCH - 1), skip_group_check=True)
                            return mm
                        up(0)
                        up(1)
                        if exists(n, NT):
                            pe_variance(pe, G, L, n)
                        at_least(pe, fin_ready, m)
                        for j in range(3):
                            pe.matmul(po[:, :], b2p[:, j, :], choice[:, k, :], start=(j == 0), stop=False,
                                      skip_group_check=True)
                        for ck in range(2, FCH):
                            down(ck - 2)
                            up(ck)
                        down(FCH - 2)
                        mm = down(FCH - 1)
                        mm.then_inc(down_made, 1)
                    elif exists(n, NT):
                        pe_variance(pe, G, L, n)
                    if exists(f, NT):
                        pe.wait_ge(fin_ready, f + 1)
                        at_least(pe, outs_ready, f)
                        for q in range(S4):
                            mm = pe.transpose(pfin[:, q * 128:(q + 1) * 128], fin[:, 1 - k, q * NB:(q + 1) * NB],
                                              G.ident[:])
                        mm.then_inc(fin_made, 1)
                    if exists(i, NT):
                        if isinstance(t, int) and i == 0:
                            pe.wait_ge(prep, 1)
                        pe.wait_ge(onehot_ready, i + 1)
                        at_least(pe, choice_ready, i)
                        pe.sem_inc(turn_begun, 1)
                        for q in range(S4):
                            mm = pe.transpose(pch[0:PE2, q * NB:(q + 1) * NB], onehot[:, q * PE2:(q + 1) * PE2],
                                              identb[:])
                        mm.then_inc(choice_made, 1)
                run_steps(pe, NT, 3, step)

            @block.scalar
            def _(act):
                act.preload_act_table_set("natural_log_exp_and_others")

                def step(t, k):
                    n, m, f = t, t - 2, t - 3
                    if exists(n, NT):
                        act_square(act, L, n)
                    if exists(m, NT):
                        at_least(act, down_made, m)
                        for ck in range(FCH):
                            act.wait_ge(up_made, 2 * FCH * m + 2 * ck + 1)
                            act.activation(hm[:, 0, ck, :], pf[0][:, :], ACT.Relu,
                                           bias=b1[:, ck:ck + 1]).then_inc(relu0, 1)
                            if ck == 2 and exists(n, NT):
                                act_rstd(act, L, n)
                    elif exists(n, NT):
                        act_rstd(act, L, n)
                    if exists(f, NT):
                        act.wait_ge(fin_made, f + 1)
                        at_least(act, stored[1 - k], 16 * half(f, 1 - k))
                        act.activation(outs[:, 1 - k, :], pfin[:, :], ACT.Identity).then_inc(outs_ready, 1)
                run_steps(act, NT, 3, step)

            @block.vector
            def _(dve):
                count = [0]

                def link(*instructions):
                    for ins in instructions:
                        ins.then_inc(prep, 1)
                    count[0] += len(instructions)
                    dve.wait_ge(prep, count[0])
                link(dve.tensor_copy(identb[:], G.ident[:]), dve.tensor_copy(w1h[:], w1[:]),
                     dve.tensor_copy(b2p[:, 0, :], b2[:]))
                dve.tensor_tensor(w1l[:], w1[:], w1h[:], ALU.subtract)
                link(dve.tensor_tensor(b2f[:, 0, :], b2[:], b2p[:, 0, :], ALU.subtract))
                link(dve.tensor_copy(b2p[:, 1, :], b2f[:, 0, :]))
                link(dve.tensor_tensor(b2f[:, 1, :], b2f[:, 0, :], b2p[:, 1, :], ALU.subtract))
                dve.tensor_copy(maskb[:], maskf[:])
                dve.tensor_copy(b2p[:, 2, :], b2f[:, 1, :]).then_inc(prep_done, 1)

                def step(t, k):
                    n, i, m = t, t - 1, t - 2

                    def relu(cks):
                        for ck in cks:
                            dve.wait_ge(up_made, 2 * FCH * m + 2 * ck + 2)
                            dve.tensor_scalar(hm[:, 1, ck, :], pf[1][:, :], b1[:, ck:ck + 1], 0.0, ALU.add,
                                              ALU.max).then_inc(relu1, 1)
                    if exists(i, NT):
                        dve.wait_ge(logit_made, i + 1)
                        dve.tensor_tensor(logit[:, :].rearrange("p (q e) -> p q e", e=PE2),
                                          plog[:, 0:LG].rearrange("p (q e) -> p q e", e=PE2),
                                          rb[:].unsqueeze(1).to_broadcast([NB, S4, PE2]), ALU.add).then_inc(logit_ready, 1)
                        dve.wait_ge(logit_ready, i + 1)
                        dve.tensor_reduce(top[:, :], by_expert(logit[:, :]), AX_X, ALU.max).then_inc(top_ready, 1)
                        dve.wait_ge(top_ready, i + 1)
                        dve.tensor_tensor(by_expert(hit[:, :]), by_expert(logit[:, :]),
                                          top[:].unsqueeze(2).to_broadcast([NB, 2 * S4, NEXP1]), ALU.is_ge).then_inc(hit_ready, 1)
                        dve.wait_ge(hit_ready, i + 1)
                    if exists(m, NT):
                        at_least(dve, down_made, m)
                        relu(range(0, 1))
                    if exists(i, NT):
                        dve.tensor_tensor(logit[:, :], hit[:, :], tie[:, :], ALU.mult).then_inc(tied_ready, 1)
                        dve.wait_ge(tied_ready, i + 1)
                        dve.tensor_reduce(first[:, :], by_expert(logit[:, :]), AX_X, ALU.max).then_inc(first_ready, 1)
                        dve.wait_ge(first_ready, i + 1)
                        at_least(dve, choice_made, i)
                        dve.tensor_tensor(by_expert(onehot[:, :]), by_expert(logit[:, :]),
                                          first[:].unsqueeze(2).to_broadcast([NB, 2 * S4, NEXP1]),
                                          ALU.is_equal).then_inc(onehot_ready, 1)
                    if exists(m, NT):
                        relu(range(1, 3))
                    if exists(i, NT):
                        dve.wait_ge(high_ready, 2 * i + 2)
                        split_low(dve, xs[:, 1 - k], xn[:, 1 - k, :], low_ready)
                    if exists(m, NT):
                        relu(range(3, FCH))
                    if exists(n, NT):
                        dve.wait_ge(L.rstd_ready, n + 1)
                        at_least(dve, logit_made, n - 1)
                        dve.tensor_tensor(xn[:, k, :], L.centered[:, :], L.rstd[:, :],
                                          ALU.mult).then_inc(L.norm_done, 1)
                    if exists(m, NT):
                        dve.wait_ge(down_made, m + 1)
                        at_least(dve, fin_made, m - 1)
                        dve.scalar_tensor_tensor(out=fin[:, k, :].rearrange("p (j b) -> p j b", b=NB),
                                                 in0=po[:, :].rearrange("p (j b) -> p j b", b=NB), scalar=0.0,
                                                 in1=stream[:, ds(m * S4, S4), :], op0=ALU.max,
                                                 op1=ALU.add).then_inc(fin_ready, 1)
                    if exists(i, NT):
                        dve.wait_ge(choice_made, i + 1)
                        at_least(dve, down_made, i - 1)
                        dve.tensor_copy(choice[0:PE2, 1 - k, :], pch[0:PE2, 0:PCOLS]).then_inc(choice_ready, 1)
                run_steps(dve, NT, 2, step)

class Shared:
    pass


def build(nc, D, out):
    with ExitStack() as ctx:
        sb = lambda n, s, d=F32: ctx.enter_context(nc.sbuf_tensor(n, s, d))
        G = Shared()
        G.dram, G.ctx = D, ctx
        G.ident, G.center_m, G.mean_m = sb("ident", [128, 128]), sb("center_m", [128, 128]), sb("mean_m", [128, 128])
        G.center_r = sb("center_r", [128, 128], F32R)
        G.flip = sb("flip", [NJ, NJ])
        G.ssm = [sb("ssm_" + n, [128, 128]) for n in ("wut", "a2t", "gt", "kt")]
        G.vec = sb("vec", [128, 16])
        G.d1h, G.d1l = (sb(f"d1_{i}", [128, LAYERS, DFF], F32R) for i in ("high", "low"))
        G.center_s = sb("center_s", [128, 2, 128], F32R)
        G.gelu_b = sb("gelu_b", [128, LAYERS, 2])
        G.d2c = sb("d2c", [128, LAYERS, 2, HID])
        G.d2bc = sb("d2bc", [128, LAYERS])
        tiles = lambda names: [(sb(n, D[n].shape, D[n].dtype), D[n]) for n in names]
        G.attention_weights = tiles(("a_w1", "a_w2", "a_vw", "a_mask", "a_vb", "a_vec", "route"))
        G.attention_loads = ctx.enter_context(nc.semaphore("attention_loads"))
        G.lag_dram = nc.dram_tensor("lag_kernels", (LAYERS, HID, NLAG), F32).ap()
        region = sb("region", [128, PC * NB])
        G.bp = region[0:NJ, :].rearrange("p (f b) -> p f b", b=NB)
        G.t_flat = region[:, 0:NB * NJ]
        G.t = G.t_flat.rearrange("p (b j) -> p b j", j=NJ)
        with ExitStack() as early:
            y = early.enter_context(nc.sbuf_tensor("conv_out", [NJ, NB * PC], F32))
            G.y_flat = y[:, :]
            G.y = G.y_flat.rearrange("p (b f) -> p b f", f=PC)
            phase_embed(nc, G)
            for layer in range(LAYERS):
                phase_conv(nc, G, layer)
                phase_ffn(nc, G, layer)
        G.routed_weights = tiles(("r_wi", "r_wo", "r_vec"))
        G.experts_weights = tiles(("x_rw", "x_rb", "x_tie", "x_w1", "x_b1", "x_w2", "x_b2", "x_mask"))
        G.later_loads = ctx.enter_context(nc.semaphore("later_loads"))
        G.expert_w = sb("expert_w", [128, 2, NEXP0 + 1, SLOT])
        G.expert_of = sb("expert_of", [1, NGROUP], I32)
        phase_attention(nc, G)
        phase_routed(nc, G)
        phase_ssm(nc, G)
        phase_experts(nc, G, out)


def lay_out_attention(A, f):
    import numpy as np
    w1 = np.zeros((128, 128), np.float32)
    for rows in (slice(0, HID), slice(HID, 128)):
        w1[rows, 0:HID], w1[rows, HID:128] = f("L0_attn_kw1").T, f("L0_attn_qw1").T
    w2 = np.zeros((128, 128), np.float32)
    vec = np.zeros((128, 8), np.float32)
    vec[:, 0] = np.concatenate([f("L0_attn_kb1"), f("L0_attn_qb1")])
    for side, (w, b) in enumerate((("L0_attn_kw2", "L0_attn_kb2"), ("L0_attn_qw2", "L0_attn_qb2"))):
        for part in range(2):
            cols = slice(side * HID + part * 32, side * HID + part * 32 + 32)
            w2[side * HID:(side + 1) * HID, cols] = f(w).T
            vec[cols, 1] = f(b)
            vec[cols, 2] = (-1.0, 1.0)[part]
            vec[cols, 3] = (-3.1415925, 3.1415925)[part]
            vec[cols, 4] = (PI / 2, 0.0)[part]
    A["a_w1"], A["a_w2"], A["a_vec"] = w1, w2, vec
    vw = np.zeros((128, HID), np.float32)
    vw[0:HID] = f("L0_attn_vw").T
    A["a_vw"] = vw
    A["a_vb"] = np.tile(f("L0_attn_vb"), (NJ, 1))
    key, query = np.arange(NJ)[:, None], np.arange(SEQ)[None, :]
    scale = 1.0 / np.sqrt((query + 1.0) * 32)
    both = [(key <= query) * scale, ((key + NJ <= query) * scale)[:, NJ:]]
    A["a_mask"] = np.concatenate(both, axis=1).astype(np.float32)


def lay_out_routed(A, f):
    import numpy as np
    w = np.zeros((128, 2, NEXP0 + 1, SLOT), np.float32)
    w[:, :, 0:NEXP0, 0:LH] = f("L0_ffn_Wr").transpose(3, 0, 1, 2)
    w[:, :, 0:NEXP0, LH] = f("L0_ffn_br").transpose(2, 0, 1)
    base = np.zeros((128, 2, SLOT), np.float32)
    base[:, :, 0:LH] = f("L0_ffn_Ws")[:, 0].transpose(2, 0, 1)
    base[:, :, LH] = f("L0_ffn_bs")[:, 0].T
    A["r_w"], A["r_base"] = w, base
    A["route"] = f("L0_ffn_route_id").reshape(1, NGROUP)
    A["r_wi"] = np.tile(f("L0_ffn_Wi").T, (2, 1))
    A["r_wo"] = np.ascontiguousarray(f("L0_ffn_Wo").T)
    bo = f("L0_ffn_bo")
    A["r_vec"] = np.stack([f("L0_ffn_bi"), np.concatenate([bo, bo])], axis=1)


def lay_out_ssm(A, f):
    import numpy as np
    rows = [f("L1_attn_Lambda_re"), f("L1_attn_Lambda_im"), f("L1_attn_log_step")]
    lam = np.zeros((128, 3, HID + 1), np.float32)
    for i, v in enumerate(rows):
        lam[:, i, 0:HID] = v[None, :]
        lam[:, i, HID] = np.concatenate([v, v])
    A["s_lam"] = lam
    b = f("L1_attn_B_ri").transpose(1, 2, 0)
    A["s_bt"] = np.concatenate([b, b], axis=0)
    A["s_crt"] = np.concatenate([f("L1_attn_C_re").T, f("L1_attn_C_im").T], axis=0)
    d = f("L1_attn_D")
    sign = np.repeat(np.array([1.0, -1.0], np.float32), HID)
    A["s_col"] = np.stack([np.concatenate([d, d]), sign], axis=1)
    A["s_shift"] = np.roll(np.eye(128, dtype=np.float32), HID, axis=1)


def lay_out_experts(A, f):
    import numpy as np
    PE2 = 2 * NEXP1
    rw = np.zeros((128, PE2), np.float32)
    b2, mask = np.zeros((128, 128), np.float32), np.zeros((128, 2, FCH * 128), np.float32)
    for par in range(2):
        rows, experts = slice(par * HID, (par + 1) * HID), slice(par * NEXP1, (par + 1) * NEXP1)
        rw[rows, experts] = f("L1_ffn_router_w").T
        b2[experts, rows] = f("L1_ffn_b2")
        mask[experts, par] = np.kron(np.eye(NEXP1), np.ones((1, EH))) * BIG
        mask[PE2, par] = -BIG
    A["x_rw"], A["x_b2"] = rw, b2
    A["x_w1"] = np.tile(f("L1_ffn_W1").transpose(1, 0, 2).reshape(HID, FCH * 128), (2, 1))
    A["x_mask"] = mask.reshape(128, 2, FCH, 128)
    A["x_rb"] = np.tile(f("L1_ffn_router_b"), (NB, 2))
    A["x_tie"] = np.tile((NEXP1 - np.arange(NEXP1)).astype(np.float32), (NB, 2 * PAIR_TILE))
    A["x_b1"] = np.ascontiguousarray(f("L1_ffn_b1").reshape(FCH, 128).T)
    A["x_w2"] = np.ascontiguousarray(f("L1_ffn_W2").reshape(FCH, 128, HID).transpose(1, 0, 2))


def lay_out(inputs):
    import numpy as np
    f = lambda n: np.asarray(inputs[n])
    dup = lambda v: np.concatenate([v, v], axis=0)
    A = {}
    A["ids"] = f("x")
    A["item_emb"] = f("L0_tok_item_emb")
    A["pos"] = np.ascontiguousarray(f("L0_tok_pos_emb").reshape(NJ, PC).T)
    A["ident"] = np.eye(128, dtype=np.float32)
    A["flip"] = np.ascontiguousarray(np.eye(NJ, dtype=np.float32)[::-1])
    half = np.eye(HID) - 1.0 / HID
    A["center_m"] = np.kron(np.eye(2), half).astype(np.float32)
    A["mean_m"] = np.kron(np.eye(2), np.full((HID, HID), 1.0 / HID)).astype(np.float32)
    vec = np.zeros((128, 16), np.float32)
    cols = [f("L0_tok_ln0_w"), f("L0_tok_ln0_b"), *f("L0_tok_fln_w"), *f("L0_tok_fln_b"),
            *f("L0_tok_iln_w"), *f("L0_tok_iln_b")]
    for i, v in enumerate(cols):
        vec[:, i] = dup(v)
    A["vec"] = vec
    A["cw"] = np.ascontiguousarray(f("L0_tok_cw").transpose(1, 0, 3, 2))
    freq = np.arange(SEQ // 2 + 1)[:, None]
    lags = (SEQ - 1) - np.arange(NLAG)[None, :]
    weight = np.where((freq == 0) | (freq == SEQ // 2), 1.0, 2.0) / SEQ
    angle = 2 * np.pi * ((freq * lags) % SEQ) / SEQ
    A["dft"] = np.stack([weight * np.cos(angle), -weight * np.sin(angle)], axis=1).astype(np.float32)
    A["d2t"] = np.ascontiguousarray(f("L0_tok_d2_w").transpose(2, 0, 1))
    A["d2b"] = dup(np.ascontiguousarray(f("L0_tok_d2_b").T))
    A["d1"] = np.ascontiguousarray(dup(f("L0_tok_d1_w").transpose(1, 0, 2)))
    center_s = np.zeros((128, 2, 128), np.float32)
    for par in range(2):
        center_s[:, par, par * HID:(par + 1) * HID] = dup(half)
    A["center_s"] = center_s
    A["gelu_b"] = np.ascontiguousarray(f("L0_tok_d1_b").reshape(LAYERS, 2, 128).transpose(2, 0, 1))
    lay_out_attention(A, f)
    lay_out_routed(A, f)
    lay_out_ssm(A, f)
    lay_out_experts(A, f)
    return A


def kernel(**inputs):
    import numpy as _np
    import concourse.bacc as _bacc
    from concourse import mybir as _mybir
    from concourse.bass_utils import run_bass_kernel_spmd as _run

    nc = _bacc.Bacc("TRN2", target_bir_lowering=False, num_devices=1)
    arrays, D = {}, {}
    for name, a in lay_out(inputs).items():
        a = _np.ascontiguousarray(a)
        arrays[f"in_{name}_dram"] = a
        D[name] = nc.dram_tensor(f"in_{name}_dram", a.shape, _mybir.dt.from_np(a.dtype), kind="ExternalInput").ap()
    out = nc.dram_tensor("out_0_dram", (NB, SEQ, HID), F32, kind="ExternalOutput").ap()
    build(nc, D, out)
    r = _run(nc, [arrays], core_ids=[0])
    return r.results[0]["out_0_dram"]
```
